# Optimizing a Trainium2 kernel written in Bass

```python
import numpy as np
import jax
import jax.numpy as jnp

def _softmax(x, axis=-1):
    return jax.nn.softmax(x, axis=axis)

def _gelu(x):
    return jax.nn.gelu(x, approximate=True)

def _silu(x):
    return jax.nn.silu(x)

def _sigmoid(x):
    return jax.nn.sigmoid(x)

def _layernorm(x, axis=-1, eps=1e-05):
    m = jnp.mean(x, axis=axis, keepdims=True)
    v = jnp.var(x, axis=axis, keepdims=True)
    return (x - m) / jnp.sqrt(v + eps)

def _scatter_add(tgt, idx, src, axis=0):
    return tgt.at[idx].add(src)

def _segment_sum(src, seg, n):
    return jax.ops.segment_sum(src, seg, n)
kernel_name = 'mk_adaln_attn_ffn_d1_seqx_r4_a67d91'

def setup_inputs(seed: int=0):
    np.random.seed(seed)
    _w = jnp.asarray

    def _rec_inputs():
        import jax
        import jax.numpy as jnp
        _rk = jax.random.key(seed)
        x = -0.0005207 + 1.001 * jax.random.normal(jax.random.fold_in(_rk, 1), (32, 64, 256), jnp.float32)
        _lenS = 64 - jax.random.randint(jax.random.fold_in(_rk, 7), (32,), 0, max(1, 64 // 4) + 1, jnp.int32)
        _lenS2 = 64 - jax.random.randint(jax.random.fold_in(_rk, 8), (32,), 0, max(1, 64 // 4) + 1, jnp.int32)
        fside_Bx8_0 = jax.random.uniform(jax.random.fold_in(_rk, 11), (32, 8), jnp.float32, 0.0, 0.556406)
        condB_sharedgateprob = jax.random.uniform(jax.random.fold_in(_rk, 12), (32,), jnp.float32, 0.0, 0.794948)
        itok_B_0_2 = jax.random.randint(jax.random.fold_in(_rk, 13), (32,), 0, 3, jnp.int32)
        return (x, fside_Bx8_0, condB_sharedgateprob, itok_B_0_2)
    x, fside_Bx8_0, condB_sharedgateprob, itok_B_0_2 = _rec_inputs()

    def _L0_cond_setup():
        import jax, jax.numpy as jnp
        import numpy as np
        E, B, S, D, F = (8, 2, 256, 256, 1024)
        key = jax.random.key(seed)
        ks = jax.random.split(key, 9)
        sc_d = 1.0 / np.sqrt(D)
        sc_f = 1.0 / np.sqrt(F)
        hidden_states = jax.random.normal(ks[0], (B, S, D), dtype=jnp.float32)
        gating_probs = jax.nn.softmax(jax.random.normal(ks[1], (B, E), dtype=jnp.float32), axis=-1)
        shared_gate_prob = jax.nn.sigmoid(jax.random.normal(ks[2], (B, 1), dtype=jnp.float32))
        Wg = jax.random.normal(ks[3], (E, D, F), dtype=jnp.float32) * sc_d
        Wu = jax.random.normal(ks[4], (E, D, F), dtype=jnp.float32) * sc_d
        Wd = jax.random.normal(ks[5], (E, F, D), dtype=jnp.float32) * sc_f
        Sg = jax.random.normal(ks[6], (D, F), dtype=jnp.float32) * sc_d
        Su = jax.random.normal(ks[7], (D, F), dtype=jnp.float32) * sc_d
        Sd = jax.random.normal(ks[8], (F, D), dtype=jnp.float32) * sc_f
        return {'hidden_states': hidden_states, 'gating_probs': gating_probs, 'shared_gate_prob': shared_gate_prob, 'Wg': Wg, 'Wu': Wu, 'Wd': Wd, 'Sg': Sg, 'Su': Su, 'Sd': Sd}
    _L0_cond_all = _L0_cond_setup()
    _L0_cond_in = {k: v for k, v in _L0_cond_all.items() if k in ('Wg', 'Wu', 'Wd', 'Sg', 'Su', 'Sd')}
    del _L0_cond_all

    def _L0_attn_setup():
        import jax, jax.numpy as jnp
        import numpy as np
        B, T, C, H = (4, 256, 256, 16)
        D = C // H

        def _expmap0_split(u):
            mink = -u[..., :1] ** 2 + jnp.sum(u[..., 1:] ** 2, axis=-1, keepdims=True)
            nomin = jnp.sqrt(jnp.maximum(mink, 1e-08))
            time = jnp.cosh(nomin)
            space = jnp.sinh(nomin) * u[..., 1:] / nomin
            return (time, space)
        key = jax.random.key(seed)
        ks = jax.random.split(key, 6)
        s = 1.0 / np.sqrt(C)
        return {'x': jax.random.normal(ks[0], (B, T, C), jnp.float32), 'W_qkv': jax.random.normal(ks[1], (C, 3 * C), jnp.float32) * s, 'b_qkv': jnp.zeros((3 * C,), jnp.float32), 'W_out': jax.random.normal(ks[2], (C, C), jnp.float32) * s, 'b_out': jnp.zeros((C,), jnp.float32), 'w_sur': jax.random.normal(ks[3], (C,), jnp.float32) * s, 'b_sur': jnp.zeros((), jnp.float32), 'threshold': jnp.float32(0.5)}
    _L0_attn_all = _L0_attn_setup()
    _L0_attn_in = {k: v for k, v in _L0_attn_all.items() if k in ('W_qkv', 'b_qkv', 'W_out', 'b_out', 'w_sur', 'b_sur', 'threshold')}
    del _L0_attn_all

    def _L0_cond2_setup():
        import jax, jax.numpy as jnp
        import numpy as np
        B, S, D, F, E = (8, 512, 256, 1024, 5)

        def _dense(x, wi_, wo_):
            return jax.nn.relu(x @ wi_) @ wo_
        key = jax.random.key(seed)
        ks = jax.random.split(key, 9)
        sc = 0.02
        return {'hidden_states': jax.random.normal(ks[0], (B, S, D), jnp.float32), 'type_label': jax.random.randint(ks[1], (B,), 0, E, jnp.int32), 'wi': jax.random.normal(ks[2], (E, D, F), jnp.float32) * sc, 'wo': jax.random.normal(ks[3], (E, F, D), jnp.float32) * sc, 'swi': jax.random.normal(ks[4], (2, D, F), jnp.float32) * sc, 'swo': jax.random.normal(ks[5], (2, F, D), jnp.float32) * sc, 'g1': jax.random.normal(ks[6], (3 * D, D), jnp.float32) * sc, 'g2': jax.random.normal(ks[7], (D, 3), jnp.float32) * sc}
    _L0_cond2_all = _L0_cond2_setup()
    _L0_cond2_in = {k: v for k, v in _L0_cond2_all.items() if k in ('wi', 'wo', 'swi', 'swo', 'g1', 'g2')}
    del _L0_cond2_all

    def _L0_ffn_setup():
        import jax, jax.numpy as jnp
        import numpy as np
        EPS = 1e-05

        def _layernorm(x, w, b):
            mu = jnp.mean(x, axis=-1, keepdims=True)
            var = jnp.mean((x - mu) ** 2, axis=-1, keepdims=True)
            return (x - mu) * jax.lax.rsqrt(var + EPS) * w + b

        def _rope_tables(T, D, base=10000.0):
            inv_freq = 1.0 / base ** (jnp.arange(0, D, 2, dtype=jnp.float32) / D)
            t = jnp.arange(T, dtype=jnp.float32)
            freqs = jnp.einsum('i,j->ij', t, inv_freq)
            emb = jnp.concatenate([freqs, freqs], axis=-1)
            return (jnp.cos(emb), jnp.sin(emb))

        def _rotate_half(x):
            x1, x2 = (x[..., :x.shape[-1] // 2], x[..., x.shape[-1] // 2:])
            return jnp.concatenate([-x2, x1], axis=-1)

        def _attn(x, ln_w, ln_b, conv_w, attn_w, proj_w, n_head):
            B, T, C = x.shape
            D = C // n_head
            h = _layernorm(x, ln_w, ln_b)
            hc = jnp.transpose(h, (0, 2, 1))
            hc = jnp.pad(hc, ((0, 0), (0, 0), (2, 0)))
            hc = jax.lax.conv_general_dilated(hc, conv_w, window_strides=(1,), padding='VALID', dimension_numbers=('NCH', 'OIH', 'NCH'), feature_group_count=C)
            h = jnp.transpose(hc, (0, 2, 1))
            qkv = h @ attn_w
            q, k, v = jnp.split(qkv, 3, axis=-1)
            q = q.reshape(B, T, n_head, D)
            k = k.reshape(B, T, n_head, D)
            v = v.reshape(B, T, n_head, D)
            cos, sin = _rope_tables(T, D)
            cos = cos[None, :, None, :]
            sin = sin[None, :, None, :]
            q = q * cos + _rotate_half(q) * sin
            k = k * cos + _rotate_half(k) * sin
            scores = jnp.einsum('bqhd,bkhd->bhqk', q, k) / jnp.sqrt(jnp.float32(D))
            causal = jnp.tril(jnp.ones((T, T), dtype=bool))
            scores = jnp.where(causal, scores, jnp.float32(-1e+30))
            p = jax.nn.softmax(scores, axis=-1)
            y = jnp.einsum('bhqk,bkhd->bqhd', p, v).reshape(B, T, C)
            return y @ proj_w

        def _moe(x, ln_w, ln_b, router_w, expert_wv, expert_proj):
            h = _layernorm(x, ln_w, ln_b)
            logits = h @ router_w
            expert_idx = jnp.argmax(logits, axis=-1)
            E = router_w.shape[-1]
            out = jnp.zeros_like(x)
            for e in range(E):
                gv = h @ expert_wv[e]
                gate_raw, value = jnp.split(gv, 2, axis=-1)
                y = gate_raw * jax.nn.sigmoid(gate_raw) * value @ expert_proj[e]
                out = out + jnp.where((expert_idx == e)[..., None], y, 0.0)
            return out
        C, H, E, B, T = (256, 16, 4, 4, 256)
        Dff = 4 * C
        key = jax.random.key(seed)
        ks = jax.random.split(key, 8)
        s = 0.02
        return {'x': jax.random.normal(ks[0], (B, T, C), dtype=jnp.float32), 'ln1_w': jnp.ones((C,), jnp.float32), 'ln1_b': jnp.zeros((C,), jnp.float32), 'ln2_w': jnp.ones((C,), jnp.float32), 'ln2_b': jnp.zeros((C,), jnp.float32), 'conv_w': jax.random.normal(ks[1], (C, 1, 3), dtype=jnp.float32) * 0.1, 'attn_w': jax.random.normal(ks[2], (C, 3 * C), dtype=jnp.float32) * s, 'proj_w': jax.random.normal(ks[3], (C, C), dtype=jnp.float32) * s, 'router_w': jax.random.normal(ks[4], (C, E), dtype=jnp.float32) * s, 'expert_wv': jax.random.normal(ks[5], (E, C, 2 * Dff), dtype=jnp.float32) * s, 'expert_proj': jax.random.normal(ks[6], (E, Dff, C), dtype=jnp.float32) * s}
    _L0_ffn_all = _L0_ffn_setup()
    _L0_ffn_in = {k: v for k, v in _L0_ffn_all.items() if k in ('ln1_w', 'ln1_b', 'ln2_w', 'ln2_b', 'conv_w', 'attn_w', 'proj_w', 'router_w', 'expert_wv', 'expert_proj')}
    del _L0_ffn_all
    return {'x': x, 'fside_Bx8_0': fside_Bx8_0, 'condB_sharedgateprob': condB_sharedgateprob, 'itok_B_0_2': itok_B_0_2, 'L0_cond_Wg': _L0_cond_in['Wg'], 'L0_cond_Wu': _L0_cond_in['Wu'], 'L0_cond_Wd': _L0_cond_in['Wd'], 'L0_cond_Sg': _L0_cond_in['Sg'], 'L0_cond_Su': _L0_cond_in['Su'], 'L0_cond_Sd': _L0_cond_in['Sd'], 'L0_attn_W_qkv': _L0_attn_in['W_qkv'], 'L0_attn_b_qkv': _L0_attn_in['b_qkv'], 'L0_attn_W_out': _L0_attn_in['W_out'], 'L0_attn_b_out': _L0_attn_in['b_out'], 'L0_attn_w_sur': _L0_attn_in['w_sur'], 'L0_attn_b_sur': _L0_attn_in['b_sur'], 'L0_attn_threshold': _L0_attn_in['threshold'], 'L0_cond2_wi': _L0_cond2_in['wi'], 'L0_cond2_wo': _L0_cond2_in['wo'], 'L0_cond2_swi': _L0_cond2_in['swi'], 'L0_cond2_swo': _L0_cond2_in['swo'], 'L0_cond2_g1': _L0_cond2_in['g1'], 'L0_cond2_g2': _L0_cond2_in['g2'], 'L0_ffn_ln1_w': _L0_ffn_in['ln1_w'], 'L0_ffn_ln1_b': _L0_ffn_in['ln1_b'], 'L0_ffn_ln2_w': _L0_ffn_in['ln2_w'], 'L0_ffn_ln2_b': _L0_ffn_in['ln2_b'], 'L0_ffn_conv_w': _L0_ffn_in['conv_w'], 'L0_ffn_attn_w': _L0_ffn_in['attn_w'], 'L0_ffn_proj_w': _L0_ffn_in['proj_w'], 'L0_ffn_router_w': _L0_ffn_in['router_w'], 'L0_ffn_expert_wv': _L0_ffn_in['expert_wv'], 'L0_ffn_expert_proj': _L0_ffn_in['expert_proj']}

def reference(x, fside_Bx8_0, condB_sharedgateprob, itok_B_0_2, L0_cond_Wg, L0_cond_Wu, L0_cond_Wd, L0_cond_Sg, L0_cond_Su, L0_cond_Sd, L0_attn_W_qkv, L0_attn_b_qkv, L0_attn_W_out, L0_attn_b_out, L0_attn_w_sur, L0_attn_b_sur, L0_attn_threshold, L0_cond2_wi, L0_cond2_wo, L0_cond2_swi, L0_cond2_swo, L0_cond2_g1, L0_cond2_g2, L0_ffn_ln1_w, L0_ffn_ln1_b, L0_ffn_ln2_w, L0_ffn_ln2_b, L0_ffn_conv_w, L0_ffn_attn_w, L0_ffn_proj_w, L0_ffn_router_w, L0_ffn_expert_wv, L0_ffn_expert_proj):
    import jax
    import jax.numpy as jnp

    def _L0_cond_ref(hidden_states, gating_probs, shared_gate_prob, Wg, Wu, Wd, Sg, Su, Sd):
        import jax, jax.numpy as jnp
        import numpy as np
        E, B, S, D, F = (8, 2, 256, 256, 1024)
        h = hidden_states
        g = jnp.einsum('bsd,edf->ebsf', h, Wg)
        u = jnp.einsum('bsd,edf->ebsf', h, Wu)
        expert_outs = jnp.einsum('ebsf,efd->ebsd', jax.nn.silu(g) * u, Wd)
        expert_output = jnp.einsum('be,ebsd->bsd', gating_probs, expert_outs)
        shared = jnp.einsum('bsf,fd->bsd', jax.nn.silu(h @ Sg) * (h @ Su), Sd)
        sg = shared_gate_prob[:, :, None]
        return (1.0 - sg) * expert_output + sg * shared

    def _L0_attn_ref(x, W_qkv, b_qkv, W_out, b_out, w_sur, b_sur, threshold):
        import jax, jax.numpy as jnp
        import numpy as np
        B, T, C, H = (4, 256, 256, 16)
        D = C // H

        def _expmap0_split(u):
            mink = -u[..., :1] ** 2 + jnp.sum(u[..., 1:] ** 2, axis=-1, keepdims=True)
            nomin = jnp.sqrt(jnp.maximum(mink, 1e-08))
            time = jnp.cosh(nomin)
            space = jnp.sinh(nomin) * u[..., 1:] / nomin
            return (time, space)
        Bx, Tx, Cx = x.shape
        importance = jax.nn.sigmoid(jnp.einsum('btc,c->bt', x, w_sur) + b_sur)
        spikes = (importance > threshold).astype(x.dtype)
        spike_mask = spikes[:, None, :, None]
        qkv = x @ W_qkv + b_qkv
        qkv = qkv.reshape(Bx, Tx, 3, H, D).transpose(2, 0, 3, 1, 4)
        q, k, v = (qkv[0], qkv[1], qkv[2])
        tq, sq = _expmap0_split(q)
        tk, sk = _expmap0_split(k)
        neg_inner = jnp.einsum('bhie,bhje->bhij', tq, tk) - jnp.einsum('bhid,bhjd->bhij', sq, sk)
        dist = jnp.arccosh(jnp.maximum(neg_inner, 1.0 + 1e-07))
        scores = -dist ** 2 / np.sqrt(D)
        causal = jnp.tril(jnp.ones((Tx, Tx), dtype=bool))
        scores = jnp.where(causal[None, None], scores, -jnp.inf)
        attn = jax.nn.softmax(scores, axis=-1) * spike_mask
        y = jnp.einsum('bhij,bhjd->bhid', attn, v)
        y = y.transpose(0, 2, 1, 3).reshape(Bx, Tx, Cx)
        return y @ W_out + b_out

    def _L0_cond2_ref(hidden_states, type_label, wi, wo, swi, swo, g1, g2):
        import jax, jax.numpy as jnp
        import numpy as np
        B, S, D, F, E = (8, 512, 256, 1024, 5)

        def _dense(x, wi_, wo_):
            return jax.nn.relu(x @ wi_) @ wo_
        x = hidden_states
        s0 = _dense(x, swi[0], swo[0])
        s1 = _dense(x, swi[1], swo[1])
        wi_sel = wi[type_label]
        wo_sel = wo[type_label]
        h = jax.nn.relu(jnp.einsum('bsd,bdf->bsf', x, wi_sel))
        eo = jnp.einsum('bsf,bfd->bsd', h, wo_sel)
        gate_in = jnp.concatenate([eo[:, 0], s0[:, 0], s1[:, 0]], axis=-1)
        w = jax.nn.softmax(jax.nn.relu(gate_in @ g1) @ g2, axis=-1)
        w = w[:, :, None, None]
        return eo * w[:, 0] + s0 * w[:, 1] + s1 * w[:, 2]

    def _L0_ffn_ref(x, ln1_w, ln1_b, ln2_w, ln2_b, conv_w, attn_w, proj_w, router_w, expert_wv, expert_proj):
        import jax, jax.numpy as jnp
        import numpy as np
        EPS = 1e-05

        def _layernorm(x, w, b):
            mu = jnp.mean(x, axis=-1, keepdims=True)
            var = jnp.mean((x - mu) ** 2, axis=-1, keepdims=True)
            return (x - mu) * jax.lax.rsqrt(var + EPS) * w + b

        def _rope_tables(T, D, base=10000.0):
            inv_freq = 1.0 / base ** (jnp.arange(0, D, 2, dtype=jnp.float32) / D)
            t = jnp.arange(T, dtype=jnp.float32)
            freqs = jnp.einsum('i,j->ij', t, inv_freq)
            emb = jnp.concatenate([freqs, freqs], axis=-1)
            return (jnp.cos(emb), jnp.sin(emb))

        def _rotate_half(x):
            x1, x2 = (x[..., :x.shape[-1] // 2], x[..., x.shape[-1] // 2:])
            return jnp.concatenate([-x2, x1], axis=-1)

        def _attn(x, ln_w, ln_b, conv_w, attn_w, proj_w, n_head):
            B, T, C = x.shape
            D = C // n_head
            h = _layernorm(x, ln_w, ln_b)
            hc = jnp.transpose(h, (0, 2, 1))
            hc = jnp.pad(hc, ((0, 0), (0, 0), (2, 0)))
            hc = jax.lax.conv_general_dilated(hc, conv_w, window_strides=(1,), padding='VALID', dimension_numbers=('NCH', 'OIH', 'NCH'), feature_group_count=C)
            h = jnp.transpose(hc, (0, 2, 1))
            qkv = h @ attn_w
            q, k, v = jnp.split(qkv, 3, axis=-1)
            q = q.reshape(B, T, n_head, D)
            k = k.reshape(B, T, n_head, D)
            v = v.reshape(B, T, n_head, D)
            cos, sin = _rope_tables(T, D)
            cos = cos[None, :, None, :]
            sin = sin[None, :, None, :]
            q = q * cos + _rotate_half(q) * sin
            k = k * cos + _rotate_half(k) * sin
            scores = jnp.einsum('bqhd,bkhd->bhqk', q, k) / jnp.sqrt(jnp.float32(D))
            causal = jnp.tril(jnp.ones((T, T), dtype=bool))
            scores = jnp.where(causal, scores, jnp.float32(-1e+30))
            p = jax.nn.softmax(scores, axis=-1)
            y = jnp.einsum('bhqk,bkhd->bqhd', p, v).reshape(B, T, C)
            return y @ proj_w

        def _moe(x, ln_w, ln_b, router_w, expert_wv, expert_proj):
            h = _layernorm(x, ln_w, ln_b)
            logits = h @ router_w
            expert_idx = jnp.argmax(logits, axis=-1)
            E = router_w.shape[-1]
            out = jnp.zeros_like(x)
            for e in range(E):
                gv = h @ expert_wv[e]
                gate_raw, value = jnp.split(gv, 2, axis=-1)
                y = gate_raw * jax.nn.sigmoid(gate_raw) * value @ expert_proj[e]
                out = out + jnp.where((expert_idx == e)[..., None], y, 0.0)
            return out
        n_head = 16
        x = x + _attn(x, ln1_w, ln1_b, conv_w, attn_w, proj_w, n_head)
        x = x + _moe(x, ln2_w, ln2_b, router_w, expert_wv, expert_proj)
        return x
    x = x + _L0_attn_ref(_L0_cond_ref(x, fside_Bx8_0, condB_sharedgateprob[:, None], L0_cond_Wg, L0_cond_Wu, L0_cond_Wd, L0_cond_Sg, L0_cond_Su, L0_cond_Sd), L0_attn_W_qkv, L0_attn_b_qkv, L0_attn_W_out, L0_attn_b_out, L0_attn_w_sur, L0_attn_b_sur, L0_attn_threshold)
    x = x + _L0_ffn_ref(_L0_cond2_ref(x, itok_B_0_2, L0_cond2_wi, L0_cond2_wo, L0_cond2_swi, L0_cond2_swo, L0_cond2_g1, L0_cond2_g2), L0_ffn_ln1_w, L0_ffn_ln1_b, L0_ffn_ln2_w, L0_ffn_ln2_b, L0_ffn_conv_w, L0_ffn_attn_w, L0_ffn_proj_w, L0_ffn_router_w, L0_ffn_expert_wv, L0_ffn_expert_proj)
    return x

_drawn_inputs = setup_inputs


def setup_inputs(seed=0):
    import zlib

    import numpy as np

    out = dict(_drawn_inputs(seed))
    spreads = {'L0_attn_b_qkv': (0.0, 0.1),
     'L0_attn_b_out': (0.0, 0.1),
     'L0_ffn_ln1_w': (1.0, 0.6),
     'L0_ffn_ln1_b': (0.0, 0.8),
     'L0_ffn_ln2_w': (1.0, 0.6),
     'L0_ffn_ln2_b': (0.0, 0.59)}
    factors = {'L0_cond2_g1': 8.0,
     'L0_cond2_g2': 8.0,
     'L0_ffn_conv_w': 3.344,
     'L0_ffn_attn_w': 3.176,
     'L0_ffn_proj_w': 3.512}
    for name, (base, spread) in spreads.items():
        noise = np.random.default_rng([zlib.crc32(name.encode()), seed]).standard_normal(out[name].shape)
        drawn = base * np.exp(spread * noise) if base else spread * noise
        out[name] = jnp.asarray(drawn.astype(out[name].dtype))
    for name, factor in factors.items():
        out[name] = (out[name] * factor).astype(out[name].dtype)
    return out
```

```python
from contextlib import ExitStack

import numpy as np
import concourse.bass as bass
from concourse import mybir

F32 = mybir.dt.float32
F32R = mybir.dt.float32r
I32 = mybir.dt.int32
ALU = mybir.AluOpType
ACT = mybir.ActivationFunctionType
AX_X = mybir.AxisListType.X

P = 128
B, T, D = 32, 64, 256
N = B * T
KC = D // P
H, DH = 16, 16
F = 1024
FC = F // P
TW = 512
TT = N // TW
BT = TW // T
STEPS = TT * FC
NP = N // P
E_COND, E_TYPE, E_SHARED, E_MOE = 8, 5, 2, 4
SLOT = 256
SLOTS = max((N + E_TYPE * (SLOT - T)) // SLOT, (N + E_MOE * (SLOT - 1)) // SLOT)
LN_EPS = 1e-5
NEG = -1.0e30

C_ID, C_MEAN, C_CAUSAL, C_HEAD4, C_HALF, C_COS, C_SIN, C_BEFORE, C_EACH, C_IOTA, C_END = np.cumsum(
    [0, P, P, T, H // 4, 2, DH, DH, P, P, SLOTS]).tolist()


def shape_constants():
    c = np.zeros((P, C_END), np.float32)
    row = np.arange(P)
    c[:, C_ID:C_ID + P] = np.eye(P)
    c[:, C_MEAN:C_MEAN + P] = 1.0 / D
    c[:, C_CAUSAL:C_CAUSAL + T] = np.where(np.arange(T)[None] <= (row % T)[:, None], 0.0, NEG)
    c[:, C_HEAD4:C_HEAD4 + H // 4] = (row % T // DH)[:, None] == np.arange(H // 4)[None]
    c[:, C_HALF:C_HALF + 2] = (row // T)[:, None] == np.arange(2)[None]
    inv = (1.0 / np.float32(10000.0) ** (np.arange(0, DH, 2, dtype=np.float32) / np.float32(DH))).astype(np.float32)
    ang = ((row % T).astype(np.float32)[:, None] * inv[None]).astype(np.float32)
    c[:, C_COS:C_COS + DH] = np.concatenate([np.cos(ang), np.cos(ang)], 1)
    c[:, C_SIN:C_SIN + DH] = np.concatenate([-np.sin(ang), np.sin(ang)], 1)
    c[:, C_BEFORE:C_BEFORE + P] = (row[:, None] < row[None]) / SLOT
    c[:, C_EACH:C_EACH + P] = 1.0 / SLOT
    c[:, C_IOTA:C_IOTA + SLOTS] = np.arange(SLOTS)
    return c


class Memory:
    pass


class StageSemaphores:

    def __init__(self, nc, tag):
        self.nc, self.tag, self.held = nc, tag, []

    def __call__(self, name):
        self.held.append(self.nc.alloc_semaphore(name=f"{self.tag}_{name}"))
        return self.held[-1]

    def give_back(self):
        self.nc.clear_and_free_semaphores(self.held)
        self.nc.all_engine_barrier()


def ffn(nc, m, tag, swiglu, groups, gate, targets, x_hi, x_lo):
    n = sum(g[0] for g in groups)
    ups = 2 if swiglu else 1
    sem = StageSemaphores(nc, tag)
    up_loaded, dn_loaded = sem("up_loaded"), sem("dn_loaded")
    up_rounded, dn_rounded = sem("up_rounded"), sem("dn_rounded")
    up_ready, dn_ready = sem("up_ready"), sem("dn_ready")
    up_done, dn_done = sem("up_done"), sem("dn_done")
    act_done = sem("act_done")
    h_rounded, h_ready = sem("h_rounded"), sem("h_ready")
    up_free = sem("up_free") if swiglu else h_ready
    gated, summed = sem("gated"), sem("summed")
    with ExitStack() as s:
        sb = lambda name, shape, dt=F32: s.enter_context(nc.sbuf_tensor(f"{tag}_{name}", shape, dt))
        w_hi = sb("w_hi", [P, ups, KC, F], F32R)
        w_lo = sb("w_lo", [P, ups, KC, F], F32R)
        d_hi = sb("d_hi", [P, FC, D], F32R)
        d_lo = sb("d_lo", [P, FC, D], F32R)
        stage_up, stage_dn = sb("stage_up", [P, ups, KC, F]), sb("stage_dn", [P, FC, D])
        HB = 4
        h_hi = sb("h_hi", [P, HB, TW], F32R)
        h_lo = sb("h_lo", [P, HB, TW], F32R)
        silu = sb("silu", [P, 2, TW])
        h = sb("h", [P, 2, TW])
        part = sb("part", [P, 2, TW])
        up_ps = [[m.bank[0], m.bank[1]], [m.bank[2], m.bank[3]]]
        y_ps = [[m.bank[4], m.bank[5]], [m.bank[6], m.bank[7]]]

        with nc.Block() as block:
            @block.sync
            def _(sp):
                done = 0
                for count, up, down in groups:
                    def load(e, k):
                        if not (isinstance(k, int) and k == 0):
                            sp.wait_ge(up_ready, k * FC)
                        for j, src in enumerate(up(e)):
                            sp.dma_start(stage_up[:, j], src).then_inc(up_loaded, 16)
                        if not (isinstance(k, int) and k == 0):
                            sp.wait_ge(dn_ready, k * FC)
                        sp.dma_start(stage_dn[:], down(e)).then_inc(dn_loaded, 16)
                    first = 1 if done == 0 else 0
                    if first:
                        load(0, 0)
                    if count - first == 1:
                        load(first, done + first)
                    elif count - first > 1:
                        with sp.Fori(first, count) as e:
                            load(e, e + done)
                    done += count

            @block.gpsimd
            def _(pool):
                def split(e):
                    for i in range(FC + 3):
                        if i < FC:
                            c = slice(i * P, (i + 1) * P)
                            pool.wait_ge(up_rounded, FC * e + i + 1)
                            for j in range(ups):
                                ins = pool.tensor_tensor(w_lo[:, j, :, c], stage_up[:, j, :, c], w_hi[:, j, :, c],
                                                         ALU.subtract)
                            ins.then_inc(up_ready, 1)
                        if i >= 3:
                            k = i - 3
                            pool.wait_ge(dn_rounded, FC * e + k + 1)
                            pool.tensor_tensor(d_lo[:, k], stage_dn[:, k], d_hi[:, k],
                                               ALU.subtract).then_inc(dn_ready, 1)
                with pool.Fori(0, n) as e:
                    split(e)

            @block.tensor
            def _(pe):
                def up_step(e, st):
                    tt, f = divmod(st, FC)
                    if tt == 0:
                        pe.wait_ge(up_ready, FC * e + f + 1)
                    pe.wait_ge(up_free, STEPS * e + st + 1)
                    tok = slice(tt * TW, (tt + 1) * TW)
                    fs = slice(f * P, (f + 1) * P)
                    for j in range(ups):
                        i = 0
                        for k in range(KC):
                            for w, x in ((w_hi, x_hi), (w_hi, x_lo), (w_lo, x_hi)):
                                ins = pe.matmul(up_ps[st % 2][j], w[:, j, k, fs], x[:, k, tok],
                                                start=(i == 0), stop=(i == 3 * KC - 1))
                                i += 1
                    ins.then_inc(up_done, 1)

                def down_step(e, st):
                    tt, f = divmod(st, FC)
                    if tt == 0:
                        pe.wait_ge(dn_ready, FC * e + f + 1)
                    pe.wait_ge(h_ready, STEPS * e + st + 3)
                    if f == 0:
                        pe.wait_ge(gated, KC * (TT * e + tt + 1))
                    for c in range(KC):
                        cs = slice(c * P, (c + 1) * P)
                        for i, (w, x) in enumerate(((d_hi, h_hi), (d_hi, h_lo), (d_lo, h_hi))):
                            ins = pe.matmul(y_ps[tt % 2][c], w[:, f, cs], x[:, st % HB],
                                            start=(f == 0 and i == 0), stop=(f == FC - 1 and i == 2))
                    ins.then_inc(dn_done, 1)

                for st in range(2):
                    up_step(0, st)
                with pe.Fori(0, n - 1) as e:
                    for st in range(STEPS):
                        up_step(e if st + 2 < STEPS else e + 1, (st + 2) % STEPS)
                        down_step(e, st)
                for st in range(STEPS):
                    if st + 2 < STEPS:
                        up_step(n - 1, st + 2)
                    down_step(n - 1, st)

            @block.scalar
            def _(act):
                def round_up(e, i):
                    if i == 0:
                        act.wait_ge(up_loaded, 16 * ups * (e + 1))
                    c = slice(i * P, (i + 1) * P)
                    for j in range(ups):
                        ins = act.activation(w_hi[:, j, :, c], stage_up[:, j, :, c], ACT.Copy)
                    ins.then_inc(up_rounded, 1)

                def round_down(e, k):
                    if k == 0:
                        act.wait_ge(dn_loaded, 16 * (e + 1))
                    act.activation(d_hi[:, k], stage_dn[:, k], ACT.Copy).then_inc(dn_rounded, 1)

                def round_hidden(e, st):
                    act.wait_ge(up_free, STEPS * e + st + 3)
                    act.activation(h_hi[:, st % HB], h[:, st % 2], ACT.Copy).then_inc(h_rounded, 1)

                def expert(e, first, last):
                    for st in range(STEPS):
                        act.wait_ge(up_done, STEPS * e + st + 1)
                        if swiglu:
                            act.activation(silu[:, st % 2], up_ps[st % 2][0], ACT.Silu).then_inc(act_done, 1)
                            if st > 0:
                                round_hidden(e, st - 1)
                            elif not first:
                                round_hidden(e - 1, STEPS - 1)
                        else:
                            act.activation(h_hi[:, st % HB], up_ps[st % 2][0], ACT.Relu).then_inc(h_rounded, 1)
                        if not first and st < 3:
                            round_down(e, FC - 3 + st)
                        if not last and st >= STEPS - FC:
                            round_up(e + 1, st - (STEPS - FC))
                        if not last and st >= STEPS - FC + 3:
                            round_down(e + 1, st - (STEPS - FC + 3))

                for i in range(FC):
                    round_up(0, i)
                for i in range(FC):
                    round_down(0, i)
                expert(0, True, False)
                if n > 2:
                    with act.Fori(1, n - 1) as e:
                        expert(e, False, False)
                expert(n - 1, False, True)
                if swiglu:
                    round_hidden(n - 1, STEPS - 1)

            @block.vector
            def _(dve):
                if swiglu:
                    dve.nop().then_inc(up_free, 2)
                dve.nop().then_inc(h_ready, 2)
                dve.nop().then_inc(gated, 2 * KC)

                def split(e, st, offset=0):
                    g = STEPS * e + st
                    dve.wait_ge(h_rounded, g + 1)
                    if swiglu:
                        dve.tensor_tensor(h_lo[:, st % HB], h[:, st % 2], h_hi[:, st % HB],
                                          ALU.subtract).then_inc(h_ready, 1)
                    else:
                        dve.scalar_tensor_tensor(h_lo[:, st % HB], up_ps[st % 2][0], 0.0, h_hi[:, st % HB],
                                                 ALU.max, ALU.subtract).then_inc(h_ready, 1)

                def take(e, tt, target):
                    dve.wait_ge(dn_done, STEPS * e + FC * (tt + 1))
                    tok = slice(tt * TW, (tt + 1) * TW)
                    for c in range(KC):
                        if gate is None or target is not targets[0]:
                            dve.tensor_copy(target[:, c, tok], y_ps[tt % 2][c]).then_inc(gated, 1)
                            continue
                        v = "p (b t) -> p b t"
                        if not (isinstance(e, int) and e == 0 and tt == 0):
                            dve.wait_ge(summed, KC * (TT * e + tt - 1) + c + 1)
                        dve.tensor_tensor(part[:, c].rearrange(v, t=T), y_ps[tt % 2][c].rearrange(v, t=T),
                                          gate(e, tt), ALU.mult).then_inc(gated, 1)
                        dve.wait_ge(gated, KC * (TT * e + tt + 2) + c + 1)
                        dve.tensor_tensor(target[:, c, tok], target[:, c, tok], part[:, c], ALU.add).then_inc(summed, 1)

                def expert(e, first, target, before):
                    for st in range(STEPS):
                        tt, f = divmod(st, FC)
                        g = STEPS * e + st
                        if swiglu:
                            dve.wait_ge(h_ready, g + 1)
                            dve.wait_ge(act_done, g + 1)
                            dve.tensor_tensor(h[:, st % 2], silu[:, st % 2], up_ps[st % 2][1],
                                              ALU.mult).then_inc(up_free, 1)
                            if st > 0:
                                split(e, st - 1)
                            elif not first:
                                split(e - 1, STEPS - 1)
                        else:
                            split(e, st)
                        if f == 4:
                            if tt > 0:
                                take(e, tt - 1, target)
                            elif not first:
                                take(e - 1, TT - 1, before)

                done = 0
                before = None
                for (count, _, _), target in zip(groups, targets):
                    expert(done, done == 0, target, before)
                    if count == 2:
                        expert(done + 1, False, target, target)
                    elif count > 2:
                        with dve.Fori(done + 1, done + count) as e:
                            expert(e, False, target, target)
                    done += count
                    before = target
                if swiglu:
                    split(n - 1, STEPS - 1)
                take(n - 1, TT - 1, before)
    sem.give_back()


def attention(nc, m, tag, hyper, srcT, resT, w_qkv, w_out, b_qkv=None, b_out=None, w_sur=None):
    QK, G, GH = 2 * D, 4, H // 4
    HP = H // 2
    VW = DH + 1
    SUB = TW // P
    head4 = m.const[:, C_HEAD4:C_HEAD4 + GH]
    half2 = m.const[:, C_HALF:C_HALF + 2]
    causal = m.const[:, C_CAUSAL:C_CAUSAL + T].unsqueeze(1).to_broadcast([P, H, T])
    with ExitStack() as s:
        sb = lambda name, shape, dt=F32: s.enter_context(nc.sbuf_tensor(f"{tag}_{name}", shape, dt))
        qk = sb("qk", [P, NP, QK])
        v_blk = sb("v_blk", [P, NP, 2, HP, 2, VW])
        wo = sb("wo", [P, KC, D])
        if hyper:
            bo, spike = sb("bo", [P, KC]), sb("spike", [P, NP])
            q_space, q_time = sb("q_space", [P, NP, 2, H]), sb("q_time", [P, NP, 2, H])
            k_space, k_time = sb("k_space", [P, NP, H]), sb("k_time", [P, NP, H])

        sem = StageSemaphores(nc, tag + "_in")
        w_loaded, w_rounded, w_ready = sem("w_loaded"), sem("w_rounded"), sem("w_ready")
        src_rounded, src_ready = sem("src_rounded"), sem("src_ready")
        qk_done, v_done, qk_taken, v_taken = sem("qk_done"), sem("v_done"), sem("qk_taken"), sem("v_taken")
        v_doubled, v_blocked, ones_set = [sem(f"v_doubled{i}") for i in range(2)], sem("v_blocked"), sem("ones_set")
        spiked, sp_small, sp_steps = sem("spiked"), sem("spike_exp"), sem("spike_steps")
        squared, summed, made, norm_act, norm = (sem(n) for n in ("squared", "summed", "made", "norm_act", "norm_steps"))
        copied, turned_sin = sem("copied"), sem("times_sin")
        with ExitStack() as s1:
            sb1 = lambda name, shape, dt=F32: s1.enter_context(nc.sbuf_tensor(f"{tag}_{name}", shape, dt))
            wq = sb1("wq", [P, KC, 3 * D])
            wq_hi, wq_lo = sb1("wq_hi", [P, KC, 3 * D], F32R), sb1("wq_lo", [P, KC, 3 * D], F32R)
            src_hi, src_lo = sb1("src_hi", [P, 2, KC, TW], F32R), sb1("src_lo", [P, 2, KC, TW], F32R)
            v_row, v_two = sb1("v_row", [P, 2, SUB, D]), sb1("v_two", [P, 2, SUB, 2, D])
            if hyper:
                bias, ws, sig = sb1("bias", [P, 3 * D]), sb1("ws", [P, KC]), sb1("sig", [P, NP])
                sq, part = sb1("sq", [P, 2, QK]), sb1("part", [P, 2, 2 * H])
                r2, ln, root, inv, ep, en, sm, ser, below, cosh = (
                    sb1(n, [P, NP, 2 * H]) for n in ("r2", "ln", "root", "inv", "ep", "en", "sm", "ser", "below", "cosh"))
            else:
                x32, rot = sb1("x32", [P, 2, QK]), sb1("rot", [P, 2, QK])
            W_N = 16 * (5 if hyper else 2)
            SERIES = [2.0 / 362880, 2.0 / 5040, 2.0 / 120, 2.0 / 6, 2.0]
            qk_ps, v_ps = [m.bank[0], m.bank[1]], [m.bank[2][:, 0:D], m.bank[3][:, 0:D]]
            heads = lambda x: x.rearrange("p (h d) -> p h d", d=DH)
            with nc.Block() as block:
                @block.sync
                def _(sp):
                    sp.dma_start(wq[:], w_qkv.rearrange("(k p) n -> p k n", p=P)).then_inc(w_loaded, 16)
                    sp.dma_start(wo[:], w_out.rearrange("(k p) n -> p k n", p=P)).then_inc(w_loaded, 16)
                    if hyper:
                        col = lambda v: v.rearrange("(k p) -> p k", p=P)
                        sp.dma_start(bias[:], b_qkv.unsqueeze(0).to_broadcast([P, 3 * D])).then_inc(w_loaded, 16)
                        sp.dma_start(bo[:], col(b_out), allow_slow_non_contiguous=True).then_inc(w_loaded, 16)
                        sp.dma_start(ws[:], col(w_sur), allow_slow_non_contiguous=True).then_inc(w_loaded, 16)
                    for tt in range(TT):
                        q = tt % 2
                        sp.wait_ge(v_taken, SUB * (tt + 1))
                        if tt >= 2:
                            sp.wait_ge(v_blocked, tt - 1)
                        for j in range(2):
                            for h in range(2):
                                sp.dma_start(v_two[h * T:(h + 1) * T, q, :, j], v_row[j * T:(j + 1) * T, q])\
                                    .then_inc(v_doubled[q], 16)

                @block.tensor
                def _(pe):
                    pe.wait_ge(w_loaded, W_N)
                    if hyper:
                        for i in range(NP):
                            for k in range(KC):
                                ins = pe.matmul(m.bank[7][:, i:i + 1], srcT[:, k, i * P:(i + 1) * P], ws[:, k:k + 1],
                                                start=(k == 0), stop=(k == KC - 1))
                        ins.then_inc(spiked, 1)
                    pe.wait_ge(w_ready, 1)
                    for i in range(NP):
                        q, t = i // SUB % 2, slice(i % SUB * P, (i % SUB + 1) * P)
                        if i % SUB == 0:
                            pe.wait_ge(src_ready, i // SUB + 1)
                        for ps, done, taken, cols in ((qk_ps, qk_done, qk_taken, slice(0, QK)),
                                                      (v_ps, v_done, v_taken, slice(QK, 3 * D))):
                            if i >= 2:
                                pe.wait_ge(taken, i - 1)
                            n = 0
                            for k in range(KC):
                                for x, w in ((src_hi, wq_hi), (src_hi, wq_lo), (src_lo, wq_hi)):
                                    ins = pe.matmul(ps[i % 2], x[:, q, k, t], w[:, k, cols], start=(n == 0), stop=(n == 3 * KC - 1))
                                    n += 1
                            ins.then_inc(done, 1)

                @block.scalar
                def _(act):
                    act.preload_act_table_set("natural_log_exp_and_others")
                    act.wait_ge(w_loaded, W_N)
                    act.activation(wq_hi[:], wq[:], ACT.Copy).then_inc(w_rounded, 1)

                    def round_src(tt):
                        if tt >= 2:
                            act.wait_ge(v_done, SUB * (tt - 1))
                        act.activation(src_hi[:, tt % 2], srcT[:, :, tt * TW:(tt + 1) * TW], ACT.Copy).then_inc(src_rounded, 1)

                    round_src(0)
                    round_src(1)
                    if hyper:
                        act.wait_ge(spiked, 1)
                        act.activation(sig[:], m.bank[7][:, 0:NP], ACT.Exp, bias=m.neg_b_sur[:], scale=-1.0).then_inc(sp_small, 1)
                    for i in range(NP):
                        if hyper:
                            act.wait_ge(qk_taken, i + 1)
                            if i >= 2:
                                act.wait_ge(made, i - 1)
                            act.activation(sq[:, i % 2], qk[:, i], ACT.Square).then_inc(squared, 1)
                        else:
                            act.wait_ge(qk_done, i + 1)
                            if i >= 2:
                                act.wait_ge(turned_sin, i - 1)
                            act.activation(x32[:, i % 2], qk_ps[i % 2], ACT.Copy).then_inc(copied, 1)
                        if i % SUB == SUB - 1 and i // SUB + 2 < TT:
                            round_src(i // SUB + 2)
                    if hyper:
                        act.wait_ge(norm, 1)
                        act.activation(ln[:], r2[:], ACT.Ln).then_inc(norm_act, 1)
                        act.wait_ge(norm_act, 1)
                        act.activation(root[:], ln[:], ACT.Exp, scale=0.5).then_inc(norm_act, 1)
                        act.activation(inv[:], ln[:], ACT.Exp, scale=-0.5).then_inc(norm_act, 1)
                        act.wait_ge(norm_act, 2)
                        act.activation(ep[:], root[:], ACT.Exp).then_inc(norm_act, 1)
                        act.activation(en[:], root[:], ACT.Exp, scale=-1.0).then_inc(norm_act, 1)

                @block.vector
                def _(dve):
                    def split_src(tt):
                        dve.wait_ge(src_rounded, tt + 1)
                        if tt >= 2:
                            dve.wait_ge(v_done, SUB * (tt - 1))
                        dve.tensor_tensor(src_lo[:, tt % 2], srcT[:, :, tt * TW:(tt + 1) * TW], src_hi[:, tt % 2],
                                          ALU.subtract).then_inc(src_ready, 1)

                    dve.wait_ge(w_rounded, 1)
                    dve.tensor_tensor(wq_lo[:], wq[:], wq_hi[:], ALU.subtract).then_inc(w_ready, 1)
                    split_src(0)
                    split_src(1)

                    def spikes():
                        dve.wait_ge(sp_small, 1)
                        dve.tensor_scalar(sig[:], sig[:], 1.0, None, ALU.add).then_inc(sp_steps, 1)
                        dve.wait_ge(sp_steps, 1)
                        dve.reciprocal(sig[:], sig[:]).then_inc(sp_steps, 1)
                        dve.wait_ge(sp_steps, 2)
                        dve.tensor_scalar(spike[:], sig[:], m.threshold[:], None, ALU.is_gt)

                    def space_norm(i):
                        dve.wait_ge(squared, i + 1)
                        x = heads(sq[:, i % 2])
                        dve.tensor_reduce(part[:, i % 2], x[:, :, 1:], AX_X, ALU.add).then_inc(summed, 1)
                        dve.wait_ge(summed, i + 1)
                        dve.tensor_tensor(r2[:, i], part[:, i % 2], x[:, :, 0], ALU.subtract).then_inc(made, 1)

                    def rotate(i):
                        dve.wait_ge(qk_taken, i + 1)
                        dve.wait_ge(turned_sin, i + 1)
                        dve.tensor_tensor(qk[:, i], qk[:, i], rot[:, i % 2], ALU.add).then_inc(made, 1)

                    later = space_norm if hyper else rotate
                    for i in range(NP):
                        dve.wait_ge(qk_done, i + 1)
                        if hyper:
                            dve.tensor_tensor(qk[:, i], qk_ps[i % 2], bias[:, 0:QK], ALU.add).then_inc(qk_taken, 1)
                        else:
                            dve.wait_ge(copied, i + 1)
                            dve.tensor_tensor(heads(qk[:, i]), heads(qk_ps[i % 2]),
                                              m.const[:, C_COS:C_COS + DH].unsqueeze(1).to_broadcast([P, 2 * H, DH]),
                                              ALU.mult).then_inc(qk_taken, 1)
                        dve.wait_ge(v_done, i + 1)
                        tt = i // SUB
                        if i % SUB == 0 and tt >= 2:
                            dve.wait_ge(v_doubled[tt % 2], 64 * (tt // 2))
                        if hyper:
                            dve.tensor_tensor(v_row[:, tt % 2, i % SUB], v_ps[i % 2], bias[:, QK:], ALU.add).then_inc(v_taken, 1)
                        else:
                            dve.tensor_copy(v_row[:, tt % 2, i % SUB], v_ps[i % 2]).then_inc(v_taken, 1)
                        if i >= 1:
                            later(i - 1)
                        if i % SUB == SUB - 1 and tt + 2 < TT:
                            split_src(tt + 2)
                        if hyper and i == 0:
                            spikes()
                    later(NP - 1)
                    if hyper:
                        done = [0]

                        def link(ins):
                            done[0] += 1
                            ins.then_inc(norm, 1)
                            dve.wait_ge(norm, done[0])

                        dve.wait_ge(made, NP)
                        link(dve.tensor_scalar(r2[:], r2[:], 1e-8, None, ALU.max))
                        link(dve.tensor_scalar(sm[:], r2[:], 1.0, None, ALU.min))
                        link(dve.tensor_scalar(ser[:], sm[:], SERIES[0], SERIES[1], ALU.mult, ALU.add))
                        for coef in SERIES[2:]:
                            link(dve.tensor_tensor(ser[:], ser[:], sm[:], ALU.mult))
                            link(dve.tensor_scalar(ser[:], ser[:], coef, None, ALU.add))
                        link(dve.tensor_scalar(below[:], r2[:], 1.0, None, ALU.is_lt))
                        dve.wait_ge(norm_act, 5)
                        link(dve.tensor_tensor(sm[:], ep[:], en[:], ALU.subtract))
                        link(dve.tensor_tensor(sm[:], sm[:], inv[:], ALU.mult))
                        link(dve.tensor_tensor(ser[:], ser[:], sm[:], ALU.subtract))
                        link(dve.tensor_tensor(ser[:], ser[:], below[:], ALU.mult))
                        link(dve.tensor_tensor(ser[:], ser[:], sm[:], ALU.add))
                        link(dve.tensor_tensor(cosh[:], ep[:], en[:], ALU.add))
                        for j in range(2):
                            hj = half2[:, j:j + 1]
                            dve.tensor_scalar(q_space[:, :, j], ser[:, :, 0:H], hj, -0.5, ALU.mult, ALU.mult)
                            dve.tensor_scalar(q_time[:, :, j], cosh[:, :, 0:H], hj, 0.5, ALU.mult, ALU.mult)
                        dve.tensor_scalar(k_space[:], ser[:, :, H:], 0.5, None, ALU.mult)
                        dve.tensor_scalar(k_time[:], cosh[:, :, H:], 0.5, None, ALU.mult)

                @block.gpsimd
                def _(pool):
                    for i in range(NP):
                        for j in range(2):
                            ins = pool.tensor_copy(v_blk[:, i, j, :, :, DH], half2.unsqueeze(1).to_broadcast([P, HP, 2]))
                    ins.then_inc(ones_set, 1)

                    def times_sin(i):
                        pool.wait_ge(copied, i + 1)
                        if i >= 2:
                            pool.wait_ge(made, i - 1)
                        e = DH // 2
                        sin = m.const[:, C_SIN:C_SIN + DH].unsqueeze(1)
                        x, r = heads(x32[:, i % 2]), heads(rot[:, i % 2])
                        pool.tensor_tensor(r[:, :, 0:e], x[:, :, e:], sin[:, :, 0:e].to_broadcast([P, 2 * H, e]), ALU.mult)
                        pool.tensor_tensor(r[:, :, e:], x[:, :, 0:e], sin[:, :, e:].to_broadcast([P, 2 * H, e]),
                                           ALU.mult).then_inc(turned_sin, 1)

                    def block_values(tt):
                        pool.wait_ge(v_doubled[tt % 2], 64 * (tt // 2 + 1))
                        vo = v_blk[:, tt * SUB:(tt + 1) * SUB].rearrange("p i j g h v -> p (i j g) h v")[:, :, :, 0:DH]
                        vi = v_two[:, tt % 2].rearrange("p i j (g h d) -> p (i j g) h d", h=2, d=DH)
                        pool.tensor_tensor(vo, vi, half2.unsqueeze(1).unsqueeze(3).to_broadcast([P, SUB * 2 * HP, 2, DH]),
                                           ALU.mult).then_inc(v_blocked, 1)

                    for i in range(NP):
                        if not hyper:
                            times_sin(i)
                        if i % SUB == 1 and i >= SUB:
                            block_values(i // SUB - 1)
                    block_values(TT - 1)
        sem.give_back()

        if hyper:
            lag = dict(fetch=1, place=0, turn=0, q_blk=0, k_blk=0, score=0, clamp=0, root=1, root_add=1, dist=1, mask=2, top=2, shift=2,
                       prob=3, p_turn=3, p_take=3, mix=3, y=4, y_turn=4, y_take=4, out=4, add=5)
            order = dict(tensor="turn y_turn p_turn score mix out", scalar="root prob q_blk y_take p_take dist",
                         vector="place y add k_blk top clamp", gpsimd="mask root_add shift", sync="fetch")
        else:
            lag = dict(fetch=0, place=0, turn=0, q_blk=0, k_blk=0, score=0, clamp=1, top=1, shift=1, prob=1, p_turn=2, p_take=2, mix=2,
                       y=2, y_turn=3, y_take=3, out=3, add=3)
            order = dict(tensor="p_turn y_turn turn mix out score", scalar="p_take y_take q_blk prob",
                         vector="place clamp top k_blk add y", gpsimd="shift", sync="fetch")
        last = max(lag.values())
        sem = StageSemaphores(nc, tag)
        placed, turned, q_taken, k_blocked = sem("placed"), sem("turned"), sem("q_taken"), sem("k_blocked")
        scored, clamped, root_steps, rooted = sem("scored"), sem("clamped"), sem("root_steps"), sem("rooted")
        root_added, dist_steps, dist_done, masked = sem("root_added"), sem("dist_steps"), sem("dist_done"), sem("masked")
        max_done, shifted, prob_done = sem("max_done"), sem("shifted"), sem("prob_done")
        p_turned, p_taken, mixed, rec_steps = sem("p_turned"), sem("p_taken"), sem("mixed"), sem("rec_steps")
        v_fetched = [sem(f"v_fetched{q}") for q in range(2)]
        y_scaled, y_turned, y_taken, out_done, added = (sem(n) for n in ("y_scaled", "y_turned", "y_taken", "out_done", "added"))
        with ExitStack() as s2:
            sb2 = lambda name, shape: s2.enter_context(nc.sbuf_tensor(f"{tag}_{name}", shape, F32))
            q_exp, k_dup = sb2("q_exp", [P, 2, G, 2, T]), sb2("k_dup", [P, 2, G, 2, T])
            q_blk, k_blk = sb2("q_blk", [P, 2, G, P]), sb2("k_blk", [P, 2, G, GH, T])
            u, prob = sb2("u", [P, 2, H, T]), sb2("prob", [P, 2, H, T])
            pT = sb2("pT", [P, 2, HP, P])
            v_now = sb2("v_now", [P, 2, 2, HP, 2, VW])
            mx, rec = sb2("mx", [P, 2, H]), sb2("rec", [P, 2, H])
            y, yT = sb2("y", [P, 2, D]), sb2("yT", [P, 2, KC, P])
            if hyper:
                z, t = sb2("z", [P, 2, H, T]), sb2("t", [P, 2, H, T])
            qT_ps, kT_ps = m.bank[0], m.bank[1]
            s_ps = m.ps[:, 2:4, :].rearrange("p a (h t) -> p (a h) t", t=T)
            pT_ps = m.ps[:, 4:6, :].rearrange("p a n -> p (a n)")
            y_ps = m.bank[6][:, 0:H * VW]
            y_ps_h = y_ps.rearrange("p (h v) -> p h v", v=VW)
            yT_ps, o_ps = m.bank[7][:, 0:D], m.bank[7][:, D:2 * D]

            def wait(eng, s, count):
                if not isinstance(count, int) or count > 0:
                    eng.wait_ge(s, count)

            def run(eng, name, phases):
                mine = order[name].split()

                def step(it, half, par):
                    for ph in mine:
                        if not isinstance(it, int) or 0 <= it - lag[ph] < NP:
                            phases[ph](it - lag[ph], (par + lag[ph]) % 2, half + (par - lag[ph]) // 2)

                first = (last + 3) // 2 * 2
                for it in range(first):
                    step(it, it // 2, it % 2)
                with eng.Fori(first // 2, NP // 2) as half:
                    for par in range(2):
                        step(half * 2 + par, half, par)
                for it in range(NP, NP + last):
                    step(it, it // 2, it % 2)

            with nc.Block() as block:
                @block.sync
                def _(sp):
                    def fetch(i, q, nth):
                        wait(sp, mixed, i - 1)
                        sp.dma_start(v_now[:, q], v_blk[:, bass.ds(i, 1)].rearrange("p o j g h v -> p (o j) g h v"))\
                            .then_inc(v_fetched[q], 16)

                    run(sp, "sync", dict(fetch=fetch))

                @block.tensor
                def _(pe):
                    def turn(i, q, nth):
                        pe.wait_ge(placed, i + 1)
                        wait(pe, q_taken, i)
                        wait(pe, k_blocked, 2 * i)
                        for dst, x in ((qT_ps, q_exp), (kT_ps, k_dup)):
                            for g in range(G):
                                ins = pe.transpose(dst[:, g * P:(g + 1) * P],
                                                   x[:, q, g].rearrange("p j t -> p (j t)"), m.ident)
                        ins.then_inc(turned, 1)

                    def score(i, q, nth):
                        pe.wait_ge(q_taken, i + 1)
                        pe.wait_ge(k_blocked, 2 * (i + 1))
                        wait(pe, clamped if hyper else masked, i)
                        for g in range(G):
                            ins = pe.matmul(s_ps[:, g * GH:(g + 1) * GH, :], q_blk[:, q, g], k_blk[:, q, g],
                                            start=True, stop=True)
                        ins.then_inc(scored, 1)

                    def p_turn(i, q, nth):
                        pe.wait_ge(prob_done, i + 1)
                        wait(pe, p_taken, i)
                        for hp in range(HP):
                            ins = pe.transpose(pT_ps[:, hp * P:(hp + 1) * P],
                                               prob[:, q, 2 * hp:2 * hp + 2].rearrange("p h t -> p (h t)"), m.ident)
                        ins.then_inc(p_turned, 1)

                    def mix(i, q, nth):
                        pe.wait_ge(p_taken, i + 1)
                        pe.wait_ge(v_fetched[q], 16 * (nth + 1))
                        wait(pe, y_scaled, i)
                        for hp in range(HP):
                            for j in range(2):
                                ins = pe.matmul(y_ps[j * T:(j + 1) * T, hp * 2 * VW:(hp + 1) * 2 * VW],
                                                pT[:, q, hp, j * T:(j + 1) * T],
                                                v_now[:, q, j, hp].rearrange("p h v -> p (h v)"), start=True, stop=True)
                        ins.then_inc(mixed, 1)

                    def y_turn(i, q, nth):
                        pe.wait_ge(y_scaled, i + 1)
                        wait(pe, y_taken, i)
                        wait(pe, added, i)
                        for c in range(KC):
                            ins = pe.transpose(yT_ps[:, c * P:(c + 1) * P], y[:, q, c * P:(c + 1) * P], m.ident)
                        ins.then_inc(y_turned, 1)

                    def out(i, q, nth):
                        pe.wait_ge(y_taken, i + 1)
                        wait(pe, added, i)
                        for c in range(KC):
                            for k in range(KC):
                                ins = pe.matmul(o_ps[:, c * P:(c + 1) * P], wo[:, k, c * P:(c + 1) * P], yT[:, q, k],
                                                start=(k == 0), stop=(k == KC - 1))
                        ins.then_inc(out_done, 1)

                    run(pe, "tensor", dict(turn=turn, score=score, p_turn=p_turn, mix=mix, y_turn=y_turn, out=out))

                @block.scalar
                def _(act):
                    def take_q(i, q, nth):
                        act.wait_ge(turned, i + 1)
                        wait(act, scored, i - 1)
                        act.activation(q_blk[:, q].rearrange("p g n -> p (g n)"), qT_ps, ACT.Copy).then_inc(q_taken, 1)

                    def root(i, q, nth):
                        act.wait_ge(clamped, i + 1)
                        wait(act, masked, i - 1)
                        act.activation(t[:, q], z[:, q], ACT.Square).then_inc(root_steps, 1)
                        act.wait_ge(root_steps, 2 * i + 1)
                        act.activation(t[:, q], t[:, q], ACT.Ln, bias=m.minus_one[:]).then_inc(root_steps, 1)
                        act.wait_ge(root_steps, 2 * i + 2)
                        act.activation(t[:, q], t[:, q], ACT.Exp, scale=0.5).then_inc(rooted, 1)

                    def dist(i, q, nth):
                        act.wait_ge(root_added, i + 1)
                        act.activation(t[:, q], z[:, q], ACT.Ln).then_inc(dist_steps, 1)
                        act.wait_ge(dist_steps, i + 1)
                        act.activation(t[:, q], t[:, q], ACT.Square, scale=0.5).then_inc(dist_done, 1)

                    def exponential(i, q, nth):
                        act.wait_ge(shifted, i + 1)
                        wait(act, p_turned, i - 1)
                        act.activation(prob[:, q], u[:, q], ACT.Exp).then_inc(prob_done, 1)

                    def p_take(i, q, nth):
                        act.wait_ge(p_turned, i + 1)
                        wait(act, mixed, i - 1)
                        act.activation(pT[:, q].rearrange("p h n -> p (h n)"), pT_ps, ACT.Copy).then_inc(p_taken, 1)

                    def y_take(i, q, nth):
                        act.wait_ge(y_turned, i + 1)
                        wait(act, out_done, i - 1)
                        act.activation(yT[:, q].rearrange("p c n -> p (c n)"), yT_ps, ACT.Copy).then_inc(y_taken, 1)

                    run(act, "scalar", dict(q_blk=take_q, root=root, dist=dist, prob=exponential, p_take=p_take, y_take=y_take))

                @block.vector
                def _(dve):
                    def place(i, q, nth):
                        wait(dve, turned, i - 1)
                        if hyper:
                            at = bass.ds(i, 1)
                            bc = lambda f: f.rearrange("p o (g h) -> p (o g) h", h=GH).unsqueeze(3).to_broadcast([P, G, GH, DH - 1])
                            cp = lambda f: f.rearrange("p o (g h) -> p (o g) h", h=GH)
                            x = qk[:, at].rearrange("p o (g h d) -> p (o g) h d", h=GH, d=DH)
                            for j in range(2):
                                qo = q_exp[:, q, :, j].rearrange("p g (h d) -> p g h d", d=DH)
                                ko = k_dup[:, q, :, j].rearrange("p g (h d) -> p g h d", d=DH)
                                dve.tensor_tensor(qo[:, :, :, 1:], x[:, 0:G, :, 1:], bc(q_space[:, at, j]), ALU.mult)
                                dve.tensor_tensor(ko[:, :, :, 1:], x[:, G:, :, 1:], bc(k_space[:, at]), ALU.mult)
                                dve.tensor_copy(qo[:, :, :, 0], cp(q_time[:, at, j]))
                                ins = dve.tensor_copy(ko[:, :, :, 0], cp(k_time[:, at]))
                        else:
                            x = qk[:, bass.ds(i, 1)].rearrange("p o (g n) -> p (o g) n", n=T).unsqueeze(2)
                            shape = [P, G, 2, T]
                            dve.tensor_tensor(q_exp[:, q], x[:, 0:G].to_broadcast(shape),
                                              half2.unsqueeze(1).unsqueeze(3).to_broadcast(shape), ALU.mult)
                            ins = dve.tensor_copy(k_dup[:, q], x[:, G:].to_broadcast(shape))
                        ins.then_inc(placed, 1)

                    def block_k(i, q, nth):
                        dve.wait_ge(turned, i + 1)
                        wait(dve, scored, i - 1)
                        for j in range(2):
                            r = slice(j * T, (j + 1) * T)
                            kj = kT_ps[r].rearrange("p (g j t) -> p g j t", g=G, j=2)[:, :, j]
                            dve.tensor_tensor(k_blk[r, q], kj.unsqueeze(2).to_broadcast([T, G, GH, T]),
                                              head4[r].unsqueeze(1).unsqueeze(3).to_broadcast([T, G, GH, T]),
                                              ALU.mult).then_inc(k_blocked, 1)

                    def clamp(i, q, nth):
                        dve.wait_ge(scored, i + 1)
                        if hyper:
                            wait(dve, dist_done, i - 1)
                            dve.tensor_scalar(z[:, q], s_ps, float(np.float32(1.0 + 1e-7)), None, ALU.max).then_inc(clamped, 1)
                        else:
                            wait(dve, prob_done, i - 1)
                            dve.scalar_tensor_tensor(u[:, q], s_ps, DH ** -0.5, causal, ALU.mult, ALU.add).then_inc(masked, 1)

                    def top(i, q, nth):
                        dve.wait_ge(masked, i + 1)
                        wait(dve, shifted, i - 1)
                        dve.tensor_reduce(mx[:, q], u[:, q], AX_X, ALU.max).then_inc(max_done, 1)

                    per = 2 if hyper else 1

                    def scale_y(i, q, nth):
                        dve.wait_ge(mixed, i + 1)
                        wait(dve, y_scaled, i - 1)
                        dve.reciprocal(rec[:, q], y_ps_h[:, :, DH]).then_inc(rec_steps, 1)
                        dve.wait_ge(rec_steps, per * i + 1)
                        if hyper:
                            dve.tensor_scalar(rec[:, q], rec[:, q], spike[:, bass.ds(i, 1)], None, ALU.mult).then_inc(rec_steps, 1)
                            dve.wait_ge(rec_steps, per * i + 2)
                        wait(dve, y_turned, i - 1)
                        dve.tensor_tensor(y[:, q].rearrange("p (h d) -> p h d", d=DH), y_ps_h[:, :, 0:DH],
                                          rec[:, q].unsqueeze(2).to_broadcast([P, H, DH]), ALU.mult).then_inc(y_scaled, 1)

                    def add(i, q, nth):
                        dve.wait_ge(out_done, i + 1)
                        for c in range(KC):
                            x = resT[:, c, bass.ds(i * P, P)]
                            op = o_ps[:, c * P:(c + 1) * P]
                            if hyper:
                                ins = dve.scalar_tensor_tensor(x, op, bo[:, c:c + 1], x, ALU.add, ALU.add)
                            else:
                                ins = dve.tensor_tensor(x, op, x, ALU.add)
                        ins.then_inc(added, 1)

                    run(dve, "vector", dict(place=place, k_blk=block_k, clamp=clamp, top=top, y=scale_y, add=add))

                @block.gpsimd
                def _(pool):
                    def root_add(i, q, nth):
                        pool.wait_ge(rooted, i + 1)
                        pool.tensor_tensor(z[:, q], z[:, q], t[:, q], ALU.add).then_inc(root_added, 1)

                    def mask(i, q, nth):
                        pool.wait_ge(dist_done, i + 1)
                        wait(pool, prob_done, i - 1)
                        pool.tensor_tensor(u[:, q], causal, t[:, q], ALU.subtract).then_inc(masked, 1)

                    def shift(i, q, nth):
                        pool.wait_ge(max_done, i + 1)
                        pool.tensor_tensor(u[:, q], u[:, q], mx[:, q].unsqueeze(2).to_broadcast([P, H, T]),
                                           ALU.subtract).then_inc(shifted, 1)

                    run(pool, "gpsimd", dict(root_add=root_add, mask=mask, shift=shift))
        sem.give_back()


def mix_gate(nc, m, g1, g2, eo, s0, s1):
    sem = StageSemaphores(nc, "mix")
    loaded, hid, hid_taken, logit, chain, e_done = (sem(n) for n in
                                                    ("loaded", "hidden", "hidden_taken", "logit", "chain", "exp"))
    spread, w_ready, scaled, steps = (sem(n) for n in ("spread", "w_ready", "scaled", "steps"))
    with ExitStack() as s:
        sb = lambda name, shape: s.enter_context(nc.sbuf_tensor(f"mix_{name}", shape, F32))
        G1, G2 = sb("g1", [P, 3 * KC, D]), sb("g2", [P, KC, 3])
        r1 = sb("r1", [P, KC, B])
        lg, top, tot = sb("lg", [B, 3]), sb("top", [B, 1]), sb("tot", [B, 1])
        dg = sb("dg", [B, 3, B])
        w = sb("w", [P, 3, B])
        firsts = [x[:, c].rearrange("p (b t) -> p b t", t=T)[:, :, 0] for x in (eo, s0, s1) for c in range(KC)]
        with nc.Block() as block:
            @block.sync
            def _(sp):
                sp.dma_start(G1[:], g1.rearrange("(k p) n -> p k n", p=P)).then_inc(loaded, 16)
                sp.dma_start(G2[:], g2.rearrange("(k p) n -> p k n", p=P)).then_inc(loaded, 16)

            @block.tensor
            def _(pe):
                pe.wait_ge(loaded, 32)
                for c in range(KC):
                    for k in range(3 * KC):
                        ins = pe.matmul(m.bank[c][:, 0:B], G1[:, k, c * P:(c + 1) * P], firsts[k],
                                        start=(k == 0), stop=(k == 3 * KC - 1))
                ins.then_inc(hid, 1)
                pe.wait_ge(hid_taken, KC)
                for c in range(KC):
                    ins = pe.matmul(m.bank[2][0:B, 0:3], r1[:, c], G2[:, c], start=(c == 0), stop=(c == KC - 1))
                ins.then_inc(logit, 1)
                pe.wait_ge(chain, 6)
                pe.matmul(m.bank[3][:, 0:3 * B], m.const[0:B, C_MEAN:C_MEAN + P], dg[:].rearrange("p j b -> p (j b)"),
                          start=True, stop=True).then_inc(spread, 1)

            @block.scalar
            def _(act):
                act.wait_ge(hid, 1)
                for c in range(KC):
                    act.activation(r1[:, c], m.bank[c][:, 0:B], ACT.Relu).then_inc(hid_taken, 1)
                act.wait_ge(chain, 2)
                act.activation(lg[:], lg[:], ACT.Exp).then_inc(e_done, 1)

            @block.vector
            def _(dve):
                def link(n, ins):
                    ins.then_inc(chain, 1)
                    dve.wait_ge(chain, n)
                dve.wait_ge(logit, 1)
                link(1, dve.tensor_reduce(top[:], m.bank[2][0:B, 0:3], AX_X, ALU.max))
                link(2, dve.tensor_scalar(lg[:], m.bank[2][0:B, 0:3], top[:], None, ALU.subtract))
                dve.wait_ge(e_done, 1)
                link(3, dve.tensor_reduce(tot[:], lg[:], AX_X, ALU.add))
                link(4, dve.reciprocal(tot[:], tot[:]))
                link(5, dve.tensor_scalar(lg[:], lg[:], tot[:], None, ALU.mult))
                link(6, dve.tensor_tensor(dg[:], lg[:].unsqueeze(2).to_broadcast([B, 3, B]),
                                          m.ident[0:B, 0:B].unsqueeze(1).to_broadcast([B, 3, B]), ALU.mult))
                dve.wait_ge(spread, 1)
                dve.tensor_scalar(w[:].rearrange("p j b -> p (j b)"), m.bank[3][:, 0:3 * B], float(D), None, ALU.mult)\
                   .then_inc(w_ready, 1)
                dve.wait_ge(w_ready, 1)
                for c in range(KC):
                    v = lambda x: x[:, c].rearrange("p (b t) -> p b t", t=T)
                    g = lambda j: w[:, j].unsqueeze(2).to_broadcast([P, B, T])
                    dve.tensor_tensor(v(eo), v(eo), g(0), ALU.mult).then_inc(steps, 1)
                    dve.tensor_tensor(v(s0), v(s0), g(1), ALU.mult).then_inc(steps, 1)
                    dve.wait_ge(steps, 4 * c + 2)
                    dve.tensor_tensor(v(eo), v(eo), v(s0), ALU.add).then_inc(steps, 1)
                    dve.wait_ge(steps, 4 * c + 3)
                    dve.wait_ge(scaled, c + 1)
                    dve.tensor_tensor(v(eo), v(eo), v(s1), ALU.add).then_inc(steps, 1)

            @block.gpsimd
            def _(pool):
                pool.wait_ge(w_ready, 1)
                for c in range(KC):
                    x = s1[:, c].rearrange("p (b t) -> p b t", t=T)
                    pool.tensor_tensor(x, x, w[:, 2].unsqueeze(2).to_broadcast([P, B, T]), ALU.mult).then_inc(scaled, 1)
    sem.give_back()


def layer_norm(nc, m, tag, srcT, ln_w, ln_b, conv_w=None, convT=None, router=None):
    sem = StageSemaphores(nc, tag)
    loaded, set_up = sem("loaded"), sem("set_up")
    summed, centred, squared, var_done = sem("summed"), sem("centred"), sem("squared"), sem("var_done")
    log_done, rstd_done, normed, h_done = sem("log_done"), sem("rstd_done"), sem("normed"), sem("h_done")
    conv_s, conv_done = sem("conv_steps"), sem("conv_done")
    logits, pick, turned, taken = sem("logits"), sem("pick"), sem("turned"), sem("taken")
    PAD = 2
    with ExitStack() as s:
        sb = lambda name, shape: s.enter_context(nc.sbuf_tensor(f"{tag}_{name}", shape, F32))
        wcol, bcol, eps = sb("w", [P, KC]), sb("b", [P, KC]), sb("eps", [P, 1])
        xc, sq, xn = sb("xc", [P, 2, KC, TW]), sb("sq", [P, 2, KC, TW]), sb("xn", [P, 2, KC, TW])
        rstd = sb("rstd", [P, 2, TW])
        n_load = 2
        if conv_w is not None:
            taps = sb("taps", [P, KC, 3])
            h = sb("h", [P, 2, KC, BT, PAD + T])
            h_out = lambda q, c: h[:, q, c, :, PAD:]
            n_load = 3
        else:
            w_r, rows, sel = router
            wr = sb("wr", [P, KC, E_MOE])
            h = sb("h", [P, 2, KC, TW])
            h_out = lambda q, c: h[:, q, c].rearrange("p (b t) -> p b t", t=T)
            SUB = TW // P
            lg, best = sb("lg", [P, 2, SUB, E_MOE]), sb("best", [P, 2, SUB])
            free = sb("free", [P, 2, SUB])
            n_load = 3
        mean = m.const[:, C_MEAN:C_MEAN + P]
        with nc.Block() as block:
            @block.sync
            def _(sp):
                col = lambda v: v.rearrange("(k p) -> p k", p=P)
                sp.dma_start(wcol[:], col(ln_w), allow_slow_non_contiguous=True).then_inc(loaded, 16)
                sp.dma_start(bcol[:], col(ln_b), allow_slow_non_contiguous=True).then_inc(loaded, 16)
                if conv_w is not None:
                    sp.dma_start(taps[:], conv_w.rearrange("(k p) o j -> p k (o j)", p=P)).then_inc(loaded, 16)
                else:
                    sp.dma_start(wr[:], w_r.rearrange("(k p) e -> p k e", p=P)).then_inc(loaded, 16)

            @block.gpsimd
            def _(pool):
                pool.memset(eps[:], LN_EPS).then_inc(set_up, 1)
                if conv_w is not None:
                    for q in range(2):
                        pool.memset(h[:, q, :, :, 0:PAD], 0.0).then_inc(set_up, 1)

            @block.tensor
            def _(pe):
                def means(t):
                    if t >= 2:
                        pe.wait_ge(centred, t - 1)
                    for c in range(KC):
                        ins = pe.matmul(m.bank[t % 2], mean, srcT[:, c, t * TW:(t + 1) * TW], start=(c == 0), stop=(c == KC - 1))
                    ins.then_inc(summed, 1)

                def variances(t):
                    pe.wait_ge(squared, t + 1)
                    if t >= 2:
                        pe.wait_ge(log_done, t - 1)
                    for c in range(KC):
                        ins = pe.matmul(m.bank[2 + t % 2], mean, sq[:, t % 2, c], start=(c == 0), stop=(c == KC - 1))
                    ins.then_inc(var_done, 1)

                def route(t):
                    if t == 0:
                        pe.wait_ge(loaded, 16 * n_load)
                    pe.wait_ge(h_done, KC * (t + 1))
                    if t >= 1:
                        pe.wait_ge(pick, 9 * t)
                    for i in range(SUB):
                        for c in range(KC):
                            ins = pe.matmul(m.bank[4][:, i * E_MOE:(i + 1) * E_MOE], h[:, t % 2, c, i * P:(i + 1) * P],
                                            wr[:, c], start=(c == 0), stop=(c == KC - 1))
                    ins.then_inc(logits, 1)
                    if t >= 1:
                        pe.wait_ge(taken, t)
                    for i in range(SUB):
                        for c in range(KC):
                            ins = pe.transpose(m.bank[5 + i // 2][:, (i % 2 * KC + c) * P:(i % 2 * KC + c + 1) * P],
                                               h[:, t % 2, c, i * P:(i + 1) * P], m.ident)
                    ins.then_inc(turned, 1)

                means(0)
                for t in range(TT):
                    if t + 1 < TT:
                        means(t + 1)
                    variances(t)
                    if conv_w is None and t >= 1:
                        route(t - 1)
                if conv_w is None:
                    route(TT - 1)

            @block.scalar
            def _(act):
                act.preload_act_table_set("natural_log_exp_and_others")
                act.wait_ge(set_up, 3 if conv_w is not None else 1)
                act.wait_ge(loaded, 16 * n_load)

                def take_rows(t):
                    act.wait_ge(turned, t + 1)
                    act.activation(rows[:, t * SUB:(t + 1) * SUB].rearrange("p (a i) d -> p a (i d)", a=2), m.ps[:, 5:7, :],
                                   ACT.Copy).then_inc(taken, 1)

                for t in range(TT):
                    q = t % 2
                    act.wait_ge(centred, t + 1)
                    if t >= 2:
                        act.wait_ge(var_done, t - 1)
                    act.activation(sq[:, q], xc[:, q], ACT.Square).then_inc(squared, 1)
                    act.wait_ge(var_done, t + 1)
                    if t >= 2:
                        act.wait_ge(normed, t - 1)
                    act.activation(rstd[:, q], m.bank[2 + q], ACT.Ln, bias=eps[:]).then_inc(log_done, 1)
                    act.wait_ge(log_done, t + 1)
                    act.activation(rstd[:, q], rstd[:, q], ACT.Exp, scale=-0.5).then_inc(rstd_done, 1)
                    act.wait_ge(normed, t + 1)
                    if t >= 2:
                        if conv_w is not None:
                            act.wait_ge(conv_done, t - 1)
                        else:
                            act.wait_ge(turned, t - 1)
                    for c in range(KC):
                        act.activation(h_out(q, c), xn[:, q, c].rearrange("p (b t) -> p b t", t=T), ACT.Identity,
                                       bias=bcol[:, c:c + 1], scale=wcol[:, c:c + 1]).then_inc(h_done, 1)
                    if conv_w is None and t >= 1:
                        take_rows(t - 1)
                if conv_w is None:
                    take_rows(TT - 1)

            @block.vector
            def _(dve):
                dve.wait_ge(loaded, 16 * n_load)

                def centre(t):
                    dve.wait_ge(summed, t + 1)
                    if t >= 2:
                        dve.wait_ge(normed, t - 1)
                    dve.tensor_tensor(xc[:, t % 2], srcT[:, :, t * TW:(t + 1) * TW],
                                      m.bank[t % 2].unsqueeze(1).to_broadcast([P, KC, TW]), ALU.subtract).then_inc(centred, 1)

                def choose(t):
                    q = t % 2
                    step = [9 * t]

                    def link(ins):
                        step[0] += 1
                        ins.then_inc(pick, 1)
                        dve.wait_ge(pick, step[0])
                    dve.wait_ge(logits, t + 1)
                    lp = m.bank[4][:, 0:SUB * E_MOE].rearrange("p (i e) -> p i e", e=E_MOE)
                    link(dve.tensor_reduce(best[:, q], lp, AX_X, ALU.max))
                    link(dve.tensor_tensor(lg[:, q], lp, best[:, q].unsqueeze(2).to_broadcast([P, SUB, E_MOE]), ALU.is_equal))
                    link(dve.tensor_scalar(free[:, q], lg[:, q, :, 0], -1.0, 1.0, ALU.mult, ALU.add))
                    link(dve.tensor_copy(sel[:, t * SUB:(t + 1) * SUB, 0], lg[:, q, :, 0]))
                    for e in range(1, E_MOE):
                        link(dve.tensor_tensor(sel[:, t * SUB:(t + 1) * SUB, e], lg[:, q, :, e], free[:, q], ALU.mult))
                        if e < E_MOE - 1:
                            link(dve.tensor_tensor(free[:, q], free[:, q], sel[:, t * SUB:(t + 1) * SUB, e], ALU.subtract))
                    assert step[0] == 9 * (t + 1)

                centre(0)
                for t in range(TT):
                    q = t % 2
                    tok = slice(t * TW, (t + 1) * TW)
                    if t + 1 < TT:
                        centre(t + 1)
                    dve.wait_ge(rstd_done, t + 1)
                    if t >= 2:
                        dve.wait_ge(h_done, KC * (t - 1))
                    dve.tensor_tensor(xn[:, q], xc[:, q], rstd[:, q].unsqueeze(1).to_broadcast([P, KC, TW]),
                                      ALU.mult).then_inc(normed, 1)
                    if conv_w is not None:
                        dve.wait_ge(h_done, KC * (t + 1))
                        for c in range(KC):
                            o = convT[:, c, tok].rearrange("p (b t) -> p b t", t=T)
                            dve.tensor_scalar(o, h[:, q, c, :, 2:2 + T], taps[:, c, 2:3], None, ALU.mult).then_inc(conv_s, 1)
                            for j in (1, 0):
                                dve.wait_ge(conv_s, 2 * (KC * t + c) + 2 - j)
                                ins = dve.scalar_tensor_tensor(o, h[:, q, c, :, j:j + T], taps[:, c, j:j + 1], o,
                                                               ALU.mult, ALU.add)
                                if j == 1:
                                    ins.then_inc(conv_s, 1)
                        ins.then_inc(conv_done, 1)
                    else:
                        choose(t)
    sem.give_back()


def route(nc, m, tag, sel, experts, rows, pos, slot_expert):
    sem = StageSemaphores(nc, tag)
    counted, ranked, totalled, chain, placed = (sem(n) for n in ("counted", "ranked", "totalled", "chain", "placed"))
    before = m.const[:, C_BEFORE:C_BEFORE + P]
    each = m.const[:, C_EACH:C_EACH + P]
    full = N // SLOT
    with ExitStack() as s:
        sb = lambda name, shape: s.enter_context(nc.sbuf_tensor(f"{tag}_{name}", shape, F32))
        count, more = sb("count", [P, experts]), sb("more", [P, experts, full])
        used, end, start = sb("used", [P, experts]), sb("end", [P, experts]), sb("start", [P, experts])
        place, at = sb("place", [P, NP, experts]), sb("at", [P, NP])
        past, owner = sb("past", [P, SLOTS, experts]), sb("owner", [P, SLOTS])
        rank_ps = m.bank[0][:, 0:NP * experts].rearrange("p (i e) -> p i e", e=experts)
        total_ps = m.bank[1][:, 0:experts]
        with nc.Block() as block:
            @block.tensor
            def _(pe):
                pe.matmul(m.bank[0][:, 0:NP * experts], before, sel[:].rearrange("p i e -> p (i e)"), start=True, stop=False)
                for j in range(NP - 1):
                    ins = pe.matmul(rank_ps[:, j + 1:], each, sel[:, j:j + 1].to_broadcast([P, NP - 1 - j, experts]),
                                    start=False, stop=(j == NP - 2))
                ins.then_inc(ranked, 1)
                pe.wait_ge(counted, 1)
                pe.matmul(total_ps, each, count[:], start=True, stop=True).then_inc(totalled, 1)

            @block.vector
            def _(dve):
                done = [0]

                def link(ins):
                    done[0] += 1
                    ins.then_inc(chain, 1)
                    dve.wait_ge(chain, done[0])

                dve.tensor_reduce(count[:], sel[:].rearrange("p i e -> p e i"), AX_X, ALU.add).then_inc(counted, 1)
                dve.wait_ge(totalled, 1)
                link(dve.tensor_tensor(more[:], total_ps.unsqueeze(2).to_broadcast([P, experts, full]),
                                       m.const[:, C_IOTA:C_IOTA + full].unsqueeze(1).to_broadcast([P, experts, full]),
                                       ALU.is_gt))
                link(dve.tensor_reduce(used[:], more[:], AX_X, ALU.add))
                link(dve.tensor_copy(end[:], used[:]))
                for e in range(1, experts):
                    link(dve.tensor_tensor(end[:, e:e + 1], end[:, e:e + 1], end[:, e - 1:e], ALU.add))
                link(dve.tensor_tensor(start[:], end[:], used[:], ALU.subtract))
                dve.wait_ge(ranked, 1)
                link(dve.tensor_tensor(place[:], rank_ps, start[:].unsqueeze(1).to_broadcast([P, NP, experts]), ALU.add))
                link(dve.tensor_tensor(place[:], place[:], sel[:], ALU.mult))
                link(dve.tensor_reduce(at[:], place[:], AX_X, ALU.add))
                dve.tensor_scalar(pos[:], at[:], float(SLOT), None, ALU.mult).then_inc(placed, 1)
                link(dve.tensor_tensor(past[:], m.const[:, C_IOTA:C_IOTA + SLOTS].unsqueeze(2).to_broadcast([P, SLOTS, experts]),
                                       end[:].unsqueeze(1).to_broadcast([P, SLOTS, experts]), ALU.is_ge))
                link(dve.tensor_reduce(owner[:], past[:], AX_X, ALU.add))
                dve.tensor_scalar(slot_expert[:], owner[:], float(experts - 1), None, ALU.min)

            @block.gpsimd
            def _(pool):
                pool.wait_ge(placed, 1)
                pool.wait_ge(m.cleared, 16)
                for i in range(NP):
                    pool.indirect_dma_start(m.x_sorted[:], bass.IndirectOffsetOnAxis(ap=pos[:, i:i + 1], axis=0),
                                            rows[:, i], None).then_inc(m.scattered, 16)
        m.scatters += NP
    sem.give_back()


def routed_ffn(nc, m, tag, swiglu, experts, up, down, slot_expert):
    ups = 2 if swiglu else 1
    n = SLOTS
    HALVES, LAG, UB, HB = SLOT // P, 3, 4, 4
    DN = LAG + 1
    sem = StageSemaphores(nc, tag)
    pair = lambda name: [sem(f"{name}{i}") for i in range(2)]
    x_loaded, up_loaded, dn_loaded, stored = pair("x_loaded"), pair("up_loaded"), pair("dn_loaded"), pair("stored")
    x_turned, x_rounded, x_ready = sem("x_turned"), sem("x_rounded"), sem("x_ready")
    up_rounded, dn_rounded = sem("up_rounded"), sem("dn_rounded")
    up_ready, dn_ready = sem("up_ready"), sem("dn_ready")
    up_done, dn_done, act_done = sem("up_done"), sem("dn_done"), sem("act_done")
    h_rounded, h_ready = sem("h_rounded"), sem("h_ready")
    up_free = sem("up_free") if swiglu else h_ready
    y_taken = sem("y_taken")
    with ExitStack() as s_:
        sb = lambda name, shape, dt=F32: s_.enter_context(nc.sbuf_tensor(f"{tag}_{name}", shape, dt))
        stage_up, stage_dn = sb("stage_up", [P, 2, ups, KC, F]), sb("stage_dn", [P, 2, FC, D])
        w_hi, w_lo = sb("w_hi", [P, ups, KC, F], F32R), sb("w_lo", [P, ups, KC, F], F32R)
        d_hi, d_lo = sb("d_hi", [P, FC, D], F32R), sb("d_lo", [P, FC, D], F32R)
        x_row = sb("x_row", [P, 2, HALVES, D])
        x_hi, x_lo = sb("x_hi", [P, 2, KC, SLOT], F32R), sb("x_lo", [P, 2, KC, SLOT], F32R)
        h_hi, h_lo = sb("h_hi", [P, HB, SLOT], F32R), sb("h_lo", [P, HB, SLOT], F32R)
        y_row = sb("y_row", [P, 2, HALVES, D])
        nought = sb("nought", [1, HALVES * D], F32R)
        if swiglu:
            silu, h = sb("silu", [P, 2, SLOT]), sb("h", [P, HB, SLOT])
        up_ps = [[m.bank[i][:, j * SLOT:(j + 1) * SLOT] for j in range(ups)] for i in range(UB)]
        y_ps = [m.bank[UB + q].rearrange("p (i d) -> p i d", d=D) for q in range(2)]
        x_ps = [m.bank[UB + 2 + q].rearrange("p (c t) -> p c t", c=KC) for q in range(2)]
        rows = lambda t, s: t[bass.ds(s * SLOT, SLOT)].rearrange("(i p) d -> p i d", p=P)
        fs = lambda f: slice(f * P, (f + 1) * P)

        def run(eng, slot):
            slot(0, 0, 0)
            full = (n - 3) // 2
            with eng.Fori(0, full) as pairs:
                slot(pairs * 2 + 1, pairs, 1)
                slot(pairs * 2 + 2, pairs + 1, 0)
            for s in range(2 * full + 1, n):
                slot(s, s // 2, s % 2)

        is_first = lambda s: isinstance(s, int) and s == 0
        is_last = lambda s: isinstance(s, int) and s == n - 1

        with nc.Block() as block:
            @block.sync
            def _(sp):
                def load(s, q):
                    e = sp.value_load(slot_expert[0:1, bass.ds(s, 1)], min_val=0, max_val=experts - 1)
                    again = not (isinstance(s, int) and s < 2)
                    if again:
                        sp.wait_ge(x_turned, s - 1)
                    sp.dma_start(x_row[:, q], rows(m.x_sorted, s)).then_inc(x_loaded[q], 16)
                    if again:
                        sp.wait_ge(up_ready, FC * (s - 1))
                    for j, src in enumerate(up(e)):
                        sp.dma_start(stage_up[:, q, j], src).then_inc(up_loaded[q], 16)
                    if again:
                        sp.wait_ge(dn_ready, FC * (s - 1))
                    sp.dma_start(stage_dn[:, q], down(e)).then_inc(dn_loaded[q], 16)

                def store(s, q):
                    sp.wait_ge(y_taken, s + 1)
                    sp.dma_start(rows(m.y_sorted, s), y_row[:, q]).then_inc(stored[q], 16)

                sp.wait_ge(m.scattered, 16 * m.scatters)
                BEHIND = 3
                for s in range(BEHIND):
                    load(s, s % 2)
                full = (n - BEHIND) // 2
                with sp.Fori(0, full) as pairs:
                    for u in range(2):
                        s = pairs * 2 + BEHIND + u
                        load(s, (BEHIND + u) % 2)
                        store(s - BEHIND, u)
                for s in range(BEHIND + 2 * full, n):
                    load(s, s % 2)
                    store(s - BEHIND, (s - BEHIND) % 2)
                for s in range(n - BEHIND, n):
                    store(s, s % 2)
                for q in range(2):
                    sp.wait_ge(stored[q], 16 * ((n + 1 - q) // 2))

            @block.gpsimd
            def _(pool):
                def up_lo(s, f, q):
                    pool.wait_ge(up_rounded, FC * s + f + 1)
                    pool.tensor_tensor(w_lo[:, :, :, fs(f)], stage_up[:, q, :, :, fs(f)], w_hi[:, :, :, fs(f)],
                                       ALU.subtract).then_inc(up_ready, 1)

                def dn_lo(s, f, q):
                    pool.wait_ge(dn_rounded, FC * s + f + 1)
                    pool.tensor_tensor(d_lo[:, f], stage_dn[:, q, f], d_hi[:, f], ALU.subtract).then_inc(dn_ready, 1)

                def slot(s, nth, q):
                    for f in range(FC):
                        if not is_last(s):
                            up_lo(s + 1, f, 1 - q)
                        if f < FC - DN:
                            dn_lo(s, f + DN, q)
                        elif not is_last(s):
                            dn_lo(s + 1, f + DN - FC, 1 - q)

                for f in range(FC):
                    up_lo(0, f, 0)
                for f in range(DN):
                    dn_lo(0, f, 0)
                run(pool, slot)

            @block.tensor
            def _(pe):
                def turn(s, nth, q):
                    pe.wait_ge(x_loaded[q], 16 * (nth + 1))
                    if not (isinstance(s, int) and s < 2):
                        pe.wait_ge(x_ready, s - 1)
                    for i in range(HALVES):
                        for c in range(KC):
                            ins = pe.transpose(x_ps[q][:, c, i * P:(i + 1) * P], x_row[:, q, i, fs(c)], m.ident)
                    ins.then_inc(x_turned, 1)

                def up_step(s, f, q):
                    g = FC * s + f
                    if f == 0:
                        pe.wait_ge(x_ready, s + 1)
                    pe.wait_ge(up_ready, g + 1)
                    pe.wait_ge(up_free, g + 1)
                    for j in range(ups):
                        i = 0
                        for k in range(KC):
                            for w, x in ((w_hi, x_hi), (w_hi, x_lo), (w_lo, x_hi)):
                                ins = pe.matmul(up_ps[f % UB][j], w[:, j, k, fs(f)], x[:, q, k],
                                                start=(i == 0), stop=(i == 3 * KC - 1))
                                i += 1
                    ins.then_inc(up_done, 1)

                def dn_step(s, f, q):
                    g = FC * s + f
                    pe.wait_ge(dn_ready, g + 1)
                    pe.wait_ge(h_ready, g + (1 if swiglu else 1 + UB))
                    if f == 0 and not (isinstance(s, int) and s < 2):
                        pe.wait_ge(y_taken, s - 1)
                    if f == 0:
                        pe.matmul(y_ps[q], nought[:, 0:P], nought[:], start=True, stop=False)
                    for i in range(HALVES):
                        for k, (x, w) in enumerate(((h_hi, d_hi), (h_lo, d_hi), (h_hi, d_lo))):
                            ins = pe.matmul(y_ps[q][:, i], x[:, f % HB, i * P:(i + 1) * P], w[:, f],
                                            start=False, stop=(f == FC - 1 and i == HALVES - 1 and k == 2))
                    if f == FC - 1:
                        ins.then_inc(dn_done, 1)

                def slot(s, nth, q):
                    for f in range(FC):
                        up_step(s, f, q)
                        if f == 4 and not is_last(s):
                            turn(s + 1, nth + q, 1 - q)
                        if f >= LAG:
                            dn_step(s, f - LAG, q)
                        elif not is_first(s):
                            dn_step(s - 1, f - LAG + FC, 1 - q)

                turn(0, 0, 0)
                run(pe, slot)
                for f in range(FC - LAG, FC):
                    dn_step(n - 1, f, (n - 1) % 2)

            @block.scalar
            def _(act):
                def round_x(s, q):
                    act.wait_ge(x_turned, s + 1)
                    act.activation(x_hi[:, q], x_ps[q], ACT.Copy).then_inc(x_rounded, 1)

                def round_up(s, nth, q, f):
                    if f == 0:
                        act.wait_ge(up_loaded[q], 16 * ups * (nth + 1))
                    act.activation(w_hi[:, :, :, fs(f)], stage_up[:, q, :, :, fs(f)], ACT.Copy).then_inc(up_rounded, 1)

                def round_hidden(s, f):
                    act.wait_ge(up_free, FC * s + f + 1 + UB)
                    act.activation(h_hi[:, f % HB], h[:, f % HB], ACT.Copy).then_inc(h_rounded, 1)

                def slot(s, nth, q):
                    for f in range(FC):
                        act.wait_ge(up_done, FC * s + f + 1)
                        if swiglu:
                            act.activation(silu[:, f % 2], up_ps[f % UB][0], ACT.Silu).then_inc(act_done, 1)
                            if f > 0:
                                round_hidden(s, f - 1)
                            elif not is_first(s):
                                round_hidden(s - 1, FC - 1)
                        else:
                            act.activation(h_hi[:, f % HB], up_ps[f % UB][0], ACT.Relu).then_inc(h_rounded, 1)
                        if not is_last(s):
                            round_up(s + 1, nth + q, 1 - q, f)
                            if f == 5:
                                round_x(s + 1, 1 - q)

                act.activation(nought[:], m.zero_row[0:1].unsqueeze(1).to_broadcast([1, HALVES, D]), ACT.Copy)
                round_x(0, 0)
                for f in range(FC):
                    round_up(0, 0, 0, f)
                run(act, slot)
                if swiglu:
                    round_hidden(n - 1, FC - 1)

            @block.vector
            def _(dve):
                dve.nop().then_inc(up_free, UB)

                def split_x(s, q):
                    dve.wait_ge(x_rounded, s + 1)
                    dve.tensor_tensor(x_lo[:, q], x_ps[q], x_hi[:, q], ALU.subtract).then_inc(x_ready, 1)

                def round_dn(s, nth, q, f):
                    if f == 0:
                        dve.wait_ge(dn_loaded[q], 16 * (nth + 1))
                    dve.tensor_copy(d_hi[:, f], stage_dn[:, q, f]).then_inc(dn_rounded, 1)

                def split_hidden(s, f):
                    dve.wait_ge(h_rounded, FC * s + f + 1)
                    if swiglu:
                        dve.tensor_tensor(h_lo[:, f % HB], h[:, f % HB], h_hi[:, f % HB], ALU.subtract).then_inc(h_ready, 1)
                    else:
                        dve.scalar_tensor_tensor(h_lo[:, f % HB], up_ps[f % UB][0], 0.0, h_hi[:, f % HB],
                                                 ALU.max, ALU.subtract).then_inc(h_ready, 1)

                def take(s, nth, q):
                    dve.wait_ge(dn_done, s + 1)
                    if not (isinstance(s, int) and s < 2):
                        dve.wait_ge(stored[q], 16 * nth)
                    dve.tensor_copy(y_row[:, q], y_ps[q]).then_inc(y_taken, 1)

                def slot(s, nth, q):
                    for f in range(FC):
                        if swiglu:
                            dve.wait_ge(act_done, FC * s + f + 1)
                            dve.tensor_tensor(h[:, f % HB], silu[:, f % 2], up_ps[f % UB][1], ALU.mult).then_inc(up_free, 1)
                            if f > 0:
                                split_hidden(s, f - 1)
                            elif not is_first(s):
                                split_hidden(s - 1, FC - 1)
                        else:
                            split_hidden(s, f)
                        if f < FC - DN:
                            round_dn(s, nth, q, f + DN)
                        elif not is_last(s):
                            round_dn(s + 1, nth + q, 1 - q, f + DN - FC)
                        if f == 4 and not is_first(s):
                            take(s - 1, nth + q - 1, 1 - q)
                        if f == 6 and not is_last(s):
                            split_x(s + 1, 1 - q)

                split_x(0, 0)
                for f in range(DN):
                    round_dn(0, 0, 0, f)
                run(dve, slot)
                if swiglu:
                    split_hidden(n - 1, FC - 1)
                take(n - 1, (n - 1) // 2, (n - 1) % 2)
    sem.give_back()


def turn_rows(nc, m, tag, src, rows):
    sem = StageSemaphores(nc, tag)
    turned, taken = sem("turned"), sem("taken")
    with nc.Block() as block:
        @block.tensor
        def _(pe):
            for i in range(NP // 2):
                if i >= 8:
                    pe.wait_ge(taken, i - 7)
                for j in range(2):
                    for c in range(KC):
                        t = (2 * i + j) * P
                        ins = pe.transpose(m.bank[i % 8][:, (j * KC + c) * P:(j * KC + c + 1) * P], src[:, c, t:t + P], m.ident)
                ins.then_inc(turned, 1)

        @block.scalar
        def _(act):
            for i in range(NP // 2):
                act.wait_ge(turned, i + 1)
                act.activation(rows[:, 2 * i:2 * i + 2], m.bank[i % 8].rearrange("p (j d) -> p j d", j=2), ACT.Copy).then_inc(taken, 1)
    sem.give_back()


def gather_turned(nc, m, tag, pos, dst):
    sem = StageSemaphores(nc, tag)
    turned, taken = sem("turned"), sem("taken")
    gathered = [sem(f"gathered{i}") for i in range(NP // 2)]
    with ExitStack() as s:
        y = s.enter_context(nc.sbuf_tensor(f"{tag}_y", [P, NP, D], F32))
        with nc.Block() as block:
            @block.gpsimd
            def _(pool):
                for i in range(NP):
                    pool.indirect_dma_start(y[:, i], None, m.y_sorted[:], bass.IndirectOffsetOnAxis(ap=pos[:, i:i + 1], axis=0))\
                        .then_inc(gathered[i // 2], 16)

            @block.tensor
            def _(pe):
                for i in range(NP // 2):
                    pe.wait_ge(gathered[i], 32)
                    for j in range(2):
                        for c in range(KC):
                            ins = pe.transpose(m.bank[i % 8][:, (c * 2 + j) * P:(c * 2 + j + 1) * P],
                                               y[:, 2 * i + j, c * P:(c + 1) * P], m.ident)
                    ins.then_inc(turned, 1)

            @block.scalar
            def _(act):
                for i in range(NP // 2):
                    act.wait_ge(turned, i + 1)
                    act.activation(dst[:, :, i * 2 * P:(i + 1) * 2 * P], m.bank[i % 8].rearrange("p (c t) -> p c t", c=KC),
                                   ACT.Copy).then_inc(taken, 1)
    sem.give_back()


def store(nc, m, a, b, pos, out):
    sem = StageSemaphores(nc, "store")
    added, turned, finished = sem("added"), sem("turned"), sem("finished")
    stored, gathered = [sem(f"stored{i}") for i in range(TT)], [sem(f"gathered{i}") for i in range(TT)]
    rows = out.rearrange("b t d -> (b t) d").rearrange("(i p) d -> p i d", p=P)
    SUB = TW // P
    with ExitStack() as s:
        total = s.enter_context(nc.sbuf_tensor("total", [P, 2, KC, TW], F32))
        o = s.enter_context(nc.sbuf_tensor("o_tok", [P, NP, D], F32))
        with nc.Block() as block:
            @block.gpsimd
            def _(pool):
                for i in range(NP):
                    pool.indirect_dma_start(o[:, i], None, m.y_sorted[:], bass.IndirectOffsetOnAxis(ap=pos[:, i:i + 1], axis=0))\
                        .then_inc(gathered[i // SUB], 16)

            @block.vector
            def _(dve):
                def add(t):
                    tok = slice(t * TW, (t + 1) * TW)
                    if t >= 2:
                        dve.wait_ge(turned, t - 1)
                    dve.tensor_tensor(total[:, t % 2], a[:, :, tok], b[:, :, tok], ALU.add).then_inc(added, 1)

                add(0)
                for t in range(TT):
                    if t + 1 < TT:
                        add(t + 1)
                    dve.wait_ge(turned, t + 1)
                    dve.wait_ge(gathered[t], 16 * SUB)
                    x = o[:, t * SUB:(t + 1) * SUB].rearrange("p (a i) d -> p a (i d)", a=2)
                    dve.tensor_tensor(x, x, m.ps[:, t % 2 * 2:t % 2 * 2 + 2, :], ALU.add).then_inc(finished, 1)

            @block.tensor
            def _(pe):
                for t in range(TT):
                    pe.wait_ge(added, t + 1)
                    if t >= 2:
                        pe.wait_ge(finished, t - 1)
                    for i in range(SUB):
                        for c in range(KC):
                            ins = pe.transpose(m.bank[t % 2 * 2 + i // 2][:, (i % 2 * KC + c) * P:(i % 2 * KC + c + 1) * P],
                                               total[:, t % 2, c, i * P:(i + 1) * P], m.ident)
                    ins.then_inc(turned, 1)

            @block.sync
            def _(sp):
                for t in range(TT):
                    sp.wait_ge(finished, t + 1)
                    sp.dma_start(rows[:, t * SUB:(t + 1) * SUB], o[:, t * SUB:(t + 1) * SUB]).then_inc(stored[t], 16)
                for t in range(TT):
                    sp.wait_ge(stored[t], 16)


def split_tokens(nc, m, tag, src, x_hi, x_lo, clear=None):
    sem = StageSemaphores(nc, tag)
    rounded = sem("rounded")
    with nc.Block() as block:
        @block.scalar
        def _(act):
            for t in range(TT):
                tok = slice(t * TW, (t + 1) * TW)
                act.activation(x_hi[:, :, tok], src[:, :, tok], ACT.Copy).then_inc(rounded, 1)

        @block.gpsimd
        def _(pool):
            if clear is not None:
                pool.memset(clear[:], 0.0)

        @block.vector
        def _(dve):
            for t in range(TT):
                tok = slice(t * TW, (t + 1) * TW)
                dve.wait_ge(rounded, t + 1)
                dve.tensor_tensor(x_lo[:, :, tok], src[:, :, tok], x_hi[:, :, tok], ALU.subtract)
    sem.give_back()


def load_inputs(nc, m, x):
    sem = StageSemaphores(nc, "load")
    const_loaded, turned, taken = sem("const_loaded"), sem("x_turned"), sem("x_taken")
    small_loaded, zeroed = sem("small_loaded"), sem("acc_zeroed")
    QT = 4
    x_loaded = [sem(f"x_loaded{q}") for q in range(QT)]
    with ExitStack() as s:
        x_tok = s.enter_context(nc.sbuf_tensor("x_tok", [P, NP, D], F32))
        with nc.Block() as block:
            @block.sync
            def _(sp):
                sp.dma_start(m.const[:], m.consts_dram).then_inc(const_loaded, 16)
                rows = x.rearrange("b t d -> (b t) d").rearrange("(i p) d -> p i d", p=P)
                for q in range(QT):
                    i = slice(q * NP // QT, (q + 1) * NP // QT)
                    sp.dma_start(x_tok[:, i], rows[:, i]).then_inc(x_loaded[q], 16)
                sp.wait_ge(zeroed, 2)
                sp.dma_start(m.x_sorted.rearrange("(i p) d -> p i d", p=P),
                             m.zero_row[:].unsqueeze(1).to_broadcast([P, SLOTS * SLOT // P, D])).then_inc(m.cleared, 16)

            @block.scalar
            def _(act):
                n = m.load_small(act, small_loaded)
                act.wait_ge(small_loaded, 16 * n)

            @block.gpsimd
            def _(pool):
                pool.memset(m.sumT[:], 0.0).then_inc(zeroed, 1)
                pool.memset(m.minus_one[:], -1.0)
                pool.memset(m.zero_row[:], 0.0).then_inc(zeroed, 1)

            @block.tensor
            def _(pe):
                pe.wait_ge(const_loaded, 16)
                for i in range(NP // 2):
                    if i % 2 == 0:
                        pe.wait_ge(x_loaded[i // 2], 16)
                    if i >= 8:
                        pe.wait_ge(taken, i - 7)
                    for j in range(2):
                        for c in range(KC):
                            ins = pe.transpose(m.bank[i % 8][:, (c * 2 + j) * P:(c * 2 + j + 1) * P],
                                               x_tok[:, 2 * i + j, c * P:(c + 1) * P], m.ident)
                    ins.then_inc(turned, 1)

            @block.vector
            def _(dve):
                for i in range(NP // 2):
                    dve.wait_ge(turned, i + 1)
                    dve.tensor_copy(m.xT[:, :, i * 2 * P:(i + 1) * 2 * P],
                                    m.bank[i % 8].rearrange("p (c t) -> p c t", c=KC)).then_inc(taken, 1)
                dve.wait_ge(zeroed, 1)
                dve.wait_ge(small_loaded, 16 * m.n_small)
                sg = m.gate_cond[:, E_COND]
                dve.tensor_scalar(m.not_shared[:], sg, -1.0, 1.0, ALU.mult, ALU.add).then_inc(m.g_small, 1)
                dve.wait_ge(m.g_small, 1)
                dve.tensor_tensor(m.gate_cond[:, 0:E_COND],
                                  m.probs[:].rearrange("p (b e) -> p e b", e=E_COND),
                                  m.not_shared[:].unsqueeze(1).to_broadcast([P, E_COND, B]), ALU.mult)
                for e in range(E_TYPE):
                    dve.tensor_scalar(m.type_sel[:, :, e], m.type_id[:], float(e), None, ALU.is_equal)
                dve.tensor_scalar(m.neg_b_sur[:], m.b_sur[:], -1.0, None, ALU.mult)
    sem.give_back()


def program(nc, a, out):
    with ExitStack() as ctx:
        m = Memory()
        sb = lambda name, shape, dt=F32: ctx.enter_context(nc.sbuf_tensor(name, shape, dt))
        ps = ctx.enter_context(nc.psum_tensor("ps", [P, 8, 512], F32))
        m.ps = ps
        m.bank = [ps[:, i, :] for i in range(8)]
        m.consts_dram = a["constants"]
        m.xT = sb("xT", [P, KC, N])
        m.sumT = sb("sumT", [P, KC, N])
        m.const = sb("const", [P, C_END])
        m.ident = m.const[:, C_ID:C_ID + P]
        m.gate_cond = sb("gate_cond", [P, E_COND + 1, B])
        m.probs = sb("probs", [P, B * E_COND])
        m.not_shared = sb("not_shared", [P, B])
        m.type_id = sb("types", [P, NP], I32)
        m.type_sel = sb("type_sel", [P, NP, E_TYPE])
        m.zero_row = sb("zero_row", [P, D])
        m.x_sorted = nc.dram_tensor("x_sorted", [SLOTS * SLOT, D], F32, kind="Internal").ap()
        m.y_sorted = nc.dram_tensor("y_sorted", [SLOTS * SLOT, D], F32, kind="Internal").ap()
        m.cleared, m.scattered = (ctx.enter_context(nc.semaphore(n)) for n in ("cleared", "scattered"))
        m.scatters = 0
        m.pos = sb("pos", [P, NP], mybir.dt.uint32)
        m.slot_expert = sb("slot_expert", [P, SLOTS], I32)
        m.b_sur = sb("b_sur", [P, 1])
        m.neg_b_sur = sb("neg_b_sur", [P, 1])
        m.threshold = sb("threshold", [P, 1])
        m.minus_one = sb("minus_one", [P, 1])
        m.g_small = ctx.enter_context(nc.semaphore("gates_made"))

        def load_small(eng, sem):
            loads = [
                (m.probs[:], a["fside_Bx8_0"].rearrange("b e -> (b e)").unsqueeze(0).to_broadcast([P, B * E_COND])),
                (m.gate_cond[:, E_COND], a["condB_sharedgateprob"].unsqueeze(0).to_broadcast([P, B])),
                (m.type_id[0:T], a["itok_B_0_2"].rearrange("(i j) -> j i", j=2)[0:1].to_broadcast([T, NP])),
                (m.type_id[T:], a["itok_B_0_2"].rearrange("(i j) -> j i", j=2)[1:2].to_broadcast([T, NP])),
                (m.b_sur[:], a["L0_attn_b_sur"].unsqueeze(0).to_broadcast([P, 1])),
                (m.threshold[:], a["L0_attn_threshold"].unsqueeze(0).to_broadcast([P, 1])),
            ]
            for dst, src in loads:
                eng.dma_start(dst, src, allow_slow_non_contiguous=True).then_inc(sem, 16)
            m.n_small = len(loads)
            return len(loads)

        m.load_small = load_small
        load_inputs(nc, m, a["x"])

        up = lambda w: (lambda e: w[bass.ds(e, 1)].rearrange("o (k p) f -> p (o k) f", p=P))
        down = lambda w: (lambda e: w[bass.ds(e, 1)].rearrange("o (c p) d -> p (o c) d", p=P))
        one = lambda w: w.unsqueeze(0)
        with ExitStack() as s:
            x_hi = s.enter_context(nc.sbuf_tensor("a_x_hi", [P, KC, N], F32R))
            x_lo = s.enter_context(nc.sbuf_tensor("a_x_lo", [P, KC, N], F32R))
            split_tokens(nc, m, "a_x", m.xT, x_hi, x_lo)
            wg, wu, wd = a["L0_cond_Wg"], a["L0_cond_Wu"], a["L0_cond_Wd"]
            sg, su, sd = one(a["L0_cond_Sg"]), one(a["L0_cond_Su"]), one(a["L0_cond_Sd"])
            groups = [(E_COND, lambda e: (up(wg)(e), up(wu)(e)), down(wd)),
                      (1, lambda e: (up(sg)(e), up(su)(e)), down(sd))]
            gate = lambda e, tt: m.gate_cond[:, bass.ds(e, 1), tt * BT:(tt + 1) * BT].rearrange(
                "p o b -> p (o b)").unsqueeze(2).to_broadcast([P, BT, T])
            ffn(nc, m, "cond", True, groups, gate, [m.sumT, m.sumT], x_hi, x_lo)
        attention(nc, m, "hyp", True, m.sumT, m.xT, a["L0_attn_W_qkv"], a["L0_attn_W_out"], a["L0_attn_b_qkv"],
                  a["L0_attn_b_out"], a["L0_attn_w_sur"])

        with ExitStack() as s:
            sb = lambda name, shape, dt=F32: s.enter_context(nc.sbuf_tensor(name, shape, dt))
            s0, s1 = sb("s0", [P, KC, N]), sb("s1", [P, KC, N])
            with ExitStack() as f:
                x_hi = f.enter_context(nc.sbuf_tensor("c_x_hi", [P, KC, N], F32R))
                x_lo = f.enter_context(nc.sbuf_tensor("c_x_lo", [P, KC, N], F32R))
                split_tokens(nc, m, "c_x", m.xT, x_hi, x_lo)
                rows = f.enter_context(nc.sbuf_tensor("c_rows", [P, NP, D], F32))
                turn_rows(nc, m, "c_turn", m.xT, rows)
                route(nc, m, "c_route", m.type_sel, E_TYPE, rows, m.pos, m.slot_expert)
                nth = lambda w, i: w[i:i + 1]
                wi, wo, si, so = a["L0_cond2_wi"], a["L0_cond2_wo"], a["L0_cond2_swi"], a["L0_cond2_swo"]
                groups = [(1, lambda e, i=i: (up(nth(si, i))(e),), down(nth(so, i))) for i in range(E_SHARED)]
                ffn(nc, m, "dense", False, groups, None, [s0, s1], x_hi, x_lo)
            routed_ffn(nc, m, "typed", False, E_TYPE, lambda e: (up(wi)(e),), down(wo), m.slot_expert)
            gather_turned(nc, m, "c_back", m.pos, m.sumT)
            mix_gate(nc, m, a["L0_cond2_g1"], a["L0_cond2_g2"], m.sumT, s0, s1)
        with ExitStack() as s:
            convT = s.enter_context(nc.sbuf_tensor("convT", [P, KC, N], F32))
            layer_norm(nc, m, "ln1", m.sumT, a["L0_ffn_ln1_w"], a["L0_ffn_ln1_b"], conv_w=a["L0_ffn_conv_w"], convT=convT)
            attention(nc, m, "rope", False, convT, m.sumT, a["L0_ffn_attn_w"], a["L0_ffn_proj_w"])
        with ExitStack() as s:
            sel = s.enter_context(nc.sbuf_tensor("moe_sel", [P, NP, E_MOE], F32))
            rows = s.enter_context(nc.sbuf_tensor("moe_rows", [P, NP, D], F32))
            layer_norm(nc, m, "ln2", m.sumT, a["L0_ffn_ln2_w"], a["L0_ffn_ln2_b"], router=(a["L0_ffn_router_w"], rows, sel))
            route(nc, m, "e_route", sel, E_MOE, rows, m.pos, m.slot_expert)
            wv = a["L0_ffn_expert_wv"]
            halves = lambda e: tuple(up(wv)(e)[:, :, j * F:(j + 1) * F] for j in range(2))
            routed_ffn(nc, m, "moe", True, E_MOE, halves, down(a["L0_ffn_expert_proj"]), m.slot_expert)
        store(nc, m, m.xT, m.sumT, m.pos, out)


_INS = ['x', 'fside_Bx8_0', 'condB_sharedgateprob', 'itok_B_0_2', 'L0_cond_Wg', 'L0_cond_Wu', 'L0_cond_Wd',
        'L0_cond_Sg', 'L0_cond_Su', 'L0_cond_Sd', 'L0_attn_W_qkv', 'L0_attn_b_qkv', 'L0_attn_W_out', 'L0_attn_b_out',
        'L0_attn_w_sur', 'L0_attn_b_sur', 'L0_attn_threshold', 'L0_cond2_wi', 'L0_cond2_wo', 'L0_cond2_swi',
        'L0_cond2_swo', 'L0_cond2_g1', 'L0_cond2_g2', 'L0_ffn_ln1_w', 'L0_ffn_ln1_b', 'L0_ffn_ln2_w', 'L0_ffn_ln2_b',
        'L0_ffn_conv_w', 'L0_ffn_attn_w', 'L0_ffn_proj_w', 'L0_ffn_router_w', 'L0_ffn_expert_wv', 'L0_ffn_expert_proj']
_OUTS = [((B, T, D), 'float32')]


def kernel(**inputs):
    import concourse.bacc as bacc
    from concourse.bass_utils import run_bass_kernel_spmd as run

    nc = bacc.Bacc("TRN2", target_bir_lowering=False, num_devices=1)
    arrays, args = {}, {}
    given = dict(inputs, constants=shape_constants())
    for name in _INS + ["constants"]:
        v = np.ascontiguousarray(given[name])
        if v.ndim == 0:
            v = v.reshape(1)
        arrays[f"in_{name}"] = v
        args[name] = nc.dram_tensor(f"in_{name}", v.shape, mybir.dt.from_np(v.dtype), kind="ExternalInput").ap()
    shape, dtype = _OUTS[0]
    out = nc.dram_tensor("out_0", shape, mybir.dt.from_np(np.dtype(dtype)), kind="ExternalOutput").ap()
    program(nc, args, out)
    r = run(nc, [arrays], core_ids=[0])
    return r.results[0]["out_0"]
```

```python
from contextlib import ExitStack

import numpy as np
import concourse.bass as bass
from concourse import mybir

F32 = mybir.dt.float32
F32R = mybir.dt.float32r
I32 = mybir.dt.int32
ALU = mybir.AluOpType
ACT = mybir.ActivationFunctionType
AX_X = mybir.AxisListType.X

P = 128
B, T, D = 32, 64, 256
N = B * T
KC = D // P
H, DH = 16, 16
F = 1024
FC = F // P
TW = 512
TT = N // TW
BT = TW // T
STEPS = TT * FC
NP = N // P
E_COND, E_TYPE, E_SHARED, E_MOE = 8, 5, 2, 4
SLOT = 256
SLOTS = max((N + E_TYPE * (SLOT - T)) // SLOT, (N + E_MOE * (SLOT - 1)) // SLOT)
LN_EPS = 1e-5
NEG = -1.0e30

C_ID, C_MEAN, C_CAUSAL, C_HEAD4, C_HALF, C_COS, C_SIN, C_BEFORE, C_EACH, C_IOTA, C_ONE, C_TWICE, C_TOKEN, C_NONE, C_END = np.cumsum(
    [0, P, P, T, H // 4, 2, DH, DH, P, P, SLOTS, 2, T, NP, SLOTS * SLOT // P]).tolist()


def shape_constants():
    c = np.zeros((P, C_END), np.float32)
    row = np.arange(P)
    c[:, C_ID:C_ID + P] = np.eye(P)
    c[:, C_MEAN:C_MEAN + P] = 1.0 / D
    c[:, C_CAUSAL:C_CAUSAL + T] = np.where(np.arange(T)[None] <= (row % T)[:, None], 0.0, NEG)
    c[:, C_HEAD4:C_HEAD4 + H // 4] = (row % T // DH)[:, None] == np.arange(H // 4)[None]
    c[:, C_HALF:C_HALF + 2] = (row // T)[:, None] == np.arange(2)[None]
    inv = (1.0 / np.float32(10000.0) ** (np.arange(0, DH, 2, dtype=np.float32) / np.float32(DH))).astype(np.float32)
    ang = ((row % T).astype(np.float32)[:, None] * inv[None]).astype(np.float32)
    c[:, C_COS:C_COS + DH] = np.concatenate([np.cos(ang), np.cos(ang)], 1)
    c[:, C_SIN:C_SIN + DH] = np.concatenate([-np.sin(ang), np.sin(ang)], 1)
    c[:, C_BEFORE:C_BEFORE + P] = (row[:, None] < row[None]) / SLOT
    c[:, C_EACH:C_EACH + P] = 1.0 / SLOT
    c[:, C_ONE:C_ONE + 2] = 1.0
    c[:, C_IOTA:C_IOTA + SLOTS] = np.arange(SLOTS)
    c[:, C_TWICE:C_TWICE + T] = (row % T)[:, None] == np.arange(T)[None]
    c[:, C_TOKEN:C_TOKEN + NP] = np.arange(NP)[None] * P + row[:, None]
    c[:, C_NONE:C_NONE + SLOTS * SLOT // P] = N + np.arange(SLOTS * SLOT // P)[None] * P + row[:, None]
    return c


class Memory:
    pass


class StageSemaphores:

    def __init__(self, nc, tag):
        self.nc, self.tag, self.held = nc, tag, []

    def __call__(self, name):
        self.held.append(self.nc.alloc_semaphore(name=f"{self.tag}_{name}"))
        return self.held[-1]

    def give_back(self):
        self.nc.clear_and_free_semaphores(self.held)
        self.nc.all_engine_barrier()


class ExpertStage:

    def __init__(self, nc, ctx, tag, ups):
        self.up = ctx.enter_context(nc.sbuf_tensor(f"{tag}_stage_up", [P, ups, KC, F], F32))
        self.down = ctx.enter_context(nc.sbuf_tensor(f"{tag}_stage_dn", [P, FC, D], F32))
        self.up_loaded = ctx.enter_context(nc.semaphore(f"{tag}_up_loaded"))
        self.dn_loaded = ctx.enter_context(nc.semaphore(f"{tag}_dn_loaded"))

    def load_up(self, sp, sources):
        for j, src in enumerate(sources):
            sp.dma_start(self.up[:, j], src).then_inc(self.up_loaded, 16)

    def load_down(self, sp, source):
        sp.dma_start(self.down[:], source).then_inc(self.dn_loaded, 16)


class Beside:

    def tensor_early(self, pe):
        pass

    def vector_early(self, dve):
        pass

    def gpsimd_early(self, pool):
        pass

    def gpsimd_late(self, pool):
        pass

    def scalar_late(self, act):
        pass

    def sync_late(self, sp):
        pass


class WeightsBeside(Beside):

    def __init__(self, weights):
        self.sync_late, self.scalar_late, self.gpsimd_late = weights.load, weights.round, weights.split


class SortBeside(Beside):

    def __init__(self, m, places, rows, slots):
        self.m, self.places, self.rows, self.slots = m, places, rows, slots
        m.scatters += NP

    def tensor_early(self, pe):
        self.places.rank(pe)

    def vector_early(self, dve):
        self.places.place_all(dve, self.m.pos, self.m.slot_expert)

    def gpsimd_early(self, pool):
        pool.wait_ge(self.places.placed, 1)
        scatter(pool, self.m, self.slots, self.rows, self.m.pos)

    def sync_late(self, sp):
        sp.wait_ge(self.places.owned, 1)
        self.slots.load_first(sp)


def ffn(nc, m, tag, swiglu, groups, gate, targets, x_hi, x_lo, stage, beside):
    n = sum(g[0] for g in groups)
    ups = 2 if swiglu else 1
    sem = StageSemaphores(nc, tag)
    up_loaded, dn_loaded = stage.up_loaded, stage.dn_loaded
    up_rounded, dn_rounded = sem("up_rounded"), sem("dn_rounded")
    up_ready, dn_ready = sem("up_ready"), sem("dn_ready")
    up_done, dn_done = sem("up_done"), sem("dn_done")
    act_done = sem("act_done")
    h_rounded, h_ready = sem("h_rounded"), sem("h_ready")
    up_free = sem("up_free") if swiglu else h_ready
    gated, summed = sem("gated"), sem("summed")
    with ExitStack() as s:
        sb = lambda name, shape, dt=F32: s.enter_context(nc.sbuf_tensor(f"{tag}_{name}", shape, dt))
        w_hi = sb("w_hi", [P, ups, KC, F], F32R)
        w_lo = sb("w_lo", [P, ups, KC, F], F32R)
        d_hi = sb("d_hi", [P, FC, D], F32R)
        d_lo = sb("d_lo", [P, FC, D], F32R)
        stage_up, stage_dn = stage.up, stage.down
        HB = 4
        h_hi = sb("h_hi", [P, HB, TW], F32R)
        h_lo = sb("h_lo", [P, HB, TW], F32R)
        if swiglu:
            silu, h = sb("silu", [P, 2, TW]), sb("h", [P, 2, TW])
        if gate is not None:
            part = sb("part", [P, 2, TW])
        up_ps = [[m.bank[0], m.bank[1]], [m.bank[2], m.bank[3]]]
        y_ps = [[m.bank[4], m.bank[5]], [m.bank[6], m.bank[7]]]

        with nc.Block() as block:
            @block.sync
            def _(sp):
                done = 0
                for count, up, down in groups:
                    def load(e, k):
                        sp.wait_ge(up_ready, k * FC)
                        stage.load_up(sp, up(e))
                        sp.wait_ge(dn_ready, k * FC)
                        stage.load_down(sp, down(e))
                    first = 1 if done == 0 else 0
                    if count - first == 1:
                        load(first, done + first)
                    elif count - first > 1:
                        with sp.Fori(first, count) as e:
                            load(e, e + done)
                    done += count
                beside.sync_late(sp)

            @block.gpsimd
            def _(pool):
                def split(e):
                    for i in range(FC + 3):
                        if i < FC:
                            c = slice(i * P, (i + 1) * P)
                            pool.wait_ge(up_rounded, FC * e + i + 1)
                            for j in range(ups):
                                ins = pool.tensor_tensor(w_lo[:, j, :, c], stage_up[:, j, :, c], w_hi[:, j, :, c],
                                                         ALU.subtract)
                            ins.then_inc(up_ready, 1)
                        if i >= 3:
                            k = i - 3
                            pool.wait_ge(dn_rounded, FC * e + k + 1)
                            pool.tensor_tensor(d_lo[:, k], stage_dn[:, k], d_hi[:, k],
                                               ALU.subtract).then_inc(dn_ready, 1)
                split(0)
                beside.gpsimd_early(pool)
                if n == 2:
                    split(1)
                else:
                    with pool.Fori(1, n) as e:
                        split(e)
                beside.gpsimd_late(pool)

            @block.tensor
            def _(pe):
                def up_step(e, st):
                    tt, f = divmod(st, FC)
                    if tt == 0:
                        pe.wait_ge(up_ready, FC * e + f + 1)
                    pe.wait_ge(up_free, STEPS * e + st + 1)
                    tok = slice(tt * TW, (tt + 1) * TW)
                    fs = slice(f * P, (f + 1) * P)
                    for j in range(ups):
                        i = 0
                        for k in range(KC):
                            for w, x in ((w_hi, x_hi), (w_hi, x_lo), (w_lo, x_hi)):
                                ins = pe.matmul(up_ps[st % 2][j], w[:, j, k, fs], x[:, k, tok],
                                                start=(i == 0), stop=(i == 3 * KC - 1))
                                i += 1
                    ins.then_inc(up_done, 1)

                def down_step(e, st):
                    tt, f = divmod(st, FC)
                    if tt == 0:
                        pe.wait_ge(dn_ready, FC * e + f + 1)
                    pe.wait_ge(h_ready, STEPS * e + st + 3)
                    if f == 0:
                        pe.wait_ge(gated, KC * (TT * e + tt + 1))
                    for c in range(KC):
                        cs = slice(c * P, (c + 1) * P)
                        for i, (w, x) in enumerate(((d_hi, h_hi), (d_hi, h_lo), (d_lo, h_hi))):
                            ins = pe.matmul(y_ps[tt % 2][c], w[:, f, cs], x[:, st % HB],
                                            start=(f == 0 and i == 0), stop=(f == FC - 1 and i == 2))
                    ins.then_inc(dn_done, 1)

                for st in range(2):
                    up_step(0, st)
                def expert(e, first):
                    for st in range(STEPS):
                        if first and st == FC:
                            beside.tensor_early(pe)
                        up_step(e if st + 2 < STEPS else e + 1, (st + 2) % STEPS)
                        down_step(e, st)

                expert(0, True)
                if n > 2:
                    with pe.Fori(1, n - 1) as e:
                        expert(e, False)
                for st in range(STEPS):
                    if st + 2 < STEPS:
                        up_step(n - 1, st + 2)
                    down_step(n - 1, st)

            @block.scalar
            def _(act):
                def round_up(e, i):
                    if i == 0:
                        act.wait_ge(up_loaded, 16 * ups * (e + 1))
                    c = slice(i * P, (i + 1) * P)
                    for j in range(ups):
                        ins = act.activation(w_hi[:, j, :, c], stage_up[:, j, :, c], ACT.Copy)
                    ins.then_inc(up_rounded, 1)

                def round_down(e, k):
                    if k == 0:
                        act.wait_ge(dn_loaded, 16 * (e + 1))
                    act.activation(d_hi[:, k], stage_dn[:, k], ACT.Copy).then_inc(dn_rounded, 1)

                def round_hidden(e, st):
                    act.wait_ge(up_free, STEPS * e + st + 3)
                    act.activation(h_hi[:, st % HB], h[:, st % 2], ACT.Copy).then_inc(h_rounded, 1)

                def expert(e, first, last):
                    for st in range(STEPS):
                        act.wait_ge(up_done, STEPS * e + st + 1)
                        if swiglu:
                            act.activation(silu[:, st % 2], up_ps[st % 2][0], ACT.Silu).then_inc(act_done, 1)
                            if st > 0:
                                round_hidden(e, st - 1)
                            elif not first:
                                round_hidden(e - 1, STEPS - 1)
                        else:
                            act.activation(h_hi[:, st % HB], up_ps[st % 2][0], ACT.Relu).then_inc(h_rounded, 1)
                        if not first and st < 3:
                            round_down(e, FC - 3 + st)
                        if not last and st >= STEPS - FC:
                            round_up(e + 1, st - (STEPS - FC))
                        if not last and st >= STEPS - FC + 3:
                            round_down(e + 1, st - (STEPS - FC + 3))

                for i in range(FC):
                    round_up(0, i)
                for i in range(FC):
                    round_down(0, i)
                expert(0, True, False)
                if n > 2:
                    with act.Fori(1, n - 1) as e:
                        expert(e, False, False)
                beside.scalar_late(act)
                expert(n - 1, False, True)
                if swiglu:
                    round_hidden(n - 1, STEPS - 1)

            @block.vector
            def _(dve):
                if swiglu:
                    dve.nop().then_inc(up_free, 2)
                dve.nop().then_inc(h_ready, 2)
                dve.nop().then_inc(gated, 2 * KC)

                def split(e, st, offset=0):
                    g = STEPS * e + st
                    dve.wait_ge(h_rounded, g + 1)
                    if swiglu:
                        dve.tensor_tensor(h_lo[:, st % HB], h[:, st % 2], h_hi[:, st % HB],
                                          ALU.subtract).then_inc(h_ready, 1)
                    else:
                        dve.scalar_tensor_tensor(h_lo[:, st % HB], up_ps[st % 2][0], 0.0, h_hi[:, st % HB],
                                                 ALU.max, ALU.subtract).then_inc(h_ready, 1)

                def take(e, tt, target):
                    dve.wait_ge(dn_done, STEPS * e + FC * (tt + 1))
                    tok = slice(tt * TW, (tt + 1) * TW)
                    for c in range(KC):
                        if gate is None or target is not targets[0]:
                            dve.tensor_copy(target[:, c, tok], y_ps[tt % 2][c]).then_inc(gated, 1)
                            continue
                        v = "p (b t) -> p b t"
                        if not (isinstance(e, int) and e == 0 and tt == 0):
                            dve.wait_ge(summed, KC * (TT * e + tt - 1) + c + 1)
                        dve.tensor_tensor(part[:, c].rearrange(v, t=T), y_ps[tt % 2][c].rearrange(v, t=T),
                                          gate(e, tt), ALU.mult).then_inc(gated, 1)
                        dve.wait_ge(gated, KC * (TT * e + tt + 2) + c + 1)
                        dve.tensor_tensor(target[:, c, tok], target[:, c, tok], part[:, c], ALU.add).then_inc(summed, 1)

                def expert(e, first, target, before):
                    for st in range(STEPS):
                        tt, f = divmod(st, FC)
                        g = STEPS * e + st
                        if swiglu:
                            dve.wait_ge(h_ready, g + 1)
                            dve.wait_ge(act_done, g + 1)
                            dve.tensor_tensor(h[:, st % 2], silu[:, st % 2], up_ps[st % 2][1],
                                              ALU.mult).then_inc(up_free, 1)
                            if st > 0:
                                split(e, st - 1)
                            elif not first:
                                split(e - 1, STEPS - 1)
                        else:
                            split(e, st)
                        if first and st == FC + 1:
                            beside.vector_early(dve)
                        if f == 4:
                            if tt > 0:
                                take(e, tt - 1, target)
                            elif not first:
                                take(e - 1, TT - 1, before)

                done = 0
                before = None
                for (count, _, _), target in zip(groups, targets):
                    expert(done, done == 0, target, before)
                    if count == 2:
                        expert(done + 1, False, target, target)
                    elif count > 2:
                        with dve.Fori(done + 1, done + count) as e:
                            expert(e, False, target, target)
                    done += count
                    before = target
                if swiglu:
                    split(n - 1, STEPS - 1)
                take(n - 1, TT - 1, before)
    sem.give_back()


class AttentionWeights:

    def __init__(self, nc, ctx, raw, tag, w_qkv, w_out, b_qkv=None, b_out=None, w_sur=None):
        sb = lambda name, shape: ctx.enter_context(nc.sbuf_tensor(f"{tag}_{name}", shape, F32))
        rows, col = lambda w: w.rearrange("(k p) n -> p k n", p=P), lambda v: v.rearrange("(k p) -> p k", p=P)
        self.wo = sb("wo", [P, KC, D])
        self.loads = [(self.wo, rows(w_out))]
        if b_qkv is not None:
            self.bias, self.bo, self.ws = sb("bias", [P, 3 * D]), sb("bo", [P, KC]), sb("ws", [P, KC])
            self.loads += [(self.bias, b_qkv.unsqueeze(0).to_broadcast([P, 3 * D])), (self.bo, col(b_out)), (self.ws, col(w_sur))]
        part = lambda name: ctx.enter_context(nc.sbuf_tensor(f"{tag}_{name}", [P, KC, 3 * D], F32R))
        self.wq_hi, self.wq_lo = part("wq_hi"), part("wq_lo")
        self.wq = raw.enter_context(nc.sbuf_tensor(f"{tag}_wq", [P, KC, 3 * D], F32))
        self.loads.append((self.wq, rows(w_qkv)))
        self.loaded, self.rounded, self.ready = (ctx.enter_context(nc.semaphore(f"{tag}_weights_{name}"))
                                                 for name in ("loaded", "rounded", "ready"))

    def round(self, act):
        act.wait_ge(self.loaded, 16 * len(self.loads))
        act.activation(self.wq_hi[:], self.wq[:], ACT.Copy).then_inc(self.rounded, 1)

    def split(self, pool):
        pool.wait_ge(self.rounded, 1)
        pool.tensor_tensor(self.wq_lo[:], self.wq[:], self.wq_hi[:], ALU.subtract).then_inc(self.ready, 1)

    def load(self, sp):
        for dst, src in self.loads:
            sp.dma_start(dst[:], src, allow_slow_non_contiguous=True).then_inc(self.loaded, 16)


def attention(nc, m, tag, hyper, srcT, resT, w):
    QK, G, GH = 2 * D, 4, H // 4
    HP = H // 2
    VW = DH + 1
    SUB = TW // P
    head4 = m.const[:, C_HEAD4:C_HEAD4 + GH]
    half2 = m.const[:, C_HALF:C_HALF + 2]
    one = m.const[:, C_ONE:C_ONE + 2]
    twice = m.const[:, C_TWICE:C_TWICE + T]
    causal = m.const[:, C_CAUSAL:C_CAUSAL + T].unsqueeze(1).to_broadcast([P, H, T])
    with ExitStack() as s:
        sb = lambda name, shape, dt=F32: s.enter_context(nc.sbuf_tensor(f"{tag}_{name}", shape, dt))
        qk = sb("qk", [P, NP, QK])
        v_blk = sb("v_blk", [P, NP, 2, HP, 2, VW])
        wo = w.wo
        if hyper:
            bias, bo, ws = w.bias, w.bo, w.ws
            spike = sb("spike", [P, NP])
            q_space, q_time = sb("q_space", [P, NP, 2, H]), sb("q_time", [P, NP, 2, H])
            k_space, k_time = sb("k_space", [P, NP, 2, H]), sb("k_time", [P, NP, 2, H])

        sem = StageSemaphores(nc, tag + "_in")
        src_rounded, src_ready = sem("src_rounded"), sem("src_ready")
        qk_done, v_done, qk_taken, v_taken = sem("qk_done"), sem("v_done"), sem("qk_taken"), sem("v_taken")
        v_doubled, v_blocked, ones_set = [sem(f"v_doubled{i}") for i in range(2)], sem("v_blocked"), sem("ones_set")
        spiked, sp_small, sp_steps = sem("spiked"), sem("spike_exp"), sem("spike_steps")
        squared, summed, made, norm_act, norm = (sem(n) for n in ("squared", "summed", "made", "norm_act", "norm_steps"))
        copied, turned_sin = sem("copied"), sem("times_sin")
        with ExitStack() as s1:
            sb1 = lambda name, shape, dt=F32: s1.enter_context(nc.sbuf_tensor(f"{tag}_{name}", shape, dt))
            wq_hi, wq_lo = w.wq_hi, w.wq_lo
            src_hi, src_lo = sb1("src_hi", [P, 2, KC, TW], F32R), sb1("src_lo", [P, 2, KC, TW], F32R)
            v_row, v_two = sb1("v_row", [P, 2, SUB, D]), sb1("v_two", [P, 2, SUB, 2, D])
            if hyper:
                sig = sb1("sig", [P, NP])
                sq, part = sb1("sq", [P, 2, QK]), sb1("part", [P, 2, 2 * H])
                r2, ln, root, inv, ep, en, sm, ser, below, cosh = (
                    sb1(n, [P, NP, 2 * H]) for n in ("r2", "ln", "root", "inv", "ep", "en", "sm", "ser", "below", "cosh"))
            else:
                x32, rot = sb1("x32", [P, 2, QK]), sb1("rot", [P, 2, QK])
            SERIES = [2.0 / 362880, 2.0 / 5040, 2.0 / 120, 2.0 / 6, 2.0]
            qk_ps, v_ps = [m.bank[0], m.bank[1]], [m.bank[2][:, 0:D], m.bank[3][:, 0:D]]
            heads = lambda x: x.rearrange("p (h d) -> p h d", d=DH)

            def block_values(eng, tt):
                eng.wait_ge(v_doubled[tt % 2], 64 * (tt // 2 + (2 if tt == TT - 1 else 1)))
                vo = v_blk[:, tt * SUB:(tt + 1) * SUB].rearrange("p i j g h v -> p (i j g) h v")[:, :, :, 0:DH]
                vi = v_two[:, tt % 2].rearrange("p i j (g h d) -> p (i j g) h d", h=2, d=DH)
                eng.tensor_tensor(vo, vi, half2.unsqueeze(1).unsqueeze(3).to_broadcast([P, SUB * 2 * HP, 2, DH]),
                                  ALU.mult).then_inc(v_blocked, 1)

            with nc.Block() as block:
                @block.sync
                def _(sp):
                    for tt in range(TT):
                        q = tt % 2
                        if tt >= 2:
                            sp.wait_ge(v_blocked, tt - 1)
                        parts = 2 if tt == TT - 1 else 1
                        for part in range(parts):
                            i = slice(part * SUB // parts, (part + 1) * SUB // parts)
                            sp.wait_ge(v_taken, SUB * tt + i.stop)
                            for j in range(2):
                                for h in range(2):
                                    sp.dma_start(v_two[h * T:(h + 1) * T, q, i, j], v_row[j * T:(j + 1) * T, q, i])\
                                        .then_inc(v_doubled[q], 16)

                @block.tensor
                def _(pe):
                    pe.wait_ge(w.loaded, 16 * len(w.loads))
                    pe.wait_ge(w.ready, 1)
                    for i in range(NP):
                        q, t = i // SUB % 2, slice(i % SUB * P, (i % SUB + 1) * P)
                        if i % SUB == 0:
                            pe.wait_ge(src_ready, i // SUB + 1)
                        for ps, done, taken, cols in ((qk_ps, qk_done, qk_taken, slice(0, QK)),
                                                      (v_ps, v_done, v_taken, slice(QK, 3 * D))):
                            if i >= 2:
                                pe.wait_ge(taken, i - 1)
                            n = 0
                            for k in range(KC):
                                for x, wx in ((src_hi, wq_hi), (src_hi, wq_lo), (src_lo, wq_hi)):
                                    ins = pe.matmul(ps[i % 2], x[:, q, k, t], wx[:, k, cols], start=(n == 0), stop=(n == 3 * KC - 1))
                                    n += 1
                            ins.then_inc(done, 1)
                    if hyper:
                        for i in range(NP):
                            for k in range(KC):
                                ins = pe.matmul(m.bank[7][:, i:i + 1], srcT[:, k, i * P:(i + 1) * P], ws[:, k:k + 1],
                                                start=(k == 0), stop=(k == KC - 1))
                        ins.then_inc(spiked, 1)

                @block.scalar
                def _(act):
                    if hyper:
                        act.preload_act_table_set("natural_log_exp_and_others")

                    def round_src(tt):
                        if tt >= 2:
                            act.wait_ge(v_done, SUB * (tt - 1))
                        act.activation(src_hi[:, tt % 2], srcT[:, :, tt * TW:(tt + 1) * TW], ACT.Copy).then_inc(src_rounded, 1)

                    round_src(0)
                    round_src(1)
                    for i in range(NP):
                        if hyper:
                            act.wait_ge(qk_taken, i + 1)
                            if i >= 2:
                                act.wait_ge(made, i - 1)
                            act.activation(sq[:, i % 2], qk[:, i], ACT.Square).then_inc(squared, 1)
                        else:
                            act.wait_ge(qk_done, i + 1)
                            if i >= 2:
                                act.wait_ge(turned_sin, i - 1)
                            act.activation(x32[:, i % 2], qk_ps[i % 2], ACT.Copy).then_inc(copied, 1)
                        if i % SUB == SUB - 1 and i // SUB + 2 < TT:
                            round_src(i // SUB + 2)
                    if hyper:
                        act.wait_ge(norm, 1)
                        act.activation(ln[:], r2[:], ACT.Ln).then_inc(norm_act, 1)
                        act.wait_ge(norm_act, 1)
                        act.activation(root[:], ln[:], ACT.Exp, scale=0.5).then_inc(norm_act, 1)
                        act.activation(inv[:], ln[:], ACT.Exp, scale=-0.5).then_inc(norm_act, 1)
                        act.wait_ge(norm_act, 2)
                        act.activation(ep[:], root[:], ACT.Exp).then_inc(norm_act, 1)
                        act.activation(en[:], root[:], ACT.Exp, scale=-1.0).then_inc(norm_act, 1)
                        act.wait_ge(spiked, 1)
                        act.activation(sig[:], m.bank[7][:, 0:NP], ACT.Exp, bias=m.neg_b_sur[:], scale=-1.0).then_inc(sp_small, 1)

                @block.vector
                def _(dve):
                    def split_src(tt):
                        dve.wait_ge(src_rounded, tt + 1)
                        if tt >= 2:
                            dve.wait_ge(v_done, SUB * (tt - 1))
                        dve.tensor_tensor(src_lo[:, tt % 2], srcT[:, :, tt * TW:(tt + 1) * TW], src_hi[:, tt % 2],
                                          ALU.subtract).then_inc(src_ready, 1)

                    split_src(0)
                    split_src(1)

                    def spikes():
                        dve.wait_ge(sp_small, 1)
                        dve.tensor_scalar(sig[:], sig[:], 1.0, None, ALU.add).then_inc(sp_steps, 1)
                        dve.wait_ge(sp_steps, 1)
                        dve.reciprocal(sig[:], sig[:]).then_inc(sp_steps, 1)
                        dve.wait_ge(sp_steps, 2)
                        dve.tensor_scalar(spike[:], sig[:], m.threshold[:], None, ALU.is_gt)

                    def space_norm(i):
                        dve.wait_ge(squared, i + 1)
                        x = heads(sq[:, i % 2])
                        dve.tensor_reduce(part[:, i % 2], x[:, :, 1:], AX_X, ALU.add).then_inc(summed, 1)
                        dve.wait_ge(summed, i + 1)
                        dve.tensor_tensor(r2[:, i], part[:, i % 2], x[:, :, 0], ALU.subtract).then_inc(made, 1)

                    def rotate(i):
                        dve.wait_ge(qk_taken, i + 1)
                        dve.wait_ge(turned_sin, i + 1)
                        dve.tensor_tensor(qk[:, i], qk[:, i], rot[:, i % 2], ALU.add).then_inc(made, 1)

                    later = space_norm if hyper else rotate
                    for i in range(NP):
                        dve.wait_ge(qk_done, i + 1)
                        if hyper:
                            dve.tensor_tensor(qk[:, i], qk_ps[i % 2], bias[:, 0:QK], ALU.add).then_inc(qk_taken, 1)
                        else:
                            dve.wait_ge(copied, i + 1)
                            dve.tensor_tensor(heads(qk[:, i]), heads(qk_ps[i % 2]),
                                              m.const[:, C_COS:C_COS + DH].unsqueeze(1).to_broadcast([P, 2 * H, DH]),
                                              ALU.mult).then_inc(qk_taken, 1)
                        dve.wait_ge(v_done, i + 1)
                        tt = i // SUB
                        if i % SUB == 0 and tt >= 2:
                            dve.wait_ge(v_doubled[tt % 2], 64 * (tt // 2))
                        if hyper:
                            dve.tensor_tensor(v_row[:, tt % 2, i % SUB], v_ps[i % 2], bias[:, QK:], ALU.add).then_inc(v_taken, 1)
                        else:
                            dve.tensor_copy(v_row[:, tt % 2, i % SUB], v_ps[i % 2]).then_inc(v_taken, 1)
                        if i >= 1:
                            later(i - 1)
                        if i % SUB == SUB - 1 and tt + 2 < TT:
                            split_src(tt + 2)
                    later(NP - 1)
                    if not hyper:
                        block_values(dve, TT - 1)
                    if hyper:
                        done = [0]

                        def link(ins):
                            done[0] += 1
                            ins.then_inc(norm, 1)
                            dve.wait_ge(norm, done[0])

                        dve.wait_ge(made, NP)
                        link(dve.tensor_scalar(r2[:], r2[:], 1e-8, None, ALU.max))
                        link(dve.tensor_scalar(sm[:], r2[:], 1.0, None, ALU.min))
                        link(dve.tensor_scalar(ser[:], sm[:], SERIES[0], SERIES[1], ALU.mult, ALU.add))
                        for coef in SERIES[2:]:
                            link(dve.tensor_tensor(ser[:], ser[:], sm[:], ALU.mult))
                            link(dve.tensor_scalar(ser[:], ser[:], coef, None, ALU.add))
                        link(dve.tensor_scalar(below[:], r2[:], 1.0, None, ALU.is_lt))
                        dve.wait_ge(norm_act, 5)
                        link(dve.tensor_tensor(sm[:], ep[:], en[:], ALU.subtract))
                        link(dve.tensor_tensor(sm[:], sm[:], inv[:], ALU.mult))
                        link(dve.tensor_tensor(ser[:], ser[:], sm[:], ALU.subtract))
                        link(dve.tensor_tensor(ser[:], ser[:], below[:], ALU.mult))
                        link(dve.tensor_tensor(ser[:], ser[:], sm[:], ALU.add))
                        link(dve.tensor_tensor(cosh[:], ep[:], en[:], ALU.add))
                        for j in range(2):
                            hj = half2[:, j:j + 1]
                            dve.tensor_scalar(q_space[:, :, j], ser[:, :, 0:H], hj, -0.5, ALU.mult, ALU.mult)
                            dve.tensor_scalar(q_time[:, :, j], cosh[:, :, 0:H], hj, 0.5, ALU.mult, ALU.mult)
                            dve.tensor_scalar(k_space[:, :, j], ser[:, :, H:], hj, 0.5, ALU.mult, ALU.mult)
                            dve.tensor_scalar(k_time[:, :, j], cosh[:, :, H:], hj, 0.5, ALU.mult, ALU.mult)
                        spikes()

                @block.gpsimd
                def _(pool):
                    for i in range(NP):
                        for j in range(2):
                            ins = pool.tensor_copy(v_blk[:, i, j, :, :, DH], half2.unsqueeze(1).to_broadcast([P, HP, 2]))
                    ins.then_inc(ones_set, 1)

                    def times_sin(i):
                        pool.wait_ge(copied, i + 1)
                        if i >= 2:
                            pool.wait_ge(made, i - 1)
                        e = DH // 2
                        sin = m.const[:, C_SIN:C_SIN + DH].unsqueeze(1)
                        x, r = heads(x32[:, i % 2]), heads(rot[:, i % 2])
                        pool.tensor_tensor(r[:, :, 0:e], x[:, :, e:], sin[:, :, 0:e].to_broadcast([P, 2 * H, e]), ALU.mult)
                        pool.tensor_tensor(r[:, :, e:], x[:, :, 0:e], sin[:, :, e:].to_broadcast([P, 2 * H, e]),
                                           ALU.mult).then_inc(turned_sin, 1)

                    for i in range(NP):
                        if not hyper:
                            times_sin(i)
                        if i % SUB == 1 and i >= SUB:
                            block_values(pool, i // SUB - 1)
                    if hyper:
                        block_values(pool, TT - 1)
        sem.give_back()

        if hyper:
            lag = dict(turn=0, q_blk=0, k_blk=0, score=0, clamp=1, root_sq=1, root_ln=2, root=2, root_add=2, dist_ln=2,
                       dist=3, mask=3, top=3, shift=3, prob=4, p_turn=4, p_take=4, mix=5, y=5, y_turn=5, y_take=6,
                       out=6, add=6, place_both=0, fetch=3)
            order = dict(tensor="mix out turn p_turn y_turn score",
                         scalar="y_take dist root_ln prob root q_blk root_sq p_take dist_ln",
                         vector="place_both clamp y add k_blk top", gpsimd="mask root_add shift", sync="fetch")
        else:
            lag = dict(place=0, turn=0, q_blk=0, k_blk=0, score=0, clamp=1, top=1, shift=1, prob=1, p_turn=2, p_take=2,
                       mix=2, y=2, y_turn=3, y_take=3, out=3, add=3, fetch=0)
            order = dict(tensor="y_turn p_turn out turn mix score", scalar="y_take p_take q_blk prob",
                         vector="clamp top add k_blk y", gpsimd="place shift", sync="fetch")
        last = max(lag.values())
        sem = StageSemaphores(nc, tag)
        placed, turned, k_turned, q_taken, k_blocked = (
            sem(n) for n in ("placed", "turned", "k_turned", "q_taken", "k_blocked"))
        scored, clamped, root_squared, root_logged, rooted = (
            sem(n) for n in ("scored", "clamped", "root_squared", "root_logged", "rooted"))
        root_added, dist_logged, dist_done, masked = sem("root_added"), sem("dist_logged"), sem("dist_done"), sem("masked")
        max_done, shifted, prob_done = sem("max_done"), sem("shifted"), sem("prob_done")
        p_turned, p_taken, mixed, rec_steps = sem("p_turned"), sem("p_taken"), sem("mixed"), sem("rec_steps")
        v_fetched = [sem(f"v_fetched{q}") for q in range(2)]
        y_scaled, y_turned, y_taken, out_done, added = (sem(n) for n in ("y_scaled", "y_turned", "y_taken", "out_done", "added"))
        with ExitStack() as s2:
            sb2 = lambda name, shape: s2.enter_context(nc.sbuf_tensor(f"{tag}_{name}", shape, F32))
            q_exp, k_exp = sb2("q_exp", [P, 2, G, 2, T]), sb2("k_exp", [P, 2, G, 2, T])
            q_blk, k_blk = sb2("q_blk", [P, 2, G, P]), sb2("k_blk", [P, 2, G, GH, T])
            u, prob = sb2("u", [P, 2, H, T]), sb2("prob", [P, 2, H, T])
            pT = sb2("pT", [P, 2, HP, P])
            fence = sb2("fence", [P, 2])
            v_now = sb2("v_now", [P, 2, 2, HP, 2, VW])
            mx, rec = sb2("mx", [P, 2, H]), sb2("rec", [P, 2, H])
            y, yT = sb2("y", [P, 2, D]), sb2("yT", [P, 2, KC, P])
            if hyper:
                z, t = sb2("z", [P, 2, H, T]), sb2("t", [P, 2, H, T])
            qT_ps, kT_ps = m.bank[0], m.bank[1][:, 0:G * T]
            s_ps = m.ps[:, 2:4, :].rearrange("p a (h t) -> p (a h) t", t=T)
            pT_ps = m.ps[:, 4:6, :].rearrange("p a n -> p (a n)")
            y_ps = m.bank[6][:, 0:H * VW]
            y_ps_h = y_ps.rearrange("p (h v) -> p h v", v=VW)
            yT_ps, o_ps = m.bank[7][:, 0:D], m.bank[7][:, D:2 * D]

            def wait(eng, s, count):
                if not isinstance(count, int) or count > 0:
                    eng.wait_ge(s, count)

            def run(eng, name, phases):
                mine = order[name].split()

                def step(it, half, par):
                    for ph in mine:
                        if not isinstance(it, int) or 0 <= it - lag[ph] < NP:
                            phases[ph](it - lag[ph], (par + lag[ph]) % 2, half + (par - lag[ph]) // 2)

                first = (last + 3) // 2 * 2
                for it in range(first):
                    step(it, it // 2, it % 2)
                with eng.Fori(first // 2, NP // 2) as half:
                    for par in range(2):
                        step(half * 2 + par, half, par)
                for it in range(NP, NP + last):
                    step(it, it // 2, it % 2)

            with nc.Block() as block:
                @block.sync
                def _(sp):
                    def fetch(i, q, nth):
                        wait(sp, mixed, i - 1)
                        sp.dma_start(v_now[:, q], v_blk[:, bass.ds(i, 1)].rearrange("p o j g h v -> p (o j) g h v"))\
                            .then_inc(v_fetched[q], 16)

                    run(sp, "sync", dict(fetch=fetch))

                @block.tensor
                def _(pe):
                    def turn(i, q, nth):
                        pe.wait_ge(placed, i + 1)
                        wait(pe, q_taken, i)
                        wait(pe, k_blocked, i)
                        both = lambda x, g: x[:, q, g].rearrange("p j t -> p (j t)")
                        for g in range(G):
                            ins = pe.matmul(kT_ps[:, g * T:(g + 1) * T], both(k_exp, g), twice, start=True, stop=True)
                        ins.then_inc(k_turned, 1)
                        for g in range(G):
                            ins = pe.transpose(qT_ps[:, g * P:(g + 1) * P], both(q_exp, g), m.ident)
                        ins.then_inc(turned, 1)

                    def score(i, q, nth):
                        pe.wait_ge(q_taken, i + 1)
                        pe.wait_ge(k_blocked, i + 1)
                        wait(pe, clamped if hyper else masked, i)
                        for g in range(G):
                            ins = pe.matmul(s_ps[:, g * GH:(g + 1) * GH, :], q_blk[:, q, g], k_blk[:, q, g],
                                            start=True, stop=True)
                        ins.then_inc(scored, 1)

                    def p_turn(i, q, nth):
                        pe.wait_ge(prob_done, i + 1)
                        wait(pe, p_taken, i)
                        for hp in range(HP):
                            ins = pe.transpose(pT_ps[:, hp * P:(hp + 1) * P],
                                               prob[:, q, 2 * hp:2 * hp + 2].rearrange("p h t -> p (h t)"), m.ident)
                        ins.then_inc(p_turned, 1)

                    def mix(i, q, nth):
                        pe.wait_ge(p_taken, i + 1)
                        pe.wait_ge(v_fetched[q], 16 * (nth + 1))
                        wait(pe, y_scaled, i)
                        for hp in range(HP):
                            for j in range(2):
                                ins = pe.matmul(y_ps[j * T:(j + 1) * T, hp * 2 * VW:(hp + 1) * 2 * VW],
                                                pT[:, q, hp, j * T:(j + 1) * T],
                                                v_now[:, q, j, hp].rearrange("p h v -> p (h v)"), start=True, stop=True)
                        ins.then_inc(mixed, 1)

                    def y_turn(i, q, nth):
                        pe.wait_ge(y_scaled, i + 1)
                        wait(pe, y_taken, i)
                        wait(pe, added, i)
                        for c in range(KC):
                            ins = pe.transpose(yT_ps[:, c * P:(c + 1) * P], y[:, q, c * P:(c + 1) * P], m.ident)
                        ins.then_inc(y_turned, 1)

                    def out(i, q, nth):
                        pe.wait_ge(y_taken, i + 1)
                        wait(pe, added, i)
                        for c in range(KC):
                            for k in range(KC):
                                ins = pe.matmul(o_ps[:, c * P:(c + 1) * P], wo[:, k, c * P:(c + 1) * P], yT[:, q, k],
                                                start=(k == 0), stop=(k == KC - 1))
                        ins.then_inc(out_done, 1)

                    run(pe, "tensor", dict(turn=turn, score=score, p_turn=p_turn, mix=mix, y_turn=y_turn, out=out))

                @block.scalar
                def _(act):
                    def take_q(i, q, nth):
                        act.wait_ge(turned, i + 1)
                        wait(act, scored, i - 1)
                        act.activation(q_blk[:, q].rearrange("p g n -> p (g n)"), qT_ps, ACT.Copy).then_inc(q_taken, 1)

                    def root_square(i, q, nth):
                        act.wait_ge(clamped, i + 1)
                        wait(act, masked, i - 1)
                        act.activation(t[:, q], z[:, q], ACT.Square).then_inc(root_squared, 1)

                    def root_log(i, q, nth):
                        act.wait_ge(root_squared, i + 1)
                        act.activation(t[:, q], t[:, q], ACT.Ln, bias=m.minus_one[:]).then_inc(root_logged, 1)

                    def root(i, q, nth):
                        act.wait_ge(root_logged, i + 1)
                        act.activation(t[:, q], t[:, q], ACT.Exp, scale=0.5).then_inc(rooted, 1)

                    def dist_log(i, q, nth):
                        act.wait_ge(root_added, i + 1)
                        act.activation(t[:, q], z[:, q], ACT.Ln).then_inc(dist_logged, 1)

                    def dist(i, q, nth):
                        act.wait_ge(dist_logged, i + 1)
                        act.activation(t[:, q], t[:, q], ACT.Square, scale=0.5).then_inc(dist_done, 1)

                    def exponential(i, q, nth):
                        act.wait_ge(shifted, i + 1)
                        wait(act, p_turned, i - 1)
                        act.activation(prob[:, q], u[:, q], ACT.Exp).then_inc(prob_done, 1)

                    def p_take(i, q, nth):
                        act.wait_ge(p_turned, i + 1)
                        wait(act, mixed, i - 1)
                        act.activation(pT[:, q].rearrange("p h n -> p (h n)"), pT_ps, ACT.Copy).then_inc(p_taken, 1)

                    def y_take(i, q, nth):
                        act.wait_ge(y_turned, i + 1)
                        wait(act, out_done, i - 1)
                        act.activation(yT[:, q].rearrange("p c n -> p (c n)"), yT_ps, ACT.Copy).then_inc(y_taken, 1)

                    run(act, "scalar", dict(q_blk=take_q, root_sq=root_square, root_ln=root_log, root=root, dist_ln=dist_log, dist=dist, prob=exponential, p_take=p_take, y_take=y_take))

                @block.vector
                def _(dve):
                    def place_both(i, q, nth):
                        wait(dve, turned, i - 1)
                        at = bass.ds(i, 1)
                        by_head = lambda f: f.rearrange("p o (g h) -> p (o g) h", h=GH)
                        x = qk[:, at].rearrange("p o (g h d) -> p (o g) h d", h=GH, d=DH)
                        for dst, part, space, time in ((q_exp, x[:, 0:G], q_space, q_time), (k_exp, x[:, G:], k_space, k_time)):
                            for j in range(2):
                                to = dst[:, q, :, j].rearrange("p g (h d) -> p g h d", d=DH)
                                dve.tensor_tensor(to[:, :, :, 1:], part[:, :, :, 1:],
                                                  by_head(space[:, at, j]).unsqueeze(3).to_broadcast([P, G, GH, DH - 1]), ALU.mult)
                                ins = dve.tensor_copy(to[:, :, :, 0], by_head(time[:, at, j]))
                        ins.then_inc(placed, 1)

                    def block_k(i, q, nth):
                        dve.wait_ge(k_turned, i + 1)
                        wait(dve, scored, i - 1)
                        shape = [P, G, GH, T]
                        dve.tensor_tensor(k_blk[:, q], kT_ps.rearrange("p (g t) -> p g t", g=G).unsqueeze(2).to_broadcast(shape),
                                          head4.unsqueeze(1).unsqueeze(3).to_broadcast(shape), ALU.mult).then_inc(k_blocked, 1)

                    def clamp(i, q, nth):
                        dve.wait_ge(scored, i + 1)
                        if hyper:
                            wait(dve, dist_logged, i - 1)
                            dve.tensor_scalar(z[:, q], s_ps, float(np.float32(1.0 + 1e-7)), None, ALU.max).then_inc(clamped, 1)
                        else:
                            wait(dve, prob_done, i - 1)
                            dve.scalar_tensor_tensor(u[:, q], s_ps, DH ** -0.5, causal, ALU.mult, ALU.add).then_inc(masked, 1)

                    def top(i, q, nth):
                        dve.wait_ge(masked, i + 1)
                        wait(dve, shifted, i - 1)
                        dve.tensor_reduce(mx[:, q], u[:, q], AX_X, ALU.max).then_inc(max_done, 1)

                    per = 2 if hyper else 1

                    def scale_y(i, q, nth):
                        dve.wait_ge(mixed, i + 1)
                        wait(dve, y_scaled, i - 1)
                        dve.reciprocal(rec[:, q], y_ps_h[:, :, DH]).then_inc(rec_steps, 1)
                        dve.wait_ge(rec_steps, per * i + 1)
                        if hyper:
                            dve.tensor_scalar(rec[:, q], rec[:, q], spike[:, bass.ds(i, 1)], None, ALU.mult).then_inc(rec_steps, 1)
                            dve.wait_ge(rec_steps, per * i + 2)
                        wait(dve, y_turned, i - 1)
                        dve.tensor_tensor(y[:, q].rearrange("p (h d) -> p h d", d=DH), y_ps_h[:, :, 0:DH],
                                          rec[:, q].unsqueeze(2).to_broadcast([P, H, DH]), ALU.mult).then_inc(y_scaled, 1)

                    def add(i, q, nth):
                        dve.wait_ge(out_done, i + 1)
                        for c in range(KC):
                            x = resT[:, c, bass.ds(i * P, P)]
                            op = o_ps[:, c * P:(c + 1) * P]
                            if hyper:
                                ins = dve.scalar_tensor_tensor(x, op, bo[:, c:c + 1], x, ALU.add, ALU.add)
                            else:
                                ins = dve.tensor_tensor(x, op, x, ALU.add)
                        ins.then_inc(added, 1)

                    run(dve, "vector", dict(place_both=place_both, k_blk=block_k, clamp=clamp, top=top, y=scale_y, add=add))

                @block.gpsimd
                def _(pool):
                    def root_add(i, q, nth):
                        pool.wait_ge(rooted, i + 1)
                        pool.tensor_tensor(z[:, q], z[:, q], t[:, q], ALU.add).then_inc(root_added, 1)

                    def mask(i, q, nth):
                        pool.wait_ge(dist_done, i + 1)
                        wait(pool, prob_done, i - 1)
                        pool.tensor_tensor(u[:, q], causal, t[:, q], ALU.subtract).then_inc(masked, 1)

                    def shift(i, q, nth):
                        pool.wait_ge(max_done, i + 1)
                        pool.tensor_tensor(u[:, q], u[:, q], mx[:, q].unsqueeze(2).to_broadcast([P, H, T]),
                                           ALU.subtract).then_inc(shifted, 1)

                    def place(i, q, nth):
                        wait(pool, turned, i - 1)
                        pool.tensor_tensor(fence[:, q:q + 1], one[:, 0:1], one[:, 0:1], ALU.mult)
                        at = bass.ds(i, 1)
                        x = qk[:, at].rearrange("p o (g n) -> p (o g) n", n=T).unsqueeze(2)
                        shape = [P, G, 2, T]
                        for dst, part in ((q_exp, x[:, 0:G]), (k_exp, x[:, G:])):
                            ins = pool.tensor_tensor(dst[:, q], part.to_broadcast(shape),
                                                     half2.unsqueeze(1).unsqueeze(3).to_broadcast(shape), ALU.mult)
                        ins.then_inc(placed, 1)

                    run(pool, "gpsimd", dict(root_add=root_add, mask=mask, shift=shift, place=place))
        sem.give_back()


class GateWeights:

    def __init__(self, nc, ctx, g1, g2):
        self.g1 = ctx.enter_context(nc.sbuf_tensor("mix_g1", [P, 3 * KC, D], F32))
        self.g2 = ctx.enter_context(nc.sbuf_tensor("mix_g2", [P, KC, 3], F32))
        self.loads = [(self.g1, g1), (self.g2, g2)]
        self.loaded = ctx.enter_context(nc.semaphore("mix_loaded"))

    def load(self, sp):
        for dst, src in self.loads:
            sp.dma_start(dst[:], src.rearrange("(k p) n -> p k n", p=P)).then_inc(self.loaded, 16)


def mix_gate(nc, m, gate, eo, s0, s1, w):
    sem = StageSemaphores(nc, "mix")
    hid, hid_taken, logit, chain, e_done = (sem(n) for n in ("hidden", "hidden_taken", "logit", "chain", "exp"))
    spread = sem("spread")
    with ExitStack() as s:
        sb = lambda name, shape: s.enter_context(nc.sbuf_tensor(f"mix_{name}", shape, F32))
        G1, G2 = gate.g1, gate.g2
        r1 = sb("r1", [P, KC, B])
        lg, top, tot = sb("lg", [B, 3]), sb("top", [B, 1]), sb("tot", [B, 1])
        dg = sb("dg", [B, 3, B])
        firsts = [x[:, c].rearrange("p (b t) -> p b t", t=T)[:, :, 0] for x in (eo, s0, s1) for c in range(KC)]
        with nc.Block() as block:
            @block.tensor
            def _(pe):
                pe.wait_ge(gate.loaded, 16 * len(gate.loads))
                for c in range(KC):
                    for k in range(3 * KC):
                        ins = pe.matmul(m.bank[c][:, 0:B], G1[:, k, c * P:(c + 1) * P], firsts[k],
                                        start=(k == 0), stop=(k == 3 * KC - 1))
                ins.then_inc(hid, 1)
                pe.wait_ge(hid_taken, KC)
                for c in range(KC):
                    ins = pe.matmul(m.bank[2][0:B, 0:3], r1[:, c], G2[:, c], start=(c == 0), stop=(c == KC - 1))
                ins.then_inc(logit, 1)
                pe.wait_ge(chain, 6)
                pe.matmul(m.bank[3][:, 0:3 * B], m.const[0:B, C_MEAN:C_MEAN + P], dg[:].rearrange("p j b -> p (j b)"),
                          start=True, stop=True).then_inc(spread, 1)

            @block.scalar
            def _(act):
                act.wait_ge(hid, 1)
                for c in range(KC):
                    act.activation(r1[:, c], m.bank[c][:, 0:B], ACT.Relu).then_inc(hid_taken, 1)
                act.wait_ge(chain, 2)
                act.activation(lg[:], lg[:], ACT.Exp).then_inc(e_done, 1)

            @block.vector
            def _(dve):
                def link(n, ins):
                    ins.then_inc(chain, 1)
                    dve.wait_ge(chain, n)
                dve.wait_ge(logit, 1)
                link(1, dve.tensor_reduce(top[:], m.bank[2][0:B, 0:3], AX_X, ALU.max))
                link(2, dve.tensor_scalar(lg[:], m.bank[2][0:B, 0:3], top[:], None, ALU.subtract))
                dve.wait_ge(e_done, 1)
                link(3, dve.tensor_reduce(tot[:], lg[:], AX_X, ALU.add))
                link(4, dve.reciprocal(tot[:], tot[:]))
                link(5, dve.tensor_scalar(lg[:], lg[:], tot[:], None, ALU.mult))
                link(6, dve.tensor_tensor(dg[:], lg[:].unsqueeze(2).to_broadcast([B, 3, B]),
                                          m.ident[0:B, 0:B].unsqueeze(1).to_broadcast([B, 3, B]), ALU.mult))
                dve.wait_ge(spread, 1)
                dve.tensor_scalar(w[:].rearrange("p j b -> p (j b)"), m.bank[3][:, 0:3 * B], float(D), None, ALU.mult)
    sem.give_back()


def layer_norm(nc, m, tag, srcT, ln_w, ln_b, conv_w=None, convT=None, mix=None, router=None, sync_late=None, scalar_early=None, gpsimd_late=None):
    sem = StageSemaphores(nc, tag)
    loaded, set_up = sem("loaded"), sem("set_up")
    summed, centred, squared, var_done = sem("summed"), sem("centred"), sem("squared"), sem("var_done")
    log_done, rstd_done, normed, h_done = sem("log_done"), sem("rstd_done"), sem("normed"), sem("h_done")
    scaled, mix_steps, mixed = sem("scaled"), sem("mix_steps"), sem("mixed")
    conv_s, conv_done = [sem(f"conv_steps{c}") for c in range(KC)], [sem(f"conv_done{c}") for c in range(KC)]
    logits, pick, turned, taken = sem("logits"), sem("pick"), sem("turned"), sem("taken")
    PAD = 2
    if mix is not None:
        s0, s1, w = mix
    with ExitStack() as s:
        sb = lambda name, shape: s.enter_context(nc.sbuf_tensor(f"{tag}_{name}", shape, F32))
        wcol, bcol, eps = sb("w", [P, KC]), sb("b", [P, KC]), sb("eps", [P, 1])
        xc, sq, xn = sb("xc", [P, 2, KC, TW]), sb("sq", [P, 2, KC, TW]), sb("xn", [P, 2, KC, TW])
        rstd = sb("rstd", [P, 2, TW])
        n_load = 2
        if conv_w is not None:
            taps = sb("taps", [P, KC, 3])
            h = sb("h", [P, 2, KC, BT, PAD + T])
            h_out = lambda q, c: h[:, q, c, :, PAD:]
            n_load = 3
        else:
            w_r, rows, sel, total = router
            wr = sb("wr", [P, KC, E_MOE])
            h = sb("h", [P, 2, KC, TW])
            h_out = lambda q, c: h[:, q, c].rearrange("p (b t) -> p b t", t=T)
            SUB = TW // P
            logit_ps = [m.bank[4], m.bank[7]]
            lg, best = sb("lg", [P, 2, SUB, E_MOE]), sb("best", [P, 2, SUB])
            free = sb("free", [P, 2, SUB])
            n_load = 3
        mean = m.const[:, C_MEAN:C_MEAN + P]
        with nc.Block() as block:
            @block.sync
            def _(sp):
                col = lambda v: v.rearrange("(k p) -> p k", p=P)
                sp.dma_start(wcol[:], col(ln_w), allow_slow_non_contiguous=True).then_inc(loaded, 16)
                sp.dma_start(bcol[:], col(ln_b), allow_slow_non_contiguous=True).then_inc(loaded, 16)
                if conv_w is not None:
                    sp.dma_start(taps[:], conv_w.rearrange("(k p) o j -> p k (o j)", p=P)).then_inc(loaded, 16)
                else:
                    sp.dma_start(wr[:], w_r.rearrange("(k p) e -> p k e", p=P)).then_inc(loaded, 16)
                if sync_late is not None:
                    sync_late(sp)

            by_batch = lambda x: x.rearrange("p (b t) -> p b t", t=T)
            tile = lambda t: slice(t * TW, (t + 1) * TW)

            def weight(j, t):
                return w[:, j, t * BT:(t + 1) * BT].unsqueeze(2).to_broadcast([P, BT, T])

            def steps(*phases):
                for step in range(TT + max(lag for lag, _ in phases)):
                    for lag, phase in phases:
                        if 0 <= step - lag < TT:
                            phase(step - lag)

            def convolve(eng, t, c):
                eng.wait_ge(h_done, KC * t + c + 1)
                if t == 0:
                    eng.wait_ge(loaded, 16 * n_load)
                o = by_batch(convT[:, c, tile(t)])
                eng.tensor_scalar(o, h[:, t % 2, c, :, 2:2 + T], taps[:, c, 2:3], None, ALU.mult).then_inc(conv_s[c], 1)
                for j in (1, 0):
                    eng.wait_ge(conv_s[c], 2 * t + 2 - j)
                    ins = eng.scalar_tensor_tensor(o, h[:, t % 2, c, :, j:j + T], taps[:, c, j:j + 1], o, ALU.mult, ALU.add)
                    ins.then_inc(conv_s[c] if j == 1 else conv_done[c], 1)

            @block.gpsimd
            def _(pool):
                pool.memset(eps[:], LN_EPS).then_inc(set_up, 1)
                if conv_w is not None:
                    for q in range(2):
                        pool.memset(h[:, q, :, :, 0:PAD], 0.0).then_inc(set_up, 1)

                def scale(t):
                    for c in range(KC):
                        for j, x in ((1, s0), (2, s1)):
                            y = by_batch(x[:, c, tile(t)])
                            ins = pool.tensor_tensor(y, y, weight(j, t), ALU.mult)
                        ins.then_inc(scaled, 1)

                if mix is not None:
                    for t in range(TT):
                        scale(t)
                if gpsimd_late is not None:
                    gpsimd_late(pool)
                if router is not None:
                    pool.tensor_copy(rows[:, :, 2 * D], m.const[:, C_TOKEN:C_TOKEN + NP])

            @block.tensor
            def _(pe):
                def means(t):
                    if mix is not None:
                        pe.wait_ge(mixed, t + 1)
                    if t >= 2:
                        pe.wait_ge(centred, t - 1)
                    for c in range(KC):
                        ins = pe.matmul(m.bank[t % 2], mean, srcT[:, c, tile(t)], start=(c == 0), stop=(c == KC - 1))
                    ins.then_inc(summed, 1)

                def variances(t):
                    pe.wait_ge(squared, t + 1)
                    if t >= 2:
                        pe.wait_ge(log_done, t - 1)
                    for c in range(KC):
                        ins = pe.matmul(m.bank[2 + t % 2], mean, sq[:, t % 2, c], start=(c == 0), stop=(c == KC - 1))
                    ins.then_inc(var_done, 1)

                def route(t):
                    if t == 0:
                        pe.wait_ge(loaded, 16 * n_load)
                    pe.wait_ge(h_done, KC * (t + 1))
                    if t >= 2:
                        pe.wait_ge(pick, 9 * (t - 1))
                    for i in range(SUB):
                        for c in range(KC):
                            ins = pe.matmul(logit_ps[t % 2][:, i * E_MOE:(i + 1) * E_MOE], h[:, t % 2, c, i * P:(i + 1) * P],
                                            wr[:, c], start=(c == 0), stop=(c == KC - 1))
                    ins.then_inc(logits, 1)
                    if t >= 1:
                        pe.wait_ge(taken, t)
                    for i in range(SUB):
                        for c in range(KC):
                            ins = pe.transpose(m.bank[5 + i // 2][:, (i % 2 * KC + c) * P:(i % 2 * KC + c + 1) * P],
                                               h[:, t % 2, c, i * P:(i + 1) * P], m.ident)
                    ins.then_inc(turned, 1)

                if conv_w is not None:
                    steps((0, means), (1, variances))
                else:
                    steps((0, means), (1, variances), (2, route))

            @block.scalar
            def _(act):
                if conv_w is not None:
                    act.preload_act_table_set("natural_log_exp_and_others")
                if scalar_early is not None:
                    scalar_early(act)
                act.wait_ge(set_up, 3 if conv_w is not None else 1)
                act.wait_ge(loaded, 16 * n_load)

                def square(t):
                    act.wait_ge(centred, t + 1)
                    if t >= 2:
                        act.wait_ge(var_done, t - 1)
                    act.activation(sq[:, t % 2], xc[:, t % 2], ACT.Square).then_inc(squared, 1)

                def inverse(t):
                    q = t % 2
                    act.wait_ge(var_done, t + 1)
                    if t >= 2:
                        act.wait_ge(normed, t - 1)
                    act.activation(rstd[:, q], m.bank[2 + q], ACT.Ln, bias=eps[:]).then_inc(log_done, 1)
                    act.wait_ge(log_done, t + 1)
                    act.activation(rstd[:, q], rstd[:, q], ACT.Exp, scale=-0.5).then_inc(rstd_done, 1)

                def affine(t):
                    act.wait_ge(normed, t + 1)
                    if t >= 2 and conv_w is None:
                        act.wait_ge(turned, t - 1)
                    for c in range(KC):
                        if t >= 2 and conv_w is not None:
                            act.wait_ge(conv_done[c], t - 1)
                        act.activation(h_out(t % 2, c), by_batch(xn[:, t % 2, c]), ACT.Identity,
                                       bias=bcol[:, c:c + 1], scale=wcol[:, c:c + 1]).then_inc(h_done, 1)

                def take_rows(t):
                    act.wait_ge(turned, t + 1)
                    act.activation(rows[:, t * SUB:(t + 1) * SUB, 0:D], m.ps[:, 5:7, :].rearrange("p a (i d) -> p (a i) d", d=D),
                                   ACT.Copy).then_inc(taken, 1)

                if conv_w is not None:
                    steps((2, affine), (1, inverse), (0, square))
                else:
                    steps((2, affine), (1, inverse), (0, square), (3, take_rows))

            @block.vector
            def _(dve):
                def mix_tile(t):
                    for c in range(KC):
                        n = 2 * (KC * t + c)
                        x = srcT[:, c, tile(t)]
                        dve.tensor_tensor(by_batch(x), by_batch(x), weight(0, t), ALU.mult).then_inc(mix_steps, 1)
                        dve.wait_ge(mix_steps, n + 1)
                        dve.wait_ge(scaled, KC * t + c + 1)
                        dve.tensor_tensor(x, x, s0[:, c, tile(t)], ALU.add).then_inc(mix_steps, 1)
                        dve.wait_ge(mix_steps, n + 2)
                        ins = dve.tensor_tensor(x, x, s1[:, c, tile(t)], ALU.add)
                    ins.then_inc(mixed, 1)

                def centre(t):
                    dve.wait_ge(summed, t + 1)
                    if t >= 2:
                        dve.wait_ge(normed, t - 1)
                    dve.tensor_tensor(xc[:, t % 2], srcT[:, :, tile(t)],
                                      m.bank[t % 2].unsqueeze(1).to_broadcast([P, KC, TW]), ALU.subtract).then_inc(centred, 1)

                def normalize(t):
                    q = t % 2
                    dve.wait_ge(rstd_done, t + 1)
                    if t >= 2:
                        dve.wait_ge(h_done, KC * (t - 1))
                    dve.tensor_tensor(xn[:, q], xc[:, q], rstd[:, q].unsqueeze(1).to_broadcast([P, KC, TW]),
                                      ALU.mult).then_inc(normed, 1)

                def choose(t):
                    q = t % 2
                    step = [9 * t]

                    def link(ins):
                        step[0] += 1
                        ins.then_inc(pick, 1)
                        dve.wait_ge(pick, step[0])

                    dve.wait_ge(logits, t + 1)
                    lp = logit_ps[t % 2][:, 0:SUB * E_MOE].rearrange("p (i e) -> p i e", e=E_MOE)
                    mine = sel[:, t * SUB:(t + 1) * SUB]
                    link(dve.tensor_reduce(best[:, q], lp, AX_X, ALU.max))
                    link(dve.tensor_tensor(lg[:, q], lp, best[:, q].unsqueeze(2).to_broadcast([P, SUB, E_MOE]), ALU.is_equal))
                    link(dve.tensor_scalar(free[:, q], lg[:, q, :, 0], -1.0, 1.0, ALU.mult, ALU.add))
                    link(dve.tensor_copy(mine[:, :, 0], lg[:, q, :, 0]))
                    for e in range(1, E_MOE):
                        link(dve.tensor_tensor(mine[:, :, e], lg[:, q, :, e], free[:, q], ALU.mult))
                        if e < E_MOE - 1:
                            link(dve.tensor_tensor(free[:, q], free[:, q], mine[:, :, e], ALU.subtract))
                    assert step[0] == 9 * (t + 1)

                if conv_w is not None:
                    mix_tile(0)
                    mix_tile(1)
                    steps((0, centre), (2, lambda t: [convolve(dve, t, c) for c in range(KC)]),
                          (0, lambda t: mix_tile(t + 2) if t + 2 < TT else None), (1, normalize))
                else:
                    def add(t):
                        x = total[:, :, tile(t)]
                        dve.tensor_tensor(x, x, srcT[:, :, tile(t)], ALU.add)

                    steps((0, centre), (3, choose), (1, normalize), (2, add))
    sem.give_back()



class Places:

    def __init__(self, nc, m, sem, sb, sel, experts, banks):
        self.m, self.sel, self.experts = m, sel, experts
        self.counted, self.ranked, self.chain = sem("counted"), sem("ranked"), sem("chain")
        self.placed, self.owned = sem("placed"), sem("owned")
        self.full = N // SLOT
        self.sums = [sb(f"sums{k}", [P, NP, experts]) for k in range(2)]
        self.more, self.used = sb("more", [P, experts, self.full]), sb("used", [P, experts])
        self.end, self.start = sb("end", [P, experts]), sb("start", [P, experts])
        self.place, self.at = sb("place", [P, NP, experts]), sb("at", [P, NP])
        self.past, self.owner = sb("past", [P, SLOTS, experts]), sb("owner", [P, SLOTS])
        self.banks = [bank[:, 0:NP * experts] for bank in banks]
        self.rank_ps, self.count_ps = (bank.rearrange("p (i e) -> p i e", e=experts) for bank in self.banks)

    def rank(self, pe):
        m, chosen = self.m, self.sel[:].rearrange("p i e -> p (i e)")
        pe.matmul(self.banks[1], m.const[:, C_EACH:C_EACH + P], chosen, start=True, stop=True).then_inc(self.counted, 1)
        pe.matmul(self.banks[0], m.const[:, C_BEFORE:C_BEFORE + P], chosen, start=True, stop=True).then_inc(self.ranked, 1)

    def place_all(self, dve, pos, slot_expert):
        m, experts, full = self.m, self.experts, self.full
        done = [0]

        def link(ins):
            done[0] += 1
            ins.then_inc(self.chain, 1)
            dve.wait_ge(self.chain, done[0])

        dve.wait_ge(self.counted, 1)
        x, y = self.sums
        link(dve.tensor_copy(x[:], self.count_ps))
        k = 1
        while k < NP:
            dve.tensor_copy(y[:, 0:k], x[:, 0:k])
            link(dve.tensor_tensor(y[:, k:], x[:, k:], x[:, 0:NP - k], ALU.add))
            x, y = y, x
            k *= 2
        iota = m.const[:, C_IOTA:C_IOTA + SLOTS]
        link(dve.tensor_tensor(self.more[:], x[:, NP - 1].unsqueeze(2).to_broadcast([P, experts, full]),
                               iota[:, 0:full].unsqueeze(1).to_broadcast([P, experts, full]), ALU.is_gt))
        link(dve.tensor_reduce(self.used[:], self.more[:], AX_X, ALU.add))
        end = self.end
        link(dve.tensor_copy(end[:], self.used[:]))
        for e in range(1, experts):
            link(dve.tensor_tensor(end[:, e:e + 1], end[:, e:e + 1], end[:, e - 1:e], ALU.add))
        link(dve.tensor_tensor(self.start[:], end[:], self.used[:], ALU.subtract))
        dve.wait_ge(self.ranked, 1)
        place = self.place
        link(dve.tensor_tensor(place[:], x[:], self.count_ps, ALU.subtract))
        link(dve.tensor_tensor(place[:], place[:], self.rank_ps, ALU.add))
        link(dve.tensor_tensor(place[:], place[:], self.start[:].unsqueeze(1).to_broadcast([P, NP, experts]), ALU.add))
        link(dve.tensor_tensor(place[:], place[:], self.sel[:], ALU.mult))
        link(dve.tensor_reduce(self.at[:], place[:], AX_X, ALU.add))
        dve.tensor_scalar(pos[:], self.at[:], float(SLOT), None, ALU.mult).then_inc(self.placed, 1)
        link(dve.tensor_tensor(self.past[:], iota.unsqueeze(2).to_broadcast([P, SLOTS, experts]),
                               end[:].unsqueeze(1).to_broadcast([P, SLOTS, experts]), ALU.is_ge))
        link(dve.tensor_reduce(self.owner[:], self.past[:], AX_X, ALU.add))
        dve.tensor_scalar(slot_expert[:], self.owner[:], float(experts - 1), None, ALU.min).then_inc(self.owned, 1)


def scatter(pool, m, stage, rows, pos, turned=None):
    pool.wait_ge(m.cleared, 16 * m.n_clear)
    for i in range(NP):
        if turned is not None and i % 2 == 0:
            pool.wait_ge(turned, i // 2 + 1)
        pool.indirect_dma_start(stage.x_sorted[:], bass.IndirectOffsetOnAxis(ap=pos[:, i:i + 1], axis=0),
                                rows[:, i], None).then_inc(m.scattered, 16)


class SlotStage:

    def __init__(self, nc, ctx, m, tag, ups, experts, up, down, slot_expert, x_sorted, target, carried):
        sb = lambda name, shape: ctx.enter_context(nc.sbuf_tensor(f"{tag}_{name}", shape, F32))
        pair = lambda name: [ctx.enter_context(nc.semaphore(f"{tag}_{name}{i}")) for i in range(2)]
        self.m, self.experts, self.up_source, self.down_source, self.slot_expert = m, experts, up, down, slot_expert
        self.ups, self.x_sorted, self.target, self.carried = ups, x_sorted, target, carried
        self.up, self.down = sb("stage_up", [P, 2, ups, KC, F]), sb("stage_dn", [P, 2, FC, D])
        self.x_row = sb("x_row", [P, 2, SLOT // P, D + carried + 1])
        self.x_loaded, self.up_loaded, self.dn_loaded = pair("x_loaded"), pair("up_loaded"), pair("dn_loaded")

    def expert(self, sp, s):
        return sp.value_load(self.slot_expert[0:1, bass.ds(s, 1)], min_val=0, max_val=self.experts - 1)

    def load_rows(self, sp, s, q):
        rows = self.x_sorted[bass.ds(s * SLOT, SLOT)].rearrange("(i p) d -> p i d", p=P)
        sp.dma_start(self.x_row[:, q], rows).then_inc(self.x_loaded[q], 16)

    def load_up(self, sp, e, q):
        for j, src in enumerate(self.up_source(e)):
            sp.dma_start(self.up[:, q, j], src).then_inc(self.up_loaded[q], 16)

    def load_down(self, sp, e, q):
        sp.dma_start(self.down[:, q], self.down_source(e)).then_inc(self.dn_loaded[q], 16)

    def load_first(self, sp):
        e = self.expert(sp, 0)
        self.load_up(sp, e, 0)
        self.load_down(sp, e, 0)
        e = self.expert(sp, 1)
        sp.wait_ge(self.m.scattered, 16 * self.m.scatters)
        self.load_rows(sp, 0, 0)
        self.load_rows(sp, 1, 1)
        self.load_up(sp, e, 1)
        self.load_down(sp, e, 1)


def sort_rows(nc, m, tag, sel, experts, rows, carried, stage):
    sem = StageSemaphores(nc, tag)
    turned, taken = sem("turned"), sem("taken")
    with ExitStack() as s:
        places = Places(nc, m, sem, lambda name, shape: s.enter_context(nc.sbuf_tensor(f"{tag}_{name}", shape, F32)),
                        sel, experts, m.bank[0:2])
        banks = m.bank[2:]
        with nc.Block() as block:
            @block.tensor
            def _(pe):
                places.rank(pe)
                for i in range(NP // 2):
                    if i >= len(banks):
                        pe.wait_ge(taken, i - len(banks) + 1)
                    for j in range(2):
                        for c in range(KC):
                            t = (2 * i + j) * P
                            ins = pe.transpose(banks[i % len(banks)][:, (j * KC + c) * P:(j * KC + c + 1) * P],
                                               carried[:, c, t:t + P], m.ident)
                    ins.then_inc(turned, 1)

            @block.scalar
            def _(act):
                for i in range(NP // 2):
                    act.wait_ge(turned, i + 1)
                    act.activation(rows[:, 2 * i:2 * i + 2, D:2 * D], banks[i % len(banks)].rearrange("p (j d) -> p j d", j=2),
                                   ACT.Copy).then_inc(taken, 1)

            @block.vector
            def _(dve):
                places.place_all(dve, m.pos, m.slot_expert)

            @block.gpsimd
            def _(pool):
                pool.wait_ge(places.placed, 1)
                scatter(pool, m, stage, rows, m.pos, taken)

            @block.sync
            def _(sp):
                sp.wait_ge(places.owned, 1)
                stage.load_first(sp)
    sem.give_back()


def routed_ffn(nc, m, tag, swiglu, stage):
    ups = 2 if swiglu else 1
    n = SLOTS
    HALVES, LAG, UB, HB = SLOT // P, 3, 4, 4
    DN = LAG + 1
    sem = StageSemaphores(nc, tag)
    pair = lambda name: [sem(f"{name}{i}") for i in range(2)]
    x_loaded, up_loaded, dn_loaded, stored = stage.x_loaded, stage.up_loaded, stage.dn_loaded, pair("stored")
    stage_up, stage_dn, x_row = stage.up, stage.down, stage.x_row
    x_turned, x_rounded, x_ready = sem("x_turned"), sem("x_rounded"), sem("x_ready")
    up_rounded, dn_rounded = sem("up_rounded"), sem("dn_rounded")
    up_ready, dn_ready = sem("up_ready"), pair("dn_ready")
    up_done, dn_done, act_done = sem("up_done"), sem("dn_done"), sem("act_done")
    h_rounded, h_ready = sem("h_rounded"), sem("h_ready")
    up_free = sem("up_free") if swiglu else h_ready
    y_taken = sem("y_taken")
    with ExitStack() as s_:
        sb = lambda name, shape, dt=F32: s_.enter_context(nc.sbuf_tensor(f"{tag}_{name}", shape, dt))
        w_hi, w_lo = sb("w_hi", [P, ups, KC, F], F32R), sb("w_lo", [P, ups, KC, F], F32R)
        d_hi, d_lo = sb("d_hi", [P, FC, D], F32R), sb("d_lo", [P, FC, D], F32R)
        x_hi, x_lo = sb("x_hi", [P, 2, KC, SLOT], F32R), sb("x_lo", [P, 2, KC, SLOT], F32R)
        h_hi, h_lo = sb("h_hi", [P, HB, SLOT], F32R), sb("h_lo", [P, HB, SLOT], F32R)
        y_row = sb("y_row", [P, 2, HALVES, D])
        carried, fence = stage.carried, sb("fence", [P, 2, HALVES, 1])
        keep, token = sb("keep", [P, 2, HALVES, carried + 1]), sb("token", [P, 2, HALVES], mybir.dt.uint32)
        nought = sb("nought", [1, HALVES * D], F32R)
        if swiglu:
            silu, h = sb("silu", [P, 2, SLOT]), sb("h", [P, HB, SLOT])
        up_ps = [[m.bank[i][:, j * SLOT:(j + 1) * SLOT] for j in range(ups)] for i in range(UB)]
        y_ps = [m.bank[UB + q].rearrange("p (i d) -> p i d", d=D) for q in range(2)]
        x_ps = [m.bank[UB + 2 + q].rearrange("p (c t) -> p c t", c=KC) for q in range(2)]
        fs = lambda f: slice(f * P, (f + 1) * P)

        def run(eng, slot):
            slot(0, 0, 0)
            full = (n - 3) // 2
            with eng.Fori(0, full) as pairs:
                slot(pairs * 2 + 1, pairs, 1)
                slot(pairs * 2 + 2, pairs + 1, 0)
            for s in range(2 * full + 1, n):
                slot(s, s // 2, s % 2)

        is_first = lambda s: isinstance(s, int) and s == 0
        is_last = lambda s: isinstance(s, int) and s == n - 1

        with nc.Block() as block:
            @block.sync
            def _(sp):
                def load(s, q):
                    e = stage.expert(sp, s)
                    sp.wait_ge(x_ready, s - 1)
                    stage.load_rows(sp, s, q)
                    sp.wait_ge(up_ready, FC * (s - 1))
                    stage.load_up(sp, e, q)
                    for r in range(2):
                        sp.wait_ge(dn_ready[r], FC // 2 * (s - 1))
                    stage.load_down(sp, e, q)

                load(2, 0)
                full = (n - 3) // 2
                with sp.Fori(0, full) as pairs:
                    for u in range(2):
                        load(pairs * 2 + 3 + u, (3 + u) % 2)
                for s in range(3 + 2 * full, n):
                    load(s, s % 2)
                for q in range(2):
                    sp.wait_ge(stored[q], 16 * HALVES * ((n + 1 - q) // 2))

            @block.gpsimd
            def _(pool):
                def up_lo(s, f, q):
                    pool.wait_ge(up_rounded, FC * s + f + 1)
                    pool.tensor_tensor(w_lo[:, :, :, fs(f)], stage_up[:, q, :, :, fs(f)], w_hi[:, :, :, fs(f)],
                                       ALU.subtract).then_inc(up_ready, 1)

                def dn_lo(s, f, q):
                    if f % 2 == 0:
                        pool.wait_ge(dn_rounded, FC * s + f + 1)
                        pool.tensor_tensor(d_lo[:, f], stage_dn[:, q, f], d_hi[:, f], ALU.subtract).then_inc(dn_ready[0], 1)

                def send(s, q, i):
                    pool.wait_ge(y_taken, s + 1)
                    pool.tensor_tensor(fence[:, q, i], m.const[:, C_ONE:C_ONE + 1], m.const[:, C_ONE:C_ONE + 1], ALU.mult)
                    pool.indirect_dma_start(stage.target, bass.IndirectOffsetOnAxis(ap=token[:, q, i:i + 1], axis=0),
                                            y_row[:, q, i], None, bounds_check=N - 1, oob_is_err=False).then_inc(stored[q], 16)

                def slot(s, nth, q):
                    for f in range(FC):
                        if not is_last(s):
                            up_lo(s + 1, f, 1 - q)
                        if f < FC - DN:
                            dn_lo(s, f + DN, q)
                        elif not is_last(s):
                            dn_lo(s + 1, f + DN - FC, 1 - q)
                        if f == 6 and not is_first(s):
                            send(s - 1, 1 - q, 0)
                            send(s - 1, 1 - q, 1)

                for f in range(FC):
                    up_lo(0, f, 0)
                    if LAG <= f < LAG + DN:
                        dn_lo(0, f - LAG, 0)
                run(pool, slot)
                for i in range(HALVES):
                    send(n - 1, (n - 1) % 2, i)

            @block.tensor
            def _(pe):
                def turn(s, nth, q):
                    pe.wait_ge(x_loaded[q], 16 * (nth + 1))
                    if not (isinstance(s, int) and s < 2):
                        pe.wait_ge(x_ready, s - 1)
                    for i in range(HALVES):
                        for c in range(KC):
                            ins = pe.transpose(x_ps[q][:, c, i * P:(i + 1) * P], x_row[:, q, i, fs(c)], m.ident)
                    ins.then_inc(x_turned, 1)

                def up_step(s, f, q):
                    g = FC * s + f
                    if f == 0:
                        pe.wait_ge(x_ready, s + 1)
                    pe.wait_ge(up_ready, g + 1)
                    pe.wait_ge(up_free, g + 1)
                    for j in range(ups):
                        i = 0
                        for k in range(KC):
                            for w, x in ((w_hi, x_hi), (w_hi, x_lo), (w_lo, x_hi)):
                                ins = pe.matmul(up_ps[f % UB][j], w[:, j, k, fs(f)], x[:, q, k],
                                                start=(i == 0), stop=(i == 3 * KC - 1))
                                i += 1
                    ins.then_inc(up_done, 1)

                def dn_step(s, f, q):
                    g = FC * s + f
                    pe.wait_ge(dn_ready[f % 2], FC // 2 * s + f // 2 + 1)
                    pe.wait_ge(h_ready, g + (1 if swiglu else 1 + UB))
                    if f == 0 and not (isinstance(s, int) and s < 2):
                        pe.wait_ge(y_taken, s - 1)
                    if f == 0:
                        pe.matmul(y_ps[q], nought[:, 0:P], nought[:], start=True, stop=False)
                    for i in range(HALVES):
                        for k, (x, w) in enumerate(((h_hi, d_hi), (h_lo, d_hi), (h_hi, d_lo))):
                            ins = pe.matmul(y_ps[q][:, i], x[:, f % HB, i * P:(i + 1) * P], w[:, f],
                                            start=False, stop=(f == FC - 1 and i == HALVES - 1 and k == 2))
                    if f == FC - 1:
                        ins.then_inc(dn_done, 1)

                def slot(s, nth, q):
                    for f in range(FC):
                        up_step(s, f, q)
                        if f == 4 and not is_last(s):
                            turn(s + 1, nth + q, 1 - q)
                        if f >= LAG:
                            dn_step(s, f - LAG, q)
                        elif not is_first(s):
                            dn_step(s - 1, f - LAG + FC, 1 - q)

                turn(0, 0, 0)
                run(pe, slot)
                for f in range(FC - LAG, FC):
                    dn_step(n - 1, f, (n - 1) % 2)

            @block.scalar
            def _(act):
                def round_x(s, q):
                    act.wait_ge(x_turned, s + 1)
                    act.activation(x_hi[:, q], x_ps[q], ACT.Copy).then_inc(x_rounded, 1)

                def round_up(s, nth, q, f):
                    if f == 0:
                        act.wait_ge(up_loaded[q], 16 * ups * (nth + 1))
                    act.activation(w_hi[:, :, :, fs(f)], stage_up[:, q, :, :, fs(f)], ACT.Copy).then_inc(up_rounded, 1)

                def round_hidden(s, f):
                    act.wait_ge(up_free, FC * s + f + 1 + UB)
                    act.activation(h_hi[:, f % HB], h[:, f % HB], ACT.Copy).then_inc(h_rounded, 1)

                def slot(s, nth, q):
                    for f in range(FC):
                        act.wait_ge(up_done, FC * s + f + 1)
                        if swiglu:
                            act.activation(silu[:, f % 2], up_ps[f % UB][0], ACT.Silu).then_inc(act_done, 1)
                            if f > 0:
                                round_hidden(s, f - 1)
                            elif not is_first(s):
                                round_hidden(s - 1, FC - 1)
                        else:
                            act.activation(h_hi[:, f % HB], up_ps[f % UB][0], ACT.Relu).then_inc(h_rounded, 1)
                        if not is_last(s):
                            round_up(s + 1, nth + q, 1 - q, f)
                            if f == 5:
                                round_x(s + 1, 1 - q)

                act.activation(nought[:], m.zero_row[0:1].unsqueeze(1).to_broadcast([1, HALVES, D]), ACT.Copy)
                round_x(0, 0)
                for f in range(FC):
                    round_up(0, 0, 0, f)
                run(act, slot)
                if swiglu:
                    round_hidden(n - 1, FC - 1)

            @block.vector
            def _(dve):
                dve.nop().then_inc(up_free, UB)

                def split_x(s, q):
                    dve.wait_ge(x_rounded, s + 1)
                    if not (isinstance(s, int) and s < 2):
                        dve.wait_ge(y_taken, s - 1)
                    dve.tensor_copy(keep[:, q], x_row[:, q, :, D:])
                    dve.tensor_tensor(x_lo[:, q], x_ps[q], x_hi[:, q], ALU.subtract).then_inc(x_ready, 1)

                def round_dn(s, nth, q, f):
                    if f == 0:
                        dve.wait_ge(dn_loaded[q], 16 * (nth + 1))
                    dve.tensor_copy(d_hi[:, f], stage_dn[:, q, f]).then_inc(dn_rounded, 1)
                    if f % 2 == 1:
                        dve.wait_ge(dn_rounded, FC * s + f + 1)
                        dve.tensor_tensor(d_lo[:, f], stage_dn[:, q, f], d_hi[:, f], ALU.subtract).then_inc(dn_ready[1], 1)

                def split_hidden(s, f):
                    dve.wait_ge(h_rounded, FC * s + f + 1)
                    if swiglu:
                        dve.tensor_tensor(h_lo[:, f % HB], h[:, f % HB], h_hi[:, f % HB], ALU.subtract).then_inc(h_ready, 1)
                    else:
                        dve.scalar_tensor_tensor(h_lo[:, f % HB], up_ps[f % UB][0], 0.0, h_hi[:, f % HB],
                                                 ALU.max, ALU.subtract).then_inc(h_ready, 1)

                def take(s, nth, q):
                    dve.wait_ge(dn_done, s + 1)
                    dve.wait_ge(x_ready, s + 1)
                    if not (isinstance(s, int) and s < 2):
                        dve.wait_ge(stored[q], 16 * HALVES * nth)
                    if carried:
                        dve.tensor_tensor(y_row[:, q], y_ps[q], keep[:, q, :, 0:D], ALU.add)
                    else:
                        dve.tensor_copy(y_row[:, q], y_ps[q])
                    dve.tensor_scalar(token[:, q], keep[:, q, :, carried], 1.0, None, ALU.mult).then_inc(y_taken, 1)

                def slot(s, nth, q):
                    for f in range(FC):
                        if swiglu:
                            dve.wait_ge(act_done, FC * s + f + 1)
                            dve.tensor_tensor(h[:, f % HB], silu[:, f % 2], up_ps[f % UB][1], ALU.mult).then_inc(up_free, 1)
                            if f > 0:
                                split_hidden(s, f - 1)
                            elif not is_first(s):
                                split_hidden(s - 1, FC - 1)
                        else:
                            split_hidden(s, f)
                        if f < FC - DN:
                            round_dn(s, nth, q, f + DN)
                        elif not is_last(s):
                            round_dn(s + 1, nth + q, 1 - q, f + DN - FC)
                        if f == 4 and not is_first(s):
                            take(s - 1, nth + q - 1, 1 - q)
                        if f == 6 and not is_last(s):
                            split_x(s + 1, 1 - q)

                split_x(0, 0)
                for f in range(DN):
                    round_dn(0, 0, 0, f)
                run(dve, slot)
                if swiglu:
                    split_hidden(n - 1, FC - 1)
                take(n - 1, (n - 1) // 2, (n - 1) % 2)
    sem.give_back()


def turn_back(nc, m, tag, src, dst, early):
    sem = StageSemaphores(nc, tag)
    turned, taken = sem("turned"), sem("taken")
    loaded = [sem(f"loaded{i}") for i in range(TT)]
    SUB = TW // P
    with ExitStack() as s:
        y = s.enter_context(nc.sbuf_tensor(f"{tag}_y", [P, NP, D], F32))
        with nc.Block() as block:
            @block.sync
            def _(sp):
                rows = src.rearrange("(i p) d -> p i d", p=P)
                for t in range(TT):
                    i = slice(t * SUB, (t + 1) * SUB)
                    sp.dma_start(y[:, i], rows[:, i]).then_inc(loaded[t], 16)
                early(sp)

            @block.tensor
            def _(pe):
                for i in range(NP // 2):
                    if i % (SUB // 2) == 0:
                        pe.wait_ge(loaded[i // (SUB // 2)], 16)
                    for j in range(2):
                        for c in range(KC):
                            ins = pe.transpose(m.bank[i % 8][:, (c * 2 + j) * P:(c * 2 + j + 1) * P],
                                               y[:, 2 * i + j, c * P:(c + 1) * P], m.ident)
                    ins.then_inc(turned, 1)

            @block.scalar
            def _(act):
                for i in range(NP // 2):
                    act.wait_ge(turned, i + 1)
                    act.activation(dst[:, :, i * 2 * P:(i + 1) * 2 * P], m.bank[i % 8].rearrange("p (c t) -> p c t", c=KC),
                                   ACT.Copy).then_inc(taken, 1)
    sem.give_back()


def split_and_turn(nc, m, tag, src, x_hi, x_lo, rows, early):
    sem = StageSemaphores(nc, tag)
    rounded, turned, taken = sem("rounded"), sem("turned"), sem("taken")
    with nc.Block() as block:
        @block.sync
        def _(sp):
            early(sp)

        @block.tensor
        def _(pe):
            for i in range(NP // 2):
                for j in range(2):
                    for c in range(KC):
                        t = (2 * i + j) * P
                        ins = pe.transpose(m.bank[i][:, (j * KC + c) * P:(j * KC + c + 1) * P], src[:, c, t:t + P], m.ident)
                ins.then_inc(turned, 1)

        def take(eng, i, copy):
            eng.wait_ge(turned, i + 1)
            copy(rows[:, 2 * i:2 * i + 2, 0:D], m.bank[i].rearrange("p (j d) -> p j d", j=2))

        @block.gpsimd
        def _(pool):
            pool.tensor_copy(rows[:, :, D], m.const[:, C_TOKEN:C_TOKEN + NP])

        @block.scalar
        def _(act):
            for t in range(TT):
                tok = slice(t * TW, (t + 1) * TW)
                act.activation(x_hi[:, :, tok], src[:, :, tok], ACT.Copy).then_inc(rounded, 1)
                take(act, 2 * t, lambda dst, bank: act.activation(dst, bank, ACT.Copy))

        @block.vector
        def _(dve):
            for t in range(TT):
                tok = slice(t * TW, (t + 1) * TW)
                dve.wait_ge(rounded, t + 1)
                dve.tensor_tensor(x_lo[:, :, tok], src[:, :, tok], x_hi[:, :, tok], ALU.subtract)
                take(dve, 2 * t + 1, dve.tensor_copy)
    sem.give_back()


def load_inputs(nc, m, x, x_hi, x_lo, stage, up, down):
    sem = StageSemaphores(nc, "load")
    const_loaded, turned, taken, rounded = sem("const_loaded"), sem("x_turned"), sem("x_taken"), sem("x_rounded")
    small_loaded, zeroed, gated, copied = sem("small_loaded"), sem("zeroed"), sem("gated"), sem("x_copied")
    QT = 4
    x_loaded = [sem(f"x_loaded{q}") for q in range(QT)]
    with ExitStack() as s:
        x_tok = s.enter_context(nc.sbuf_tensor("x_tok", [P, NP, D], F32))
        BANKS = 8
        with nc.Block() as block:
            @block.sync
            def _(sp):
                sp.dma_start(m.const[:], m.consts_dram).then_inc(const_loaded, 16)
                rows = x.rearrange("b t d -> (b t) d").rearrange("(i p) d -> p i d", p=P)
                for q in range(QT):
                    i = slice(q * NP // QT, (q + 1) * NP // QT)
                    sp.dma_start(x_tok[:, i], rows[:, i]).then_inc(x_loaded[q], 16)
                stage.load_up(sp, up)
                stage.load_down(sp, down)
                sp.wait_ge(zeroed, 2)
                sp.wait_ge(const_loaded, 16)
                for x_sorted in (m.typed_sorted, m.moe_sorted):
                    last = x_sorted.shape[1] - 1
                    for k in range(last // D):
                        sp.dma_start(x_sorted[:, k * D:(k + 1) * D].rearrange("(i p) d -> p i d", p=P),
                                     m.zero_row[:].unsqueeze(1).to_broadcast([P, SLOTS * SLOT // P, D])).then_inc(m.cleared, 16)
                    sp.dma_start(x_sorted[:, last:last + 1].rearrange("(i p) d -> p i d", p=P),
                                 m.const[:, C_NONE:C_NONE + SLOTS * SLOT // P].unsqueeze(2),
                                 allow_slow_non_contiguous=True).then_inc(m.cleared, 16)
                m.n_clear = 5

            @block.gpsimd
            def _(pool):
                pool.memset(m.sumT[:], 0.0).then_inc(zeroed, 1)
                pool.memset(m.minus_one[:], -1.0)
                pool.memset(m.zero_row[:], 0.0).then_inc(zeroed, 1)

            @block.tensor
            def _(pe):
                pe.wait_ge(const_loaded, 16)
                for i in range(NP // 2):
                    if i % 2 == 0:
                        pe.wait_ge(x_loaded[i // 2], 16)
                    if i >= BANKS:
                        pe.wait_ge(taken, i - BANKS + 1)
                    for j in range(2):
                        for c in range(KC):
                            ins = pe.transpose(m.bank[i % BANKS][:, (c * 2 + j) * P:(c * 2 + j + 1) * P],
                                               x_tok[:, 2 * i + j, c * P:(c + 1) * P], m.ident)
                    ins.then_inc(turned, 1)

            @block.scalar
            def _(act):
                m.load_small(act, small_loaded)
                for i in range(NP // 2):
                    tok = slice(i * 2 * P, (i + 1) * 2 * P)
                    bank = m.bank[i % BANKS].rearrange("p (c t) -> p c t", c=KC)
                    act.wait_ge(turned, i + 1)
                    act.activation(x_hi[:, :, tok], bank, ACT.Copy).then_inc(rounded, 1)
                    if i % 2 == 1:
                        act.activation(m.xT[:, :, tok], bank, ACT.Copy).then_inc(copied, 1)

            @block.vector
            def _(dve):
                for i in range(NP // 2):
                    tok = slice(i * 2 * P, (i + 1) * 2 * P)
                    bank = m.bank[i % BANKS].rearrange("p (c t) -> p c t", c=KC)
                    dve.wait_ge(rounded, i + 1)
                    if i % 2 == 0:
                        dve.tensor_copy(m.xT[:, :, tok], bank)
                    else:
                        dve.wait_ge(copied, i // 2 + 1)
                    dve.tensor_tensor(x_lo[:, :, tok], bank, x_hi[:, :, tok], ALU.subtract).then_inc(taken, 1)
                dve.wait_ge(small_loaded, 16 * m.n_small)
                sg = m.gate_cond[:, E_COND]
                dve.tensor_scalar(m.not_shared[:], sg, -1.0, 1.0, ALU.mult, ALU.add).then_inc(gated, 1)
                dve.wait_ge(gated, 1)
                dve.tensor_tensor(m.gate_cond[:, 0:E_COND],
                                  m.probs[:].rearrange("p (b e) -> p e b", e=E_COND),
                                  m.not_shared[:].unsqueeze(1).to_broadcast([P, E_COND, B]), ALU.mult)
                dve.tensor_scalar(m.neg_b_sur[:], m.b_sur[:], -1.0, None, ALU.mult)
                dve.tensor_scalar(m.type_in[:], m.type_id[:], 0.0, float(E_TYPE - 1), ALU.max, ALU.min).then_inc(gated, 1)
                dve.wait_ge(gated, 2)
                for e in range(E_TYPE):
                    dve.tensor_scalar(m.type_sel[:, :, e], m.type_in[:], float(e), None, ALU.is_equal)
    sem.give_back()


def program(nc, a, out):
    with ExitStack() as ctx:
        m = Memory()
        sb = lambda name, shape, dt=F32: ctx.enter_context(nc.sbuf_tensor(name, shape, dt))
        ps = ctx.enter_context(nc.psum_tensor("ps", [P, 8, 512], F32))
        m.ps = ps
        m.bank = [ps[:, i, :] for i in range(8)]
        m.consts_dram = a["constants"]
        m.xT = sb("xT", [P, KC, N])
        sum_store = sb("sum", [P, KC * N + NP])
        m.sumT = sum_store[:, 0:KC * N].rearrange("p (c n) -> p c n", c=KC)
        m.const = sb("const", [P, C_END])
        m.ident = m.const[:, C_ID:C_ID + P]
        m.gate_cond = sb("gate_cond", [P, E_COND + 1, B])
        m.probs = sb("probs", [P, B * E_COND])
        m.not_shared = sb("not_shared", [P, B])
        m.type_id = sb("types", [P, NP], I32)
        m.type_in = sb("types_in", [P, NP])
        m.type_sel = sb("type_sel", [P, NP, E_TYPE])
        m.zero_row = sb("zero_row", [P, D])
        scratch = lambda name, rows, width: nc.dram_tensor(name, [rows, width], F32, kind="Internal").ap()
        m.typed_sorted = scratch("typed_sorted", SLOTS * SLOT, D + 1)
        m.moe_sorted = scratch("moe_sorted", SLOTS * SLOT, 2 * D + 1)
        m.typed_rows = scratch("typed_rows", N, D)
        m.cleared, m.scattered = (ctx.enter_context(nc.semaphore(n)) for n in ("cleared", "scattered"))
        m.scatters = 0
        m.pos = sb("pos", [P, NP], mybir.dt.uint32)
        m.slot_expert = sb("slot_expert", [P, SLOTS], I32)
        m.b_sur = sb("b_sur", [P, 1])
        m.neg_b_sur = sb("neg_b_sur", [P, 1])
        m.threshold = sb("threshold", [P, 1])
        m.minus_one = sb("minus_one", [P, 1])

        def load_small(eng, sem):
            loads = [
                (m.probs[:], a["fside_Bx8_0"].rearrange("b e -> (b e)").unsqueeze(0).to_broadcast([P, B * E_COND])),
                (m.gate_cond[:, E_COND], a["condB_sharedgateprob"].unsqueeze(0).to_broadcast([P, B])),
                (m.type_id[0:T], a["itok_B_0_2"].rearrange("(i j) -> j i", j=2)[0:1].to_broadcast([T, NP])),
                (m.type_id[T:], a["itok_B_0_2"].rearrange("(i j) -> j i", j=2)[1:2].to_broadcast([T, NP])),
                (m.b_sur[:], a["L0_attn_b_sur"].unsqueeze(0).to_broadcast([P, 1])),
                (m.threshold[:], a["L0_attn_threshold"].unsqueeze(0).to_broadcast([P, 1])),
            ]
            for dst, src in loads:
                eng.dma_start(dst, src, allow_slow_non_contiguous=True).then_inc(sem, 16)
            m.n_small = len(loads)
            return len(loads)

        m.load_small = load_small
        up = lambda w: (lambda e: w[bass.ds(e, 1)].rearrange("o (k p) f -> p (o k) f", p=P))
        down = lambda w: (lambda e: w[bass.ds(e, 1)].rearrange("o (c p) d -> p (o c) d", p=P))
        one = lambda w: w.unsqueeze(0)

        with ExitStack() as both:
            hyp = AttentionWeights(nc, both, both, "hyp", a["L0_attn_W_qkv"], a["L0_attn_W_out"], a["L0_attn_b_qkv"],
                                   a["L0_attn_b_out"], a["L0_attn_w_sur"])
            with ExitStack() as s:
                stage = ExpertStage(nc, s, "cond", 2)
                x_hi = s.enter_context(nc.sbuf_tensor("a_x_hi", [P, KC, N], F32R))
                x_lo = s.enter_context(nc.sbuf_tensor("a_x_lo", [P, KC, N], F32R))
                wg, wu, wd = a["L0_cond_Wg"], a["L0_cond_Wu"], a["L0_cond_Wd"]
                sg, su, sd = one(a["L0_cond_Sg"]), one(a["L0_cond_Su"]), one(a["L0_cond_Sd"])
                load_inputs(nc, m, a["x"], x_hi, x_lo, stage, (up(wg)(0), up(wu)(0)), down(wd)(0))
                groups = [(E_COND, lambda e: (up(wg)(e), up(wu)(e)), down(wd)),
                          (1, lambda e: (up(sg)(e), up(su)(e)), down(sd))]
                gate = lambda e, tt: m.gate_cond[:, bass.ds(e, 1), tt * BT:(tt + 1) * BT].rearrange(
                    "p o b -> p (o b)").unsqueeze(2).to_broadcast([P, BT, T])
                ffn(nc, m, "cond", True, groups, gate, [m.sumT, m.sumT], x_hi, x_lo, stage, WeightsBeside(hyp))

            attention(nc, m, "hyp", True, m.sumT, m.xT, hyp)

        wi, wo, si, so = a["L0_cond2_wi"], a["L0_cond2_wo"], a["L0_cond2_swi"], a["L0_cond2_swo"]
        with ExitStack() as s:
            sb = lambda name, shape, dt=F32: s.enter_context(nc.sbuf_tensor(name, shape, dt))
            s0, s1 = sb("s0", [P, KC, N]), sb("s1", [P, KC, N])
            with ExitStack() as f:
                slots = SlotStage(nc, f, m, "typed", 1, E_TYPE, lambda e: (up(wi)(e),), down(wo), m.slot_expert,
                                  m.typed_sorted, m.typed_rows[:], 0)
                with ExitStack() as g:
                    stage = ExpertStage(nc, g, "dense", 1)
                    x_hi = g.enter_context(nc.sbuf_tensor("c_x_hi", [P, KC, N], F32R))
                    x_lo = g.enter_context(nc.sbuf_tensor("c_x_lo", [P, KC, N], F32R))
                    nth = lambda w, i: w[i:i + 1]
                    groups = [(1, lambda e, i=i: (up(nth(si, i))(0),), lambda e, i=i: down(nth(so, i))(0)) for i in range(E_SHARED)]

                    def first_shared(sp):
                        stage.load_up(sp, groups[0][1](0))
                        stage.load_down(sp, groups[0][2](0))

                    rows = sum_store[:].rearrange("p (i d) -> p i d", d=D + 1)
                    split_and_turn(nc, m, "c_x", m.xT, x_hi, x_lo, rows, first_shared)
                    sem = StageSemaphores(nc, "typed_sort")
                    places = Places(nc, m, sem, lambda name, shape: g.enter_context(nc.sbuf_tensor(f"typed_{name}", shape, F32)),
                                    m.type_sel, E_TYPE, [m.bank[1], m.bank[3]])
                    ffn(nc, m, "dense", False, groups, None, [s0, s1], x_hi, x_lo, stage, SortBeside(m, places, rows, slots))
                    sem.give_back()
                routed_ffn(nc, m, "typed", False, slots)
            w_mix = sb("w_mix", [P, 3, B])
            with ExitStack() as f:
                mixing = GateWeights(nc, f, a["L0_cond2_g1"], a["L0_cond2_g2"])
                turn_back(nc, m, "c_back", m.typed_rows, m.sumT, mixing.load)
                mix_gate(nc, m, mixing, m.sumT, s0, s1, w_mix)

            with ExitStack() as raw:
                rope = AttentionWeights(nc, s, raw, "rope", a["L0_ffn_attn_w"], a["L0_ffn_proj_w"])
                layer_norm(nc, m, "ln1", m.sumT, a["L0_ffn_ln1_w"], a["L0_ffn_ln1_b"], conv_w=a["L0_ffn_conv_w"], convT=s0,
                           mix=(s0, s1, w_mix), sync_late=rope.load, scalar_early=rope.round, gpsimd_late=rope.split)
            attention(nc, m, "rope", False, s0, m.sumT, rope)

        with ExitStack() as s:
            wv = a["L0_ffn_expert_wv"]
            halves = lambda e: tuple(up(wv)(e)[:, :, j * F:(j + 1) * F] for j in range(2))
            slots = SlotStage(nc, s, m, "moe", 2, E_MOE, halves, down(a["L0_ffn_expert_proj"]), m.slot_expert,
                              m.moe_sorted, out.rearrange("b t d -> (b t) d"), D)
            with ExitStack() as f:
                sel = f.enter_context(nc.sbuf_tensor("moe_sel", [P, NP, E_MOE], F32))
                rows = f.enter_context(nc.sbuf_tensor("moe_rows", [P, NP, 2 * D + 1], F32))
                layer_norm(nc, m, "ln2", m.sumT, a["L0_ffn_ln2_w"], a["L0_ffn_ln2_b"], router=(a["L0_ffn_router_w"], rows, sel, m.xT))
                m.scatters += NP
                sort_rows(nc, m, "e_sort", sel, E_MOE, rows, m.xT, slots)
            routed_ffn(nc, m, "moe", True, slots)


_INS = ['x', 'fside_Bx8_0', 'condB_sharedgateprob', 'itok_B_0_2', 'L0_cond_Wg', 'L0_cond_Wu', 'L0_cond_Wd',
        'L0_cond_Sg', 'L0_cond_Su', 'L0_cond_Sd', 'L0_attn_W_qkv', 'L0_attn_b_qkv', 'L0_attn_W_out', 'L0_attn_b_out',
        'L0_attn_w_sur', 'L0_attn_b_sur', 'L0_attn_threshold', 'L0_cond2_wi', 'L0_cond2_wo', 'L0_cond2_swi',
        'L0_cond2_swo', 'L0_cond2_g1', 'L0_cond2_g2', 'L0_ffn_ln1_w', 'L0_ffn_ln1_b', 'L0_ffn_ln2_w', 'L0_ffn_ln2_b',
        'L0_ffn_conv_w', 'L0_ffn_attn_w', 'L0_ffn_proj_w', 'L0_ffn_router_w', 'L0_ffn_expert_wv', 'L0_ffn_expert_proj']
_OUTS = [((B, T, D), 'float32')]


def kernel(**inputs):
    import concourse.bacc as bacc
    from concourse.bass_utils import run_bass_kernel_spmd as run

    nc = bacc.Bacc("TRN2", target_bir_lowering=False, num_devices=1)
    arrays, args = {}, {}
    given = dict(inputs, constants=shape_constants())
    for name in _INS + ["constants"]:
        v = np.ascontiguousarray(given[name])
        if v.ndim == 0:
            v = v.reshape(1)
        arrays[f"in_{name}"] = v
        args[name] = nc.dram_tensor(f"in_{name}", v.shape, mybir.dt.from_np(v.dtype), kind="ExternalInput").ap()
    shape, dtype = _OUTS[0]
    out = nc.dram_tensor("out_0", shape, mybir.dt.from_np(np.dtype(dtype)), kind="ExternalOutput").ap()
    program(nc, args, out)
    r = run(nc, [arrays], core_ids=[0])
    return r.results[0]["out_0"]
```
